# Optimizing a Trainium2 kernel written in Bass

```python
import numpy as np
import jax
import jax.numpy as jnp

def _softmax(x, axis=-1):
    return jax.nn.softmax(x, axis=axis)

def _gelu(x):
    return jax.nn.gelu(x, approximate=True)

def _silu(x):
    return jax.nn.silu(x)

def _sigmoid(x):
    return jax.nn.sigmoid(x)

def _layernorm(x, axis=-1, eps=1e-05):
    m = jnp.mean(x, axis=axis, keepdims=True)
    v = jnp.var(x, axis=axis, keepdims=True)
    return (x - m) / jnp.sqrt(v + eps)

def _scatter_add(tgt, idx, src, axis=0):
    return tgt.at[idx].add(src)

def _segment_sum(src, seg, n):
    return jax.ops.segment_sum(src, seg, n)
kernel_name = 'mk_decoder_postln_d2_seqx_r8_729a65'

def setup_inputs(seed: int=0):
    np.random.seed(seed)
    _w = jnp.asarray

    def _rec_inputs():
        import jax
        import jax.numpy as jnp
        _rk = jax.random.key(seed)
        x = -0.000125 + 0.9999 * jax.random.normal(jax.random.fold_in(_rk, 1), (4, 256, 256), jnp.float32)
        _lenS = 256 - jax.random.randint(jax.random.fold_in(_rk, 7), (4,), 0, max(1, 256 // 4) + 1, jnp.int32)
        _lenS2 = 256 - jax.random.randint(jax.random.fold_in(_rk, 8), (4,), 0, max(1, 256 // 4) + 1, jnp.int32)
        itok_BxS_13_99985 = jax.random.randint(jax.random.fold_in(_rk, 11), (4, 256), 13, 99986, jnp.int32)
        _ctx_2048P = jax.random.normal(jax.random.fold_in(_rk, 12), (4, 16, 256), jnp.float32)
        _ctx_2048c = jax.random.dirichlet(jax.random.fold_in(_rk, 512), 0.3 * jnp.ones((16,), jnp.float32), (4, 256))
        _ctx_2048t = jnp.einsum('bsk,bkd->bsd', _ctx_2048c, _ctx_2048P)
        _ctx_2048t = _ctx_2048t * jax.lax.rsqrt(jnp.mean(jnp.square(_ctx_2048t)) + 1e-12) * 0.953939
        ctx_2048 = 6.82029e-06 + 0.0200006 * (_ctx_2048t + 0.3 * jax.random.normal(jax.random.fold_in(_rk, 612), (4, 256, 256), jnp.float32))
        itok_BxS_0_1023 = jax.random.randint(jax.random.fold_in(_rk, 13), (4, 256), 0, 128, jnp.int32)
        return (x, itok_BxS_13_99985, ctx_2048, itok_BxS_0_1023)
    x, itok_BxS_13_99985, ctx_2048, itok_BxS_0_1023 = _rec_inputs()

    def _L0_attn_setup():
        import jax, jax.numpy as jnp
        import numpy as np
        import math
        H = 256
        NH = 16
        HD = H // NH
        THETA = 10000.0

        def rotate_half(x):
            x1, x2 = (x[..., :HD // 2], x[..., HD // 2:])
            return jnp.concatenate((-x2, x1), axis=-1)

        def rope_tables(seq_len, dtype):
            inv_freq = 1.0 / THETA ** (np.arange(0, HD, 2, dtype=np.float32) / HD)
            t = np.arange(seq_len, dtype=np.float32)
            freqs = np.einsum('i,j->ij', t, inv_freq)
            emb = np.concatenate((freqs, freqs), axis=-1)
            return (jnp.asarray(np.cos(emb), dtype), jnp.asarray(np.sin(emb), dtype))
        key = jax.random.key(seed)
        ks = jax.random.split(key, 5)
        B, S = (2, 256)
        scale = 1.0 / math.sqrt(H)
        return {'hidden_states': jax.random.normal(ks[0], (B, S, H), jnp.float32), 'Wq': jax.random.normal(ks[1], (H, H), jnp.float32) * scale, 'Wk': jax.random.normal(ks[2], (H, H), jnp.float32) * scale, 'Wv': jax.random.normal(ks[3], (H, H), jnp.float32) * scale, 'Wo': jax.random.normal(ks[4], (H, H), jnp.float32) * scale}
    _L0_attn_all = _L0_attn_setup()
    _L0_attn_in = {k: v for k, v in _L0_attn_all.items() if k in ('Wq', 'Wk', 'Wv', 'Wo')}
    del _L0_attn_all

    def _L0_xattn_setup():
        import jax, jax.numpy as jnp
        import numpy as np
        B, S, D = (4, 512, 256)
        E = 4
        F = 1024 // E
        VOCAB = 12500
        key = jax.random.key(seed)
        k1, k2, k3, k4, k5 = jax.random.split(key, 5)
        hidden_states = jax.random.normal(k1, (B, S, D), dtype=jnp.float32)
        token_ids = jax.random.randint(k2, (B, S), 0, VOCAB, dtype=jnp.int64)
        Wg = jax.random.normal(k3, (E, F, D), dtype=jnp.float32) * 0.02
        Wu = jax.random.normal(k4, (E, F, D), dtype=jnp.float32) * 0.02
        Wd = jax.random.normal(k5, (E, D, F), dtype=jnp.float32) * 0.02
        return {'hidden_states': hidden_states, 'token_ids': token_ids, 'Wg': Wg, 'Wu': Wu, 'Wd': Wd}
    _L0_xattn_all = _L0_xattn_setup()
    _L0_xattn_in = {k: v for k, v in _L0_xattn_all.items() if k in ()}
    del _L0_xattn_all

    def _L0_ffn_setup():
        import jax, jax.numpy as jnp
        import numpy as np
        B, S, D, K, R = (4, 256, 256, 8, 64)
        key = jax.random.key(seed)
        ks = jax.random.split(key, 7)
        x = jax.random.normal(ks[0], (B, S, D), dtype=jnp.float32)
        U = jax.random.normal(ks[1], (K, D, R), dtype=jnp.float32) * 0.02
        V = jax.random.normal(ks[2], (K, R, D), dtype=jnp.float32) * 0.02
        W1 = jax.random.normal(ks[3], (D, D), dtype=jnp.float32) * 0.02
        b1 = jnp.zeros((D,), dtype=jnp.float32)
        W2 = jax.random.normal(ks[4], (D, K), dtype=jnp.float32) * 0.02
        b2 = jnp.zeros((K,), dtype=jnp.float32)
        return {'x': x, 'U': U, 'V': V, 'W1': W1, 'b1': b1, 'W2': W2, 'b2': b2}
    _L0_ffn_all = _L0_ffn_setup()
    _L0_ffn_in = {k: v for k, v in _L0_ffn_all.items() if k in ('U', 'V', 'W1', 'b1', 'W2', 'b2')}
    del _L0_ffn_all

    def _L1_attn_setup():
        import jax, jax.numpy as jnp
        import numpy as np
        BATCH, SEQ, EMBED, STATE = (4, 256, 256, 16)
        key = jax.random.key(seed)
        ks = jax.random.split(key, 8)
        s = 0.02
        return {'x': jax.random.normal(ks[0], (BATCH, SEQ, EMBED), jnp.float32), 'proj_in_w': jax.random.normal(ks[1], (EMBED, EMBED), jnp.float32) * s, 'proj_in_b': jnp.zeros((EMBED,), jnp.float32), 'proj_out_w': jax.random.normal(ks[2], (EMBED, EMBED), jnp.float32) * s, 'proj_out_b': jnp.zeros((EMBED,), jnp.float32), 'A': jax.random.normal(ks[3], (EMBED, STATE), jnp.float32) * 0.01, 'B_w': jax.random.normal(ks[4], (STATE, EMBED), jnp.float32) * s, 'C_w': jax.random.normal(ks[5], (EMBED, STATE), jnp.float32) * s, 'D_param': jnp.ones((EMBED,), jnp.float32)}
    _L1_attn_all = _L1_attn_setup()
    _L1_attn_in = {k: v for k, v in _L1_attn_all.items() if k in ('proj_in_w', 'proj_in_b', 'proj_out_w', 'proj_out_b', 'A', 'B_w', 'C_w', 'D_param')}
    del _L1_attn_all

    def _L1_xattn_setup():
        import jax, jax.numpy as jnp
        import numpy as np
        B, Lq, Lk = (2, 512, 128)
        Q_DIM, KV_DIM = (256, 256)
        H, HD = (16, 128)
        KVC, QC, R = (64, 96, 64)
        LOOKBACK = 8
        NEG = -1e+30

        def _rope(x, L):
            half = x.shape[-1] // 2
            inv_freq = 1.0 / 10000.0 ** (jnp.arange(half, dtype=jnp.float32) / half)
            ang = jnp.arange(L, dtype=jnp.float32)[:, None] * inv_freq
            cos, sin = (jnp.cos(ang), jnp.sin(ang))
            x1, x2 = (x[..., :half], x[..., half:])
            return jnp.concatenate([x1 * cos - x2 * sin, x1 * sin + x2 * cos], axis=-1)
        key = jax.random.key(seed)
        ks = jax.random.split(key, 11)

        def w(k, shape, fan_in):
            return jax.random.normal(k, shape, jnp.float32) / np.sqrt(fan_in).astype(np.float32)
        return {'q': jax.random.normal(ks[0], (B, Lq, Q_DIM), jnp.float32), 'kv': jax.random.normal(ks[1], (B, Lk, KV_DIM), jnp.float32), 'seg_id': jnp.sort(jax.random.randint(ks[2], (B, Lq), 0, Lk), axis=-1), 'W_kvc': w(ks[3], (KV_DIM, KVC), KV_DIM), 'W_dq': w(ks[4], (Q_DIM, QC), Q_DIM), 'W_uq': w(ks[5], (QC, H * HD), QC), 'W_qr': w(ks[6], (QC, H * R), QC), 'W_uk': w(ks[7], (KVC, H * HD), KVC), 'W_kr': w(ks[8], (KVC, R), KVC), 'W_uv': w(ks[9], (KVC, H * HD), KVC), 'W_o': w(ks[10], (H * HD, Q_DIM), H * HD)}
    _L1_xattn_all = _L1_xattn_setup()
    _L1_xattn_in = {k: v for k, v in _L1_xattn_all.items() if k in ('W_kvc', 'W_dq', 'W_uq', 'W_qr', 'W_uk', 'W_kr', 'W_uv', 'W_o')}
    del _L1_xattn_all

    def _L1_ffn_setup():
        import jax, jax.numpy as jnp
        import numpy as np
        B, S, D = (2, 256, 256)
        MOE_D = 176
        E = 16
        K = 6
        ALPHA = 0.001

        def _moe_forward(x, gate_w, w_gate, w_up, w_down):
            b, s, d = x.shape
            T = b * s
            h = x.reshape(T, d)
            logits = h @ gate_w.T
            scores = jax.nn.softmax(logits.astype(jnp.float32), axis=-1)
            topk_w, topk_idx = jax.lax.top_k(scores, K)
            cw = jnp.zeros((T, E), jnp.float32)
            cw = cw.at[jnp.arange(T)[:, None], topk_idx].add(topk_w)
            y = jnp.zeros((T, d), x.dtype)
            for e in range(E):
                g = h @ w_gate[e].T
                u = h @ w_up[e].T
                out = jax.nn.silu(g) * u @ w_down[e].T
                y = y + cw[:, e:e + 1].astype(x.dtype) * out
            counts = jnp.sum(jax.nn.one_hot(topk_idx.reshape(b, s * K), E, dtype=jnp.float32), axis=1)
            ce = counts * (E / (s * K))
            scores_bse = scores.reshape(b, s, E)
            aux = jnp.mean(jnp.sum(ce * scores_bse.mean(axis=1), axis=1)) * ALPHA
            return (y.reshape(b, s, d), aux)
        key = jax.random.key(seed)
        ks = jax.random.split(key, 5)
        sd = 1.0 / np.sqrt(D)
        sm = 1.0 / np.sqrt(MOE_D)
        return {'x': jax.random.normal(ks[0], (B, S, D), jnp.float32), 'gate_w': jax.random.normal(ks[1], (E, D), jnp.float32) * sd, 'w_gate': jax.random.normal(ks[2], (E, MOE_D, D), jnp.float32) * sd, 'w_up': jax.random.normal(ks[3], (E, MOE_D, D), jnp.float32) * sd, 'w_down': jax.random.normal(ks[4], (E, D, MOE_D), jnp.float32) * sm}
    _L1_ffn_all = _L1_ffn_setup()
    _L1_ffn_in = {k: v for k, v in _L1_ffn_all.items() if k in ('gate_w', 'w_gate', 'w_up', 'w_down')}
    del _L1_ffn_all
    return {'x': x, 'itok_BxS_13_99985': itok_BxS_13_99985, 'ctx_2048': ctx_2048, 'itok_BxS_0_1023': itok_BxS_0_1023, 'L0_attn_Wq': _L0_attn_in['Wq'], 'L0_attn_Wk': _L0_attn_in['Wk'], 'L0_attn_Wv': _L0_attn_in['Wv'], 'L0_attn_Wo': _L0_attn_in['Wo'], 'L0_ffn_U': _L0_ffn_in['U'], 'L0_ffn_V': _L0_ffn_in['V'], 'L0_ffn_W1': _L0_ffn_in['W1'], 'L0_ffn_b1': _L0_ffn_in['b1'], 'L0_ffn_W2': _L0_ffn_in['W2'], 'L0_ffn_b2': _L0_ffn_in['b2'], 'L1_attn_proj_in_w': _L1_attn_in['proj_in_w'], 'L1_attn_proj_in_b': _L1_attn_in['proj_in_b'], 'L1_attn_proj_out_w': _L1_attn_in['proj_out_w'], 'L1_attn_proj_out_b': _L1_attn_in['proj_out_b'], 'L1_attn_A': _L1_attn_in['A'], 'L1_attn_B_w': _L1_attn_in['B_w'], 'L1_attn_C_w': _L1_attn_in['C_w'], 'L1_attn_D_param': _L1_attn_in['D_param'], 'L1_xattn_W_kvc': _L1_xattn_in['W_kvc'], 'L1_xattn_W_dq': _L1_xattn_in['W_dq'], 'L1_xattn_W_uq': _L1_xattn_in['W_uq'], 'L1_xattn_W_qr': _L1_xattn_in['W_qr'], 'L1_xattn_W_uk': _L1_xattn_in['W_uk'], 'L1_xattn_W_kr': _L1_xattn_in['W_kr'], 'L1_xattn_W_uv': _L1_xattn_in['W_uv'], 'L1_xattn_W_o': _L1_xattn_in['W_o'], 'L1_ffn_gate_w': _L1_ffn_in['gate_w'], 'L1_ffn_w_gate': _L1_ffn_in['w_gate'], 'L1_ffn_w_up': _L1_ffn_in['w_up'], 'L1_ffn_w_down': _L1_ffn_in['w_down']}

def reference(x, itok_BxS_13_99985, ctx_2048, itok_BxS_0_1023, L0_attn_Wq, L0_attn_Wk, L0_attn_Wv, L0_attn_Wo, L0_ffn_U, L0_ffn_V, L0_ffn_W1, L0_ffn_b1, L0_ffn_W2, L0_ffn_b2, L1_attn_proj_in_w, L1_attn_proj_in_b, L1_attn_proj_out_w, L1_attn_proj_out_b, L1_attn_A, L1_attn_B_w, L1_attn_C_w, L1_attn_D_param, L1_xattn_W_kvc, L1_xattn_W_dq, L1_xattn_W_uq, L1_xattn_W_qr, L1_xattn_W_uk, L1_xattn_W_kr, L1_xattn_W_uv, L1_xattn_W_o, L1_ffn_gate_w, L1_ffn_w_gate, L1_ffn_w_up, L1_ffn_w_down):
    import jax
    import jax.numpy as jnp

    def _L0_attn_ref(hidden_states, Wq, Wk, Wv, Wo):
        import jax, jax.numpy as jnp
        import numpy as np
        import math
        H = 256
        NH = 16
        HD = H // NH
        THETA = 10000.0

        def rotate_half(x):
            x1, x2 = (x[..., :HD // 2], x[..., HD // 2:])
            return jnp.concatenate((-x2, x1), axis=-1)

        def rope_tables(seq_len, dtype):
            inv_freq = 1.0 / THETA ** (np.arange(0, HD, 2, dtype=np.float32) / HD)
            t = np.arange(seq_len, dtype=np.float32)
            freqs = np.einsum('i,j->ij', t, inv_freq)
            emb = np.concatenate((freqs, freqs), axis=-1)
            return (jnp.asarray(np.cos(emb), dtype), jnp.asarray(np.sin(emb), dtype))
        B, S, _ = hidden_states.shape

        def proj(W):
            y = jnp.einsum('bsh,oh->bso', hidden_states, W)
            return y.reshape(B, S, NH, HD).transpose(0, 2, 1, 3)
        q, k, v = (proj(Wq), proj(Wk), proj(Wv))
        cos, sin = rope_tables(S, hidden_states.dtype)
        cos, sin = (cos[None, None], sin[None, None])
        q = q * cos + rotate_half(q) * sin
        k = k * cos + rotate_half(k) * sin
        scores = jnp.einsum('bhqd,bhkd->bhqk', q, k) / math.sqrt(HD)
        causal = jnp.triu(jnp.ones((S, S), bool), k=1)
        scores = jnp.where(causal, -jnp.inf, scores)
        attn = jax.nn.softmax(scores, axis=-1)
        out = jnp.einsum('bhqk,bhkd->bhqd', attn, v)
        out = out.transpose(0, 2, 1, 3).reshape(B, S, H)
        return jnp.einsum('bsh,oh->bso', out, Wo)

    def _L0_xattn_ref(hidden_states, token_ids, Wg, Wu, Wd):
        import jax, jax.numpy as jnp
        import numpy as np
        B, S, D = (4, 512, 256)
        E = 4
        F = 1024 // E
        VOCAB = 12500
        tokens_per_expert = VOCAB // E
        tid = jnp.clip(token_ids, 0, VOCAB - 1)
        expert_ids = jnp.minimum(tid // tokens_per_expert, E - 1)
        out = jnp.zeros_like(hidden_states)
        for e in range(E):
            g = jax.nn.silu(jnp.einsum('bsd,fd->bsf', hidden_states, Wg[e]))
            u = jnp.einsum('bsd,fd->bsf', hidden_states, Wu[e])
            y = jnp.einsum('bsf,df->bsd', g * u, Wd[e])
            out = jnp.where((expert_ids == e)[..., None], y, out)
        return out

    def _L0_ffn_ref(x, U, V, W1, b1, W2, b2):
        import jax, jax.numpy as jnp
        import numpy as np
        B, S, D, K, R = (4, 256, 256, 8, 64)
        h = jax.nn.relu(jnp.einsum('bsd,de->bse', x, W1) + b1)
        alpha = jax.nn.softmax(jnp.einsum('bse,ek->bsk', h, W2) + b2, axis=-1)
        vx = jnp.einsum('krd,bsd->bskr', V, x)
        uvx = jnp.einsum('kdr,bskr->bskd', U, vx)
        out = jnp.einsum('bsk,bskd->bsd', alpha, uvx)
        return out

    def _L1_attn_ref(x, proj_in_w, proj_in_b, proj_out_w, proj_out_b, A, B_w, C_w, D_param):
        import jax, jax.numpy as jnp
        import numpy as np
        BATCH, SEQ, EMBED, STATE = (4, 256, 256, 16)
        x_proj = x @ proj_in_w.T + proj_in_b
        delta = jax.nn.softplus(x_proj @ B_w.T)
        sigA = jax.nn.sigmoid(A)
        Bsz, L, D = x.shape
        S = A.shape[1]

        def step(h, inp):
            x_t, d_t = inp
            h = h * sigA + x_t[:, :, None] * d_t[:, None, :]
            y_t = h.sum(axis=1) @ C_w.T + D_param * x_t
            return (h, y_t)
        h0 = jnp.zeros((Bsz, D, S), x.dtype)
        xs = (jnp.swapaxes(x_proj, 0, 1), jnp.swapaxes(delta, 0, 1))
        _, ys = jax.lax.scan(step, h0, xs)
        y = jnp.swapaxes(ys, 0, 1)
        y = y @ proj_out_w.T + proj_out_b
        return y + x

    def _L1_xattn_ref(q, kv, seg_id, W_kvc, W_dq, W_uq, W_qr, W_uk, W_kr, W_uv, W_o):
        import jax, jax.numpy as jnp
        import numpy as np
        B, Lq, Lk = (2, 512, 128)
        Q_DIM, KV_DIM = (256, 256)
        H, HD = (16, 128)
        KVC, QC, R = (64, 96, 64)
        LOOKBACK = 8
        NEG = -1e+30

        def _rope(x, L):
            half = x.shape[-1] // 2
            inv_freq = 1.0 / 10000.0 ** (jnp.arange(half, dtype=jnp.float32) / half)
            ang = jnp.arange(L, dtype=jnp.float32)[:, None] * inv_freq
            cos, sin = (jnp.cos(ang), jnp.sin(ang))
            x1, x2 = (x[..., :half], x[..., half:])
            return jnp.concatenate([x1 * cos - x2 * sin, x1 * sin + x2 * cos], axis=-1)
        b, lq, _ = q.shape
        lk = kv.shape[1]
        kv_c = kv @ W_kvc
        q_c = q @ W_dq
        q_nope = (q_c @ W_uq).reshape(b, lq, H, HD).transpose(0, 2, 1, 3)
        q_rope = (q_c @ W_qr).reshape(b, lq, H, R).transpose(0, 2, 1, 3)
        k_nope = (kv_c @ W_uk).reshape(b, lk, H, HD)
        v = (kv_c @ W_uv).reshape(b, lk, H, HD)
        k_rope = kv_c @ W_kr
        q_rope = _rope(q_rope, lq)
        k_rope = _rope(k_rope, lk)
        scale = 1.0 / np.sqrt(HD + R).astype(np.float32)
        scores = (jnp.einsum('bhqd,bkhd->bhqk', q_nope, k_nope) + jnp.einsum('bhqr,bkr->bhqk', q_rope, k_rope)) * scale
        k_ids = jnp.arange(lk)[None, None, :]
        qs = seg_id[:, :, None]
        good = (k_ids <= qs) & (k_ids >= qs - LOOKBACK)
        scores = jnp.where(good[:, None, :, :], scores, NEG)
        attn = jax.nn.softmax(scores, axis=-1)
        out = jnp.einsum('bhqk,bkhd->bqhd', attn, v).reshape(b, lq, H * HD)
        return out @ W_o

    def _L1_ffn_ref(x, gate_w, w_gate, w_up, w_down):
        import jax, jax.numpy as jnp
        import numpy as np
        B, S, D = (2, 256, 256)
        MOE_D = 176
        E = 16
        K = 6
        ALPHA = 0.001

        def _moe_forward(x, gate_w, w_gate, w_up, w_down):
            b, s, d = x.shape
            T = b * s
            h = x.reshape(T, d)
            logits = h @ gate_w.T
            scores = jax.nn.softmax(logits.astype(jnp.float32), axis=-1)
            topk_w, topk_idx = jax.lax.top_k(scores, K)
            cw = jnp.zeros((T, E), jnp.float32)
            cw = cw.at[jnp.arange(T)[:, None], topk_idx].add(topk_w)
            y = jnp.zeros((T, d), x.dtype)
            for e in range(E):
                g = h @ w_gate[e].T
                u = h @ w_up[e].T
                out = jax.nn.silu(g) * u @ w_down[e].T
                y = y + cw[:, e:e + 1].astype(x.dtype) * out
            counts = jnp.sum(jax.nn.one_hot(topk_idx.reshape(b, s * K), E, dtype=jnp.float32), axis=1)
            ce = counts * (E / (s * K))
            scores_bse = scores.reshape(b, s, E)
            aux = jnp.mean(jnp.sum(ce * scores_bse.mean(axis=1), axis=1)) * ALPHA
            return (y.reshape(b, s, d), aux)
        y, _aux = _moe_forward(x, gate_w, w_gate, w_up, w_down)
        return y
    x = _layernorm(x + _L0_attn_ref(x, L0_attn_Wq, L0_attn_Wk, L0_attn_Wv, L0_attn_Wo), axis=-1)
    x = _layernorm(x + _L0_xattn_ref(x, itok_BxS_13_99985, ctx_2048, ctx_2048, ctx_2048), axis=-1)
    x = _layernorm(x + _L0_ffn_ref(x, L0_ffn_U, L0_ffn_V, L0_ffn_W1, L0_ffn_b1, L0_ffn_W2, L0_ffn_b2), axis=-1)
    x = _layernorm(x + _L1_attn_ref(x, L1_attn_proj_in_w, L1_attn_proj_in_b, L1_attn_proj_out_w, L1_attn_proj_out_b, L1_attn_A, L1_attn_B_w, L1_attn_C_w, L1_attn_D_param), axis=-1)
    x = _layernorm(x + _L1_xattn_ref(x, ctx_2048, itok_BxS_0_1023, L1_xattn_W_kvc, L1_xattn_W_dq, L1_xattn_W_uq, L1_xattn_W_qr, L1_xattn_W_uk, L1_xattn_W_kr, L1_xattn_W_uv, L1_xattn_W_o), axis=-1)
    x = _layernorm(x + _L1_ffn_ref(x, L1_ffn_gate_w, L1_ffn_w_gate, L1_ffn_w_up, L1_ffn_w_down), axis=-1)
    return x

_drawn_inputs = setup_inputs


def setup_inputs(seed=0):
    import zlib

    import numpy as np

    out = dict(_drawn_inputs(seed))
    spreads = {'L0_ffn_b1': (0.0, 0.8),
     'L0_ffn_b2': (0.0, 0.8),
     'L1_attn_proj_in_b': (0.0, 0.339),
     'L1_attn_proj_out_b': (0.0, 0.1),
     'L1_attn_D_param': (1.0, 0.6)}
    factors = {'L0_ffn_U': 2.675,
     'L0_ffn_V': 2.689,
     'L0_ffn_W1': 8.0,
     'L0_ffn_W2': 8.0,
     'L1_attn_A': 8.0,
     'L1_attn_B_w': 8.0,
     'L1_xattn_W_kvc': 4.099,
     'L1_xattn_W_dq': 8.0,
     'L1_xattn_W_uq': 8.0,
     'L1_xattn_W_qr': 8.0,
     'L1_xattn_W_uk': 8.0,
     'L1_xattn_W_kr': 8.0,
     'L1_xattn_W_uv': 4.111,
     'L1_xattn_W_o': 3.955}
    for name, (base, spread) in spreads.items():
        noise = np.random.default_rng([zlib.crc32(name.encode()), seed]).standard_normal(out[name].shape)
        drawn = base * np.exp(spread * noise) if base else spread * noise
        out[name] = jnp.asarray(drawn.astype(out[name].dtype))
    for name, factor in factors.items():
        out[name] = (out[name] * factor).astype(out[name].dtype)
    return out
```

```python
def build(nc, d, out):
    import numpy as np
    from concourse import mybir
    from contextlib import ExitStack

    f32, bf16, i32, u16 = mybir.dt.float32, mybir.dt.bfloat16, mybir.dt.int32, mybir.dt.uint16
    ALU = mybir.AluOpType
    ACT = mybir.ActivationFunctionType
    AX = mybir.AxisListType.X

    B, S, D = 4, 256, 256
    P = 128
    T = B * S
    NT = T // P
    DC = D // P
    HALF = 512
    NH = 16
    NPAIR = NH // 2
    PAD = 32
    HD0 = 16
    EPS = 1e-5
    QC, KVC = 96, 64
    MLA_SCALE = float((128 + 64) ** -0.5)
    ST = 16
    NE, FF = 16, 176
    FCH = NE * FF // P
    TOPK = 6
    NEG = -float(np.frombuffer(np.uint32(np.float32(1e30).view(np.uint32) & 0xFFFF0000).tobytes(), np.float32)[0])
    LATQ = 5
    E0, F0 = 4, 256
    PER_EXPERT = 12500 // E0

    ctx = ExitStack()
    with ctx:
        def sb(name, shape, dt=f32):
            return ctx.enter_context(nc.sbuf_tensor(name, shape, dt))

        sems = {}

        def sem(name):
            if name not in sems:
                sems[name] = ctx.enter_context(nc.semaphore(name))
            return sems[name]

        x_tok = sb("x_tok", [P, NT, D])
        xT = sb("xT", [P, DC, T])
        A = sb("A", [P, 16384])
        Wb = sb("Wb", [P, 2 * DC * 2816])
        C = sb("C", [P, 8192])
        ctxT = sb("ctxT", [P, B, DC, 256])
        probs = sb("probs", [P, 4, 2, 256])
        probsT = sb("probsT", [P, 2, 2, 2, 256])
        ident = sb("ident", [P, P])
        ident_b = sb("ident_b", [P, P], bf16)
        qk_fold = sb("qk_fold", [QC, NPAIR, P])
        vo_fold = sb("vo_fold", [P, NPAIR, D])
        neg_max = sb("neg_max", [P, 4, 2])
        row_sum = sb("row_sum", [P, 4, 2])
        row_rec = sb("row_rec", [P, 4, 2])
        stats = sb("stats", [P, NT, 6])
        meanvar = sb("meanvar", [P, NT, 2])
        veps = sb("veps", [P, NT])
        rstd = sb("rstd", [P, NT])
        minus_half = sb("minus_half", [P, NT])
        vecs = sb("vecs", [P, 8, 2])
        rows = sb("rows", [1, 8 + 256 + 128])
        small = sb("small", [P, 12, 128])
        small_b = sb("small_b", [P, 128], bf16)
        decay = sb("decay", [P, DC, ST])
        wBT = sb("wBT", [P, DC, ST])
        wgateT = sb("wgateT", [P, DC, NE])
        w2s = sb("w2s", [P, DC, 8])
        pieces = sb("pieces", [P, NT, 48])
        onesel = sb("onesel", [P, 4, 32])
        e16 = sb("e16", [48, ST], bf16)
        piecesT = sb("piecesT", [48, T], bf16)
        seg_i = sb("seg_i", [P, NT], i32)
        seg_f = sb("seg_f", [P, NT])
        top8 = sb("top8", [P, NT, 8])
        bank = [ctx.enter_context(nc.psum_tensor(f"bank{i}", [P, 512], f32)) for i in range(8)]

        def view(t, at, shape, dt=None):
            n = 1
            for k in shape[1:]:
                n *= k
            v = t[0:shape[0], at:at + n]
            if len(shape) == 3:
                v = v.rearrange("p (a b) -> p a b", a=shape[1])
            if len(shape) == 4:
                v = v.rearrange("p (a b c) -> p a b c", a=shape[1], b=shape[2])
            return v

        ctx_flat = ctxT[:, :, :, :].rearrange("p b c t -> p (b c t)")
        mask_m = ctx_flat[:, 0:1024].bitcast(bf16).rearrange("p (i k) -> p i k", i=NT)
        tab_qc = ctx_flat[:, 1024:1280]
        tab_qs = ctx_flat[:, 1280:1536]
        reset = ctx_flat[:, 1536:1664]
        distance = ctx_flat[:, 1664:1920]
        qT = view(A, 0, [P, 4, T])
        kT = view(A, 4096, [P, 4, T])
        v_pad = view(A, 8192, [P, NT, NH * PAD])
        oT = view(A, 12288, [P, 4, T])
        wq = view(C, 0, [P, DC, 512])
        wk_raw = view(C, 1024, [P, DC, 512])
        wk_swp = view(C, 2048, [P, DC, 512])
        wv = view(C, 3072, [P, DC, D])
        wo_pad = view(C, 3584, [P, 4, D])
        tab_q = view(C, 4608, [P, S])
        tab_c = view(C, 4864, [P, S])
        tab_s = view(C, 5120, [P, S])
        w1 = view(C, 5376, [P, DC, D])
        vT = view(C, 5888, [P, DC, 512])
        uw = view(C, 6912, [P, 4, D])
        causal = sb("causal", [P, P])
        causal_b = sb("causal_b", [P, P], bf16)
        w_uqT = view(Wb, 0, [P, NH, QC])
        w_ukT = view(Wb, 1536, [P, NH, KVC])
        w_uvT = view(Wb, 2560, [P, NH, KVC])
        w_o = view(Wb, 3584, [P, NH, D])
        tid_f = view(Wb, 7680, [P, T])
        emask = [view(Wb, 8704 + 512 * e, [P, 512]).bitcast(bf16) for e in range(E0)]
        tid_i = probsT[:, 0].rearrange("p a b c -> p (a b c)").bitcast(i32)
        lt_tmp = probsT[:, 1].rearrange("p a b c -> p (a b c)")
        pinT = view(Wb, 0, [P, DC, D])
        poutT = view(Wb, 512, [P, DC, D])
        CwP = view(Wb, 1024, [P, DC, P])
        gateT = view(Wb, 0, [P, DC, NE * FF])
        upT = view(Wb, DC * NE * FF, [P, DC, NE * FF])
        hid0 = view(A, 0, [P, 8, T])
        silu0 = view(A, 8192, [P, 4, HALF])
        h1T = view(A, 0, [P, DC, T])
        bc_s = view(A, 2048, [P, 2, HALF])
        vxa = view(A, 4096, [P, 4, T])
        xpT = view(A, 0, [P, DC, T])
        dl = view(A, 2048, [P, 4, T])
        hs = view(A, 6144, [P, 2, 4 * T]).rearrange("p r (j t) -> p r j t", j=4)
        zT = probs[:, 0:2].rearrange("p a b c -> p (a b c)")
        qm = view(A, 0, [P, 2 * NH, S])
        om = view(A, 8192, [P, NPAIR, T])
        keys_a = view(C, 0, [P, T])
        keys_b = view(C, 1024, [P, T])
        kv_tok = view(C, 2048, [P, NT, KVC])
        qcT = view(C, 2560, [QC, T])
        wqr_raw = view(C, 3584, [QC, NPAIR, P])
        wqr_swp = view(C, 4608, [QC, NPAIR, P])
        w_dq = view(C, 5632, [P, DC, QC])
        w_kvc = view(C, 5824, [P, DC, P])
        w_kr = view(C, 6080, [KVC, 2, P])
        tab_kc = view(C, 6336, [P, S])
        tab_ks = view(C, 6592, [P, S])
        iota4 = view(C, 6848, [P, 256])
        ropes = view(C, 7104, [P, 2, 512])
        downT = view(A, 0, [P, FCH, D])
        silu1 = view(A, 5632, [P, 2, HALF])
        hid1 = probsT[:, :].rearrange("p r a b c -> p (r a) (b c)")
        sel_e = probs[0:48, 0:3].rearrange("p a b c -> p (a b c)")[:, 0:1408].bitcast(bf16)

        def bc(ap, n, dim=1):
            v = ap.unsqueeze(dim)
            shape = list(v.shape)
            shape[dim] = n
            return v.broadcast_to(shape)

        LOADS = {
            "ld_first": ("xT", "wq", "tab_q"), "ld_keys": ("wk_raw", "wk_swp", "tab_c", "tab_s", "wv"),
            "ld_const": ("ident", "causal", "x_tok", "tid"),
            "ld_fold": ("wo_pad", "w_uqT", "w_ukT", "w_uvT", "w_o"), "ld_ctx": ("ctxT",),
            "ld_ffn": ("w1", "vT", "uw", "w2s", "vecs", "rows", "wBT", "onesel", "e16", "seg", "wgateT"),
            "ld_decay": ("decay",), "ld_scan": ("pinT", "poutT", "CwP"),
            "ld_latent": ("wqr_raw", "wqr_swp", "w_dq", "w_kvc", "w_kr", "tab_kc", "tab_ks", "iota4"),
            "ld_tabs": ("tab_qc", "tab_qs", "reset"), "ld_up": ("gateT", "upT"), "ld_down": ("downT", "sel_e"),
        }
        GROUP = {name: g for g, names in LOADS.items() for name in names}

        def loaded(eng, *names):
            for g in sorted({GROUP[n] for n in names}):
                eng.wait_ge(sem(g), 16 * len(LOADS[g]))

        def copy_probs(eng, n, v, causal_keys, copy, which):
            g, kcs = v // 2, 1 + v % 2 if causal_keys else 2
            eng.wait_ge(sem(n + "tr"), v + 1)
            if g >= 2:
                eng.wait_ge(sem(n + "av"), g - 1)
            src = bank[2 + v % 2][:, 0:kcs * 256].rearrange("p (k j q) -> p k j q", k=kcs, j=2)
            copy(probsT[:, g % 2, 0:kcs, :, (v % 2) * P:(v % 2 + 1) * P], src
                 ).then_inc(sem(n + "pT" + which), 1)

        block = ctx.enter_context(nc.Block())

        @block.sync
        def _(sp):
            def load(name, dst, src=None):
                sp.dma_start(dst, d[name] if src is None else src).then_inc(sem(GROUP[name]), 16)

            load("xT", xT[:, :, :])
            load("wq", wq)
            load("tab_q", tab_q)
            load("wk_raw", wk_raw)
            load("wk_swp", wk_swp)
            load("tab_c", tab_c)
            load("tab_s", tab_s)
            load("wv", wv)
            load("ident", ident[:, :])
            load("causal", causal[:, :])
            load("x_tok", x_tok[:, :, :])
            load("tid", tid_i, d["tid"].partition_broadcast(P))
            load("wo_pad", wo_pad)
            load("w_uqT", w_uqT)
            load("w_ukT", w_ukT)
            load("w_uvT", w_uvT)
            load("w_o", w_o)
            load("ctxT", ctxT[:, :, :, :])
            load("w1", w1)
            load("vT", vT)
            load("uw", uw)
            load("w2s", w2s[:, :, :])
            load("vecs", vecs[:, :, :])
            load("rows", rows[:, :])
            load("decay", decay[:, :, :])
            load("wBT", wBT[:, :, :])
            load("onesel", onesel[:, :, :])
            load("e16", e16[:, :].bitcast(u16))
            load("seg", seg_i[:, :])
            load("wgateT", wgateT[:, :, :])
            sp.wait_ge(sem("fold_vo"), 1)
            load("pinT", pinT)
            load("poutT", poutT)
            load("CwP", CwP)
            sp.wait_ge(sem("fin2"), NT)
            load("wqr_raw", wqr_raw)
            load("wqr_swp", wqr_swp)
            load("w_dq", w_dq)
            load("w_kvc", w_kvc)
            load("w_kr", w_kr)
            load("tab_kc", tab_kc)
            load("tab_ks", tab_ks)
            load("iota4", iota4)
            sp.wait_ge(sem("fin3"), NT)
            sp.wait_ge(sem("k_tok"), 1)
            load("tab_qc", tab_qc)
            load("tab_qs", tab_qs)
            load("reset", reset)
            load("gateT", gateT)
            load("upT", upT)
            sp.wait_ge(sem("fin4"), NT)
            load("downT", downT)
            load("sel_e", sel_e.bitcast(u16))
            for i in range(NT):
                sp.wait_ge(sem("ln5_x"), i + 1)
                sp.dma_start(out[i], x_tok[:, i, :]).then_inc(sem("stored"), 16)
            sp.wait_ge(sem("stored"), 16 * NT)

        @block.tensor
        def _(pe):
            mm = pe.matmul

            def ln_transposes(k):
                for q in range(NT // 2):
                    pe.wait_ge(sem(f"ln{k}_x"), 2 * q + 2)
                    if q >= 2:
                        pe.wait_ge(sem(f"ln{k}_xT"), q - 1)
                    for j in range(2):
                        for c in range(DC):
                            o = (2 * j + c) * P
                            last = pe.transpose(bank[4 + q % 2][:, o:o + P],
                                                x_tok[:, 2 * q + j, c * P:(c + 1) * P], ident[:, :])
                    last.then_inc(sem(f"ln{k}_t"), 1)

            def final(k, tiles, emit):
                for i in tiles:
                    if i >= 2:
                        pe.wait_ge(sem(f"ln{k}_r"), i - 1)
                    emit(i, bank[6 + i % 2][:, 0:D]).then_inc(sem(f"fin{k}"), 1)

            def proj(o, w, col, half, m=P):
                for c in range(DC):
                    last = mm(o, w[:, c, col:col + m], xT[:, c, half * HALF:(half + 1) * HALF],
                              start=(c == 0), stop=(c == DC - 1))
                return last

            def attention(n, scores, apply, causal_keys, ring):
                U = 2 * B * NPAIR
                for u in range(U + 6):
                    if u < U:
                        if u >= len(ring):
                            pe.wait_ge(sem(n + "exp"), u - len(ring) + 1)
                        scores(u, bank[ring[u % len(ring)]]).then_inc(sem(n + "sc"), 1)
                    v = u - 2
                    if 0 <= v < U:
                        pe.wait_ge(sem(n + "norm"), v + 1)
                        if v >= 2:
                            pe.wait_ge(sem(n + "pT" + "ad"[v % 2]), v // 2)
                        for kc in range(1 + v % 2 if causal_keys else 2):
                            for j in range(2):
                                o = (2 * kc + j) * P
                                last = pe.transpose(bank[2 + v % 2][:, o:o + P],
                                                    probs[:, v % 4, j, kc * P:(kc + 1) * P], ident[:, :])
                        last.then_inc(sem(n + "tr"), 1)
                    if u >= 5 and u % 2 == 1 and (u - 5) // 2 < U // 2:
                        g = (u - 5) // 2
                        pe.wait_ge(sem(n + "pTa"), g + 1)
                        pe.wait_ge(sem(n + "pTd"), g + 1)
                        if g >= 2:
                            pe.wait_ge(sem(n + "oT"), g - 1)
                        apply(g, bank[(4, 6)[g % 2]]).then_inc(sem(n + "av"), 1)

            loaded(pe, "xT", "wq", "wk_raw", "wk_swp", "wv")
            n = 0
            for w in (wq, wk_raw, wk_swp):
                for c in range(4):
                    for half in range(2):
                        if n >= 4:
                            pe.wait_ge(sem("qkv_out"), n - 3)
                        proj(bank[n % 4][:, :], w, c * P, half).then_inc(sem("qkv"), 1)
                        n += 1
            for i in range(NT):
                if i >= 2:
                    pe.wait_ge(sem("v_out"), i - 1)
                for c in range(DC):
                    last = mm(bank[4 + i % 2][:, 0:D], xT[:, c, i * P:(i + 1) * P], wv[:, c, :],
                              start=(c == 0), stop=(c == DC - 1))
                last.then_inc(sem("v"), 1)

            pe.wait_ge(sem("kT"), 8)
            pe.wait_ge(sem("qkv_out"), 24)
            pe.wait_ge(sem("v_out"), NT)
            pe.wait_ge(sem("const_b"), 2)
            loaded(pe, "ident")

            def scores0(u, o):
                b, p, qt = u // 16, u // 2 % 8, u % 2
                o3 = o[:, :].rearrange("p (j k) -> p j k", j=2)
                for j in range(2):
                    r, c = PAD * (p % 4), 2 * (p // 4) + j
                    mm(o3[:, j, 0:(qt + 1) * P], qT[r:r + PAD, c, b * S + qt * P:b * S + (qt + 1) * P],
                       kT[r:r + PAD, c, b * S:b * S + (qt + 1) * P],
                       start=(j == 0), stop=False, skip_group_check=True)
                return mm(o3[:, :, qt * P:(qt + 1) * P], ident_b[:, :], bc(causal_b[:, :], 2),
                          start=False, stop=True, skip_group_check=True)

            def apply0(g, o):
                b, p = g // 8, g % 8
                r = PAD * (p % 4)
                for j in range(2):
                    h = 4 * (2 * (p // 4) + j) + p % 4
                    for kc in range(2):
                        last = mm(o[r:r + PAD, j * S + kc * P:(j + 1) * S], v_pad[:, 2 * b + kc, PAD * h:PAD * h + PAD],
                                  probsT[:, g % 2, kc, j, kc * P:S], start=(kc == 0), stop=(kc == 1),
                                  skip_group_check=True)
                return last

            attention("a0_", scores0, apply0, True, (0, 1, 5))
            pe.wait_ge(sem("a0_oT"), B * NPAIR)
            loaded(pe, "wo_pad")

            def out0(i, o):
                for c in range(4):
                    last = mm(o, oT[:, c, i * P:(i + 1) * P], wo_pad[:, c, :], start=(c == 0), stop=(c == 3))
                return last

            final(0, range(NT), out0)

            loaded(pe, "w_uqT", "w_ukT", "w_uvT", "w_o")
            for p in range(NPAIR):
                for j in range(2):
                    h = 2 * p + j
                    at = (p % 4) * P + (1 - j) * KVC
                    last = mm(bank[4 + p // 4][0:QC, at:at + KVC], w_uqT[:, h, :], w_ukT[:, h, :],
                              start=True, stop=True)
            last.then_inc(sem("fold_qk"), 1)
            for p in range(NPAIR):
                for j in range(2):
                    h = 2 * p + j
                    last = mm(bank[p // 2][KVC * j:KVC * j + KVC, (p % 2) * D:(p % 2 + 1) * D],
                              w_uvT[:, h, :], w_o[:, h, :], start=True, stop=True)
            last.then_inc(sem("fold_vo"), 1)
            pe.wait_ge(sem("fold_out"), 6)
            ln_transposes(0)

            loaded(pe, "ctxT")
            for k in range(16):
                half, e, fc = k // 8, k // 2 % 4, k % 2
                pe.wait_ge(sem("ln0_xT"), 2 * (half + 1))
                if k >= 4:
                    pe.wait_ge(sem("r_mul"), k - 3)
                proj(bank[k % 4][:, :], ctxT[:, e], fc * P, half).then_inc(sem("r_up"), 1)

            def out1(i, o):
                pe.wait_ge(sem("r_hid"), 8 * (i // 4 + 1))
                for k in range(8):
                    last = mm(o, hid0[:, k, i * P:(i + 1) * P], ctxT[:, k // 2, k % 2, :],
                              start=(k == 0), stop=(k == 7))
                return last

            final(1, range(NT), out1)
            ln_transposes(1)

            loaded(pe, "w1", "w2s", "vT", "uw", "rows")
            for k in range(4):
                c, half = k % 2, k // 2
                pe.wait_ge(sem("ln1_xT"), 2 * (half + 1))
                proj(bank[k][:, :], w1, c * P, half).then_inc(sem("f_h"), 1)
            pe.wait_ge(sem("f_hT"), 4)
            for i in range(NT):
                o = bank[4][:, 8 * i:8 * i + 8]
                for c in range(DC):
                    mm(o, h1T[:, c, i * P:(i + 1) * P], w2s[:, c, :], start=(c == 0), stop=False)
                last = mm(o, rows[0:1, 264:264 + P], rows[0:1, 0:8], start=False, stop=True)
            last.then_inc(sem("f_lg"), 1)
            for k in range(8):
                c, half = k % 4, k // 4
                if k >= 4:
                    pe.wait_ge(sem("f_vx"), k - 3)
                proj(bank[k % 4][:, :], vT, c * P, half).then_inc(sem("f_v"), 1)
                if k < 2:
                    continue
                for kk in ((0, 1, 2) if k == 2 else (k,)):
                    pe.wait_ge(sem("f_alpha"), 1)
                    if kk >= 2:
                        pe.wait_ge(sem("f_bc_s"), kk - 1)
                    c2, half2 = kk % 4, kk // 4
                    for i in range(4):
                        for j in range(2):
                            at = 8 * (4 * half2 + i) + 2 * c2 + j
                            last = mm(bank[6 + kk % 2][64 * j:64 * j + 64, i * P:(i + 1) * P],
                                      small[:, 5, at:at + 1].broadcast_to([P, 64]), ident[:, :],
                                      start=True, stop=True, skip_group_check=True)
                    last.then_inc(sem("f_bc"), 1)

            def out2(i, o):
                pe.wait_ge(sem("f_vx"), 4 * (i // 4 + 1))
                pe.wait_ge(sem("f_bc_s"), 8)
                for c in range(4):
                    last = mm(o, vxa[:, c, i * P:(i + 1) * P], uw[:, c, :], start=(c == 0), stop=(c == 3))
                return last

            final(2, range(NT), out2)
            ln_transposes(2)

            loaded(pe, "pinT", "wBT", "CwP", "onesel", "e16", "poutT")
            for k in range(4):
                c, half = k % 2, k // 2
                pe.wait_ge(sem("ln2_xT"), 2 * (half + 1))
                proj(bank[k][:, :], pinT, c * P, half).then_inc(sem("s_xp"), 1)
            pe.wait_ge(sem("s_xpT"), 4)
            for i in range(NT):
                for c in range(DC):
                    last = mm(bank[4][:, ST * i:ST * i + ST], xpT[:, c, i * P:(i + 1) * P], wBT[:, c, :],
                              start=(c == 0), stop=(c == DC - 1))
            last.then_inc(sem("s_pre"), 1)

            def pieces_transposed(n):
                pe.wait_ge(sem(n + "pieces"), 1)
                for i in range(NT):
                    last = pe.transpose(bank[i // 4][0:48, (i % 4) * P:(i % 4 + 1) * P],
                                        pieces[:, i, :], ident[:, :])
                last.then_inc(sem(n + "piecesT"), 1)
                pe.wait_ge(sem(n + "piecesB"), 2)

            pieces_transposed("s_")

            def step_sizes(q):
                for s in range(4 * q, 4 * q + 4):
                    for half in range(2):
                        r = 2 * s + half
                        if r >= 4:
                            pe.wait_ge(sem("s_bc_s"), r - 3)
                        mm(bank[r % 4][:, :], e16[:, s:s + 1].broadcast_to([48, P]),
                           piecesT[:, half * HALF:(half + 1) * HALF], start=True, stop=True
                           ).then_inc(sem("s_bc"), 1)

            def state_sums(g):
                pe.wait_ge(sem("s_scan"), g + 1)
                for half in range(2):
                    for j in range(4):
                        last = mm(bank[6 + half][32 * j:32 * j + 32, :], onesel[:, g // 2, :],
                                  hs[:, g % 2, j, half * HALF:(half + 1) * HALF],
                                  start=(g == 0), stop=(g == 7), skip_group_check=True)
                last.then_inc(sem("s_z"), 1)

            step_sizes(0)
            for q in range(1, 4):
                step_sizes(q)
                state_sums(2 * q - 2)
                state_sums(2 * q - 1)
            state_sums(6)
            state_sums(7)
            pe.wait_ge(sem("s_zT"), 2)
            for k in range(4):
                c, half = k % 2, k // 2
                mm(bank[k][:, :], CwP[:, c, :], zT[:, half * HALF:(half + 1) * HALF],
                   start=True, stop=True).then_inc(sem("s_y"), 1)

            def out3(i, o):
                pe.wait_ge(sem("s_yT"), 2 * (i // 4 + 1))
                for c in range(DC):
                    mm(o, xpT[:, c, i * P:(i + 1) * P], poutT[:, c, :], start=(c == 0), stop=False)
                return mm(o, rows[0:1, 264:264 + P], rows[0:1, 8:264], start=False, stop=True)

            final(3, range(NT), out3)

            loaded(pe, "w_kvc", "w_kr", "w_dq")
            for half in range(2):
                for c in range(DC):
                    last = mm(bank[half][:, :], w_kvc[:, c, :],
                              ctxT[:, 2 * half:2 * half + 2, c, :], start=(c == 0), stop=(c == DC - 1))
                last.then_inc(sem("k_lat"), 1)
            for i in range(NT):
                for c in range(DC):
                    last = mm(bank[2][:, KVC * i:KVC * i + KVC],
                              ctxT[:, i // 2, c, (i % 2) * P:(i % 2 + 1) * P], w_kvc[:, c, 0:KVC],
                              start=(c == 0), stop=(c == DC - 1))
            last.then_inc(sem("k_tok"), 1)
            for half in range(2):
                pe.wait_ge(sem("k_latT"), 2 * (half + 1))
                for r in range(2):
                    mm(bank[(3, 4)[r]][:, :] if half == 0 else bank[(0, 1)[r]][:, :], w_kr[:, r, :],
                       keys_b[0:KVC, half * HALF:(half + 1) * HALF], start=True, stop=True
                       ).then_inc(sem("k_rope"), 1)
                if half == 0:
                    pe.wait_ge(sem("k_latT"), 4)
            pe.wait_ge(sem("k_mul"), 4)
            ln_transposes(3)
            for half in range(2):
                pe.wait_ge(sem("ln3_xT"), 2 * (half + 1))
                for c in range(DC):
                    last = mm(bank[half][0:QC, :], w_dq[:, c, :], xT[:, c, half * HALF:(half + 1) * HALF],
                              start=(c == 0), stop=(c == DC - 1))
                last.then_inc(sem("qc"), 1)
            loaded(pe, "wqr_raw", "wqr_swp")
            pe.wait_ge(sem("qcT"), 2)
            pe.wait_ge(sem("k_add"), 4)
            pe.wait_ge(sem("k_tokT"), 1)
            pe.wait_ge(sem("mask"), NT)

            def queries(b):
                rhs = qcT[:, b * S:(b + 1) * S]
                for p in range(NPAIR):
                    n = b * NPAIR + p
                    if n >= 1:
                        pe.wait_ge(sem("q_mul"), n)
                        pe.wait_ge(sem("q_lat"), n)
                    mm(bank[7][:, 0:S], wqr_raw[:, p, :], rhs, start=True, stop=True)
                    mm(bank[7][:, S:2 * S], wqr_swp[:, p, :], rhs, start=True, stop=True).then_inc(sem("q_rope"), 1)
                    mm(bank[LATQ][:, 0:S], qk_fold[:, p, :], rhs,
                       start=True, stop=True).then_inc(sem("q_l"), 1)
                pe.wait_ge(sem("q_add"), NPAIR * (b + 1))
                pe.wait_ge(sem("q_lat"), NPAIR * (b + 1))

            def scores4(u, o):
                b, p, qt = u // 16, u // 2 % 8, u % 2
                if u % 16 == 0:
                    queries(b)
                o3 = o[:, :].rearrange("p (j k) -> p j k", j=2)
                for j in range(2):
                    mm(o3[:, j, :], qm[:, NH * (b % 2) + 2 * p + j, qt * P:(qt + 1) * P],
                       (keys_a, keys_b)[j][:, b * S:(b + 1) * S], start=(j == 0), stop=False,
                       skip_group_check=True)
                return mm(o3, ident_b[:, :], bc(mask_m[:, 2 * b + qt, :], 2), start=False, stop=True,
                          skip_group_check=True)

            def apply4(g, o):
                b = g // 8
                for kc in range(2):
                    for j in range(2):
                        last = mm(o[KVC * j:KVC * j + KVC, 0:S], kv_tok[:, 2 * b + kc, :],
                                  probsT[:, g % 2, kc, j, :], start=(kc == 0), stop=(kc == 1),
                                  skip_group_check=True)
                return last

            attention("a4_", scores4, apply4, False, (0, 1))
            pe.wait_ge(sem("a4_oT"), B * NPAIR)

            def out4(i, o):
                for p in range(NPAIR):
                    last = mm(o, om[:, p, i * P:(i + 1) * P], vo_fold[:, p, :], start=(p == 0),
                              stop=(p == NPAIR - 1))
                return last

            final(4, range(NT), out4)
            ln_transposes(4)

            loaded(pe, "wgateT", "gateT", "upT", "sel_e", "downT")
            pe.wait_ge(sem("ln4_xT"), 4)
            for i in range(NT):
                for c in range(DC):
                    last = mm(bank[0][:, NE * i:NE * i + NE], xT[:, c, i * P:(i + 1) * P], wgateT[:, c, :],
                              start=(c == 0), stop=(c == DC - 1))
            last.then_inc(sem("m_lg"), 1)
            pe.wait_ge(sem("m_pieces"), 1)
            for i in range(NT):
                last = pe.transpose(bank[2 + i // 4][0:48, (i % 4) * P:(i % 4 + 1) * P],
                                    pieces[:, i, :], ident[:, :])
            last.then_inc(sem("m_piecesT"), 1)
            pe.wait_ge(sem("m_piecesB"), 2)
            K = 2 * FCH
            for k in range(K + 2):
                if k < K:
                    half, c = k // FCH, k % FCH
                    if k >= 2:
                        pe.wait_ge(sem("m_hid"), k - 1)
                    proj(bank[k % 2][:, :], gateT, c * P, half).then_inc(sem("m_g"), 1)
                    proj(bank[2 + k % 2][:, :], upT, c * P, half)
                    mm(bank[4 + k % 2][:, :], sel_e[:, c * P:(c + 1) * P],
                       piecesT[:, half * HALF:(half + 1) * HALF], start=True, stop=True).then_inc(sem("m_u"), 1)
                if k >= 2:
                    kk = k - 2
                    half, c = kk // FCH, kk % FCH
                    pe.wait_ge(sem("m_hid"), kk + 1)
                    if kk == FCH:
                        pe.wait_ge(sem("ln5_r"), 4)
                    for i in range(4):
                        last = mm(bank[6 + i // 2][:, (i % 2) * D:(i % 2 + 1) * D],
                                  hid1[:, kk % 4, i * P:(i + 1) * P], downT[:, c, :],
                                  start=(c == 0 and i % 2 == 0), stop=(c == FCH - 1), skip_group_check=True)
                        if c == FCH - 1:
                            last.then_inc(sem("fin5"), 1)
                    if c < FCH - 1:
                        last.then_inc(sem("m_down"), 1)

        @block.vector
        def _(dve):
            tt, ts, stt, cp = dve.tensor_tensor, dve.tensor_scalar, dve.scalar_tensor_tensor, dve.tensor_copy
            chain = [0]

            def link(ins):
                chain[0] += 1
                ins.then_inc(sem("dve_chain"), 1)
                dve.wait_ge(sem("dve_chain"), chain[0])

            def norm(k, scale, place):
                for i in range(NT):
                    dve.wait_ge(sem(f"fin{k}"), i + 1)
                    if k == 0 and i == 0:
                        loaded(dve, "x_tok")
                    if k and i == 0:
                        dve.wait_ge(sem(f"ln{k-1}_t"), 4)
                    stt(x_tok[:, i, :], x_tok[:, i, :], scale, place(i), ALU.mult, ALU.add
                        ).then_inc(sem(f"ln{k}_r"), 1)
                    dve.wait_ge(sem(f"ln{k}_r"), i + 1)
                    link(dve.bn_stats(stats[:, i, :], x_tok[:, i, :]))
                    dve.bn_aggr(meanvar[:, i, :], stats[:, i, :]).then_inc(sem(f"ln{k}_v"), 1)
                for i in range(NT):
                    dve.wait_ge(sem(f"ln{k}_v"), i + 1)
                    dve.wait_ge(sem(f"ln{k}_rstd"), i // 4 + 1)
                    ts(x_tok[:, i, :], x_tok[:, i, :], meanvar[:, i, 0:1], rstd[:, i:i + 1],
                       ALU.subtract, ALU.mult).then_inc(sem(f"ln{k}_x"), 1)

            fin_bank = lambda i: bank[6 + i % 2][:, 0:D]

            def softmax_small(n, lg, w, e_row):
                sh = lambda r: small[:, r, 0:NT * w].rearrange("p (i w) -> p i w", w=w)
                col = small[:, 11, 0:NT]
                link(dve.tensor_reduce(col, lg, axis=AX, op=ALU.max, negate=True))
                tt(sh(0), lg, bc(col, w, 2), ALU.add).then_inc(sem(n + "sub"), 1)
                dve.wait_ge(sem(n + "e"), 1)
                link(dve.tensor_reduce(small[:, 11, 8:16], sh(1), axis=AX, op=ALU.add))
                link(dve.reciprocal(small[:, 11, 16:24], small[:, 11, 8:16]))
                return tt(sh(e_row), sh(1), bc(small[:, 11, 16:24], w, 2), ALU.mult)

            def split(n, row):
                src = small[:, row, :].rearrange("p (i w) -> p i w", w=16)
                cur = src
                b3 = small_b[:, :].rearrange("p (i w) -> p i w", w=16)
                rest = small[:, 10, :].rearrange("p (i w) -> p i w", w=16)
                for j in range(2):
                    link(cp(b3, cur))
                    link(cp(pieces[:, :, 16 * j:16 * j + 16], b3))
                    link(tt(rest, cur, pieces[:, :, 16 * j:16 * j + 16], ALU.subtract))
                    cur = rest
                cp(pieces[:, :, 32:48], rest).then_inc(sem(n + "pieces"), 1)

            def attention(n, causal_keys, ring, extra=None):
                U = 2 * B * NPAIR
                for u in range(U + 4):
                    if extra:
                        extra(u)
                    if u < U:
                        keys = (u % 2 + 1) * P if causal_keys else 256
                        s3 = bank[ring[u % len(ring)]][:, :].rearrange("p (j k) -> p j k", j=2)
                        dve.wait_ge(sem(n + "sc"), u + 1)
                        dve.tensor_reduce(neg_max[:, u % 4, :], s3[:, :, 0:keys], axis=AX, op=ALU.max,
                                          negate=True).then_inc(sem(n + "max"), 1)
                    v = u - 1
                    if 0 <= v < U:
                        dve.wait_ge(sem(n + "exp"), v + 1)
                        if v >= 4:
                            dve.wait_ge(sem(n + "norm"), v - 3)
                        dve.reciprocal(row_rec[:, v % 4, :], row_sum[:, v % 4, :]).then_inc(sem(n + "rec"), 1)
                    v = u - 3
                    if 0 <= v < U and v % 2 == 1:
                        copy_probs(dve, n, v, causal_keys, lambda o, i: cp(o, i), "d")

            loaded(dve, "ident", "causal")
            cp(ident_b[:, :], ident[:, :]).then_inc(sem("const_b"), 1)
            cp(causal_b[:, :], causal[:, :]).then_inc(sem("const_b"), 1)

            loaded(dve, "tab_q", "tab_c", "tab_s")
            n = 0
            for w in range(3):
                for c in range(4):
                    for half in range(2):
                        src = bank[n % 4][:, :].rearrange("p (b s) -> p b s", b=2)
                        hh = slice(half * HALF, (half + 1) * HALF)
                        dve.wait_ge(sem("qkv"), n + 1)
                        if w == 0:
                            dst, tab = qT[:, c, hh], tab_q
                        elif w == 1:
                            dst, tab = kT[:, c, hh], tab_c
                        else:
                            r = (c * 2 + half) % 2
                            if c * 2 + half >= 2:
                                dve.wait_ge(sem("kT"), c * 2 + half - 1)
                            dst, tab = probs[:, r].rearrange("p a b -> p (a b)"), tab_s
                        tt(dst.rearrange("p (b s) -> p b s", b=2), src, bc(tab, 2), ALU.mult
                           ).then_inc(sem("qkv_out"), 1)
                        n += 1
            loaded(dve, "tid")
            link(cp(tid_f, tid_i))
            ts(emask[0], tid_f, float(PER_EXPERT), None, ALU.is_lt).then_inc(sem("emask"), 1)
            for e in (1, 2):
                link(ts(lt_tmp, tid_f, float(PER_EXPERT * (e + 1)), None, ALU.is_lt))
                stt(emask[e], tid_f, float(PER_EXPERT * e), lt_tmp, ALU.is_ge, ALU.mult).then_inc(sem("emask"), 1)
                dve.wait_ge(sem("emask"), e + 1)
            ts(emask[3], tid_f, float(PER_EXPERT * 3), None, ALU.is_ge).then_inc(sem("emask"), 1)

            attention("a0_", True, (0, 1, 5))
            norm(0, 1.0, fin_bank)

            for k in range(16):
                half = k // 8
                dve.wait_ge(sem("r_silu"), k + 1)
                tt(hid0[:, k % 8, half * HALF:(half + 1) * HALF], silu0[:, k % 4, :], bank[k % 4][:, :],
                   ALU.mult).then_inc(sem("r_mul"), 1)
            norm(1, 1.0, fin_bank)

            dve.wait_ge(sem("f_lg"), 1)
            softmax_small("f_", bank[4][:, 0:64].rearrange("p (i w) -> p i w", w=8), 8, 5
                          ).then_inc(sem("f_alpha"), 1)
            for k in range(8):
                c, half = k % 4, k // 4
                dve.wait_ge(sem("f_v"), k + 1)
                dve.wait_ge(sem("f_bc_s"), k + 1)
                tt(vxa[:, c, half * HALF:(half + 1) * HALF], bc_s[:, k % 2, :], bank[k % 4][:, :],
                   ALU.mult).then_inc(sem("f_vx"), 1)
            norm(2, 1.0, fin_bank)

            dve.wait_ge(sem("decayed"), 1)
            dve.wait_ge(sem("s_soft"), 1)
            link(tt(small[:, 3, :], small[:, 2, :], small[:, 1, :], ALU.add))
            split("s_", 3)
            for g in range(8):
                c = g % 2
                for j in range(4):
                    s = 4 * (g // 2) + j
                    u_s = hs[:, g % 2, j, :]
                    if c == 0:
                        dve.wait_ge(sem("s_bc_s"), 2 * s + 2)
                        if g >= 2:
                            dve.wait_ge(sem("s_z"), g - 1)
                        link(tt(u_s, dl[:, j, :], xpT[:, 0, :], ALU.mult))
                    else:
                        dve.wait_ge(sem("s_u1"), s + 1)
                    for b in range(B):
                        col = hs[:, g % 2, j, b * S:(b + 1) * S]
                        last = dve.tensor_tensor_scan(col, decay[:, c, s:s + 1].broadcast_to([P, S]), col,
                                                      0.0, ALU.mult, ALU.add)
                last.then_inc(sem("s_scan"), 1)
            for k in range(4):
                c, half = k % 2, k // 2
                hh = slice(half * HALF, (half + 1) * HALF)
                dve.wait_ge(sem("s_y"), k + 1)
                stt(xpT[:, c, hh], xpT[:, c, hh], vecs[:, 2, c:c + 1], bank[k][:, :], ALU.mult, ALU.add
                    ).then_inc(sem("s_yT"), 1)
            norm(3, 2.0, fin_bank)

            loaded(dve, "tab_kc", "tab_ks", "iota4", "seg")
            for half in range(2):
                for r in range(2):
                    n = 2 * half + r
                    dve.wait_ge(sem("k_rope"), n + 1)
                    if half == 1 and r == 0:
                        dve.wait_ge(sem("k_add"), 2)
                    src = (bank[(3, 4)[r]] if half == 0 else bank[r])[:, :].rearrange("p (b s) -> p b s", b=2)
                    tt(ropes[:, r, :].rearrange("p (b s) -> p b s", b=2), src, bc((tab_kc, tab_ks)[r], 2),
                       ALU.mult).then_inc(sem("k_mul"), 1)
                dve.wait_ge(sem("k_mul"), 2 * half + 2)
                hh = slice(half * HALF, (half + 1) * HALF)
                tt(keys_a[0:64, hh], ropes[0:64, 0, :], ropes[0:64, 1, :], ALU.add).then_inc(sem("k_add"), 1)
                tt(keys_b[64:128, hh], ropes[64:128, 0, :], ropes[64:128, 1, :], ALU.add).then_inc(sem("k_add"), 1)
            link(cp(seg_f[:, :], seg_i[:, :]))
            dve.wait_ge(sem("k_tok"), 1)
            for i in range(NT):
                link(ts(distance, iota4, seg_f[:, i:i + 1], None, ALU.subtract))
                link(tt(distance, distance, distance, ALU.mult))
                ts(mask_m[:, i, :], distance, 16.0, NEG, ALU.is_gt, ALU.mult).then_inc(sem("mask"), 1)
                dve.wait_ge(sem("mask"), i + 1)

            def rotate_queries(u):
                if u % 16 or u >= 64:
                    return
                b = u // 16
                for p in range(NPAIR):
                    n = b * NPAIR + p
                    dve.wait_ge(sem("q_rope"), n + 1)
                    if n >= 2:
                        dve.wait_ge(sem("q_add"), n - 1)
                    tt(ropes[:, n % 2, 0:S], bank[7][:, 0:S], tab_qc, ALU.mult)
                    tt(ropes[:, n % 2, S:2 * S], bank[7][:, S:2 * S], tab_qs, ALU.mult).then_inc(sem("q_mul"), 1)

            loaded(dve, "tab_qc", "tab_qs")
            attention("a4_", False, (0, 1), rotate_queries)
            norm(4, 1.0, fin_bank)

            dve.wait_ge(sem("m_lg"), 1)
            link(softmax_small("m_", bank[0][:, 0:128].rearrange("p (i w) -> p i w", w=16), 16, 3))
            sc3 = small[:, 3, :].rearrange("p (i w) -> p i w", w=16)
            r3 = lambda r: small[:, r, :].rearrange("p (i w) -> p i w", w=16)
            for i in range(NT):
                last = dve.max(top8[:, i, :], sc3[:, i, :])
            link(last)
            thr = top8[:, :, TOPK - 1].unsqueeze(2).broadcast_to([P, NT, NE])
            link(tt(r3(4), sc3, thr, ALU.is_gt))
            link(tt(r3(5), sc3, thr, ALU.is_equal))
            link(dve.tensor_reduce(small[:, 11, 24:32], r3(4), axis=AX, op=ALU.add))
            loaded(dve, "reset")
            link(dve.tensor_tensor_scan(small[:, 6, :], reset[:, :], small[:, 5, :], 0.0, ALU.mult, ALU.add))
            link(tt(r3(7), r3(6), bc(small[:, 11, 24:32], NE, 2), ALU.add))
            link(stt(small[:, 8, :], small[:, 7, :], float(TOPK), small[:, 5, :], ALU.is_le, ALU.mult))
            link(tt(small[:, 9, :], small[:, 8, :], small[:, 4, :], ALU.add))
            link(tt(small[:, 9, :], small[:, 9, :], small[:, 3, :], ALU.mult))
            split("m_", 9)
            K = 2 * FCH

            def residual5(half):
                for i in range(4 * half, 4 * half + 4):
                    dve.wait_ge(sem("fin5"), i // 2 * 2 + 2)
                    stt(x_tok[:, i, :], x_tok[:, i, :], 1.0,
                        bank[6 + i % 4 // 2][:, (i % 2) * D:(i % 2 + 1) * D], ALU.mult, ALU.add
                        ).then_inc(sem("ln5_r"), 1)

            dve.wait_ge(sem("ln4_t"), 4)
            for k in range(K):
                dve.wait_ge(sem("m_silu"), k + 1)
                dve.wait_ge(sem("m_u"), k + 1)
                if k >= 4:
                    kk = k - 4
                    dve.wait_ge(sem("m_down"), kk + 1 - (kk + 1) // FCH)
                    if kk >= FCH - 1:
                        dve.wait_ge(sem("fin5"), 4)
                link(tt(hid1[:, k % 4, :], silu1[:, k % 2, :], bank[2 + k % 2][:, :], ALU.mult))
                tt(hid1[:, k % 4, :], hid1[:, k % 4, :], bank[4 + k % 2][:, :], ALU.mult).then_inc(sem("m_hid"), 1)
                if k == FCH + 1:
                    residual5(0)
            residual5(1)
            for i in range(NT):
                dve.wait_ge(sem("ln5_r"), i + 1)
                link(dve.bn_stats(stats[:, i, :], x_tok[:, i, :]))
                dve.bn_aggr(meanvar[:, i, :], stats[:, i, :]).then_inc(sem("ln5_v"), 1)
            for i in range(NT):
                dve.wait_ge(sem("ln5_v"), i + 1)
                dve.wait_ge(sem("ln5_rstd"), i // 4 + 1)
                ts(x_tok[:, i, :], x_tok[:, i, :], meanvar[:, i, 0:1], rstd[:, i:i + 1],
                   ALU.subtract, ALU.mult).then_inc(sem("ln5_x"), 1)

        @block.scalar
        def _(act):
            af = act.activation

            def ln_out(k):
                for q in range(NT // 2):
                    act.wait_ge(sem(f"ln{k}_t"), q + 1)
                    src = bank[4 + q % 2][:, :].rearrange("p (i c t) -> p i c t", i=2, c=2)
                    dst = xT[:, :, q * 2 * P:(q + 1) * 2 * P].rearrange("p c (i t) -> p i c t", i=2)
                    af(dst, src, ACT.Copy).then_inc(sem(f"ln{k}_xT"), 1)

            def attention(n, causal_keys, ring, out_of, extra=None):
                U = 2 * B * NPAIR
                for u in range(U + 6):
                    if extra:
                        extra(u)
                    if u < U:
                        keys = (u % 2 + 1) * P if causal_keys else 256
                        act.wait_ge(sem(n + "max"), u + 1)
                        if u >= 4:
                            act.wait_ge(sem(n + "tr"), u - 3)
                            act.wait_ge(sem(n + "rec"), u - 3)
                        for j in range(2):
                            last = af(probs[:, u % 4, j, 0:keys],
                                      bank[ring[u % len(ring)]][:, j * 256:j * 256 + keys], ACT.Exp,
                                      bias=neg_max[:, u % 4, j:j + 1], accum_out=row_sum[:, u % 4, j:j + 1])
                        last.then_inc(sem(n + "exp"), 1)
                    v = u - 3
                    if 0 <= v < U and v % 2 == 0:
                        copy_probs(act, n, v, causal_keys, lambda o, i: af(o, i, ACT.Copy), "a")
                    if u >= 6 and u % 2 == 0 and (u - 6) // 2 < U // 2:
                        g = (u - 6) // 2
                        act.wait_ge(sem(n + "av"), g + 1)
                        dst, src = out_of(g)
                        af(dst, src, ACT.Copy).then_inc(sem(n + "oT"), 1)

            loaded(act, "decay")
            af(decay[:, :, :], decay[:, :, :], ACT.Sigmoid).then_inc(sem("decayed"), 1)
            act.wait_ge(sem("zeroed"), 1)
            for i in range(NT):
                act.wait_ge(sem("v"), i + 1)
                af(v_pad[:, i, :].rearrange("p (h w) -> p h w", w=PAD)[:, :, 0:HD0],
                   bank[4 + i % 2][:, 0:D].rearrange("p (h w) -> p h w", w=HD0), ACT.Copy
                   ).then_inc(sem("v_out"), 1)

            def out_of0(g):
                b, p = g // 8, g % 8
                r, c = PAD * (p % 4), 2 * (p // 4)
                return (oT[r:r + PAD, c:c + 2, b * S:(b + 1) * S],
                        bank[(4, 6)[g % 2]][r:r + PAD, :].rearrange("p (j q) -> p j q", j=2))

            attention("a0_", True, (0, 1, 5), out_of0)
            act.wait_ge(sem("fold_qk"), 1)
            for k in range(2):
                af(qk_fold[:, 4 * k:4 * k + 4, :],
                   bank[4 + k][0:QC, :].rearrange("p (a b) -> p a b", a=4), ACT.Copy, scale=MLA_SCALE
                   ).then_inc(sem("fold_out"), 1)
            act.wait_ge(sem("fold_vo"), 1)
            for k in range(4):
                af(vo_fold[:, 2 * k:2 * k + 2, :], bank[k][:, :].rearrange("p (a b) -> p a b", a=2), ACT.Copy
                   ).then_inc(sem("fold_out"), 1)
            ln_out(0)

            for k in range(16):
                act.wait_ge(sem("r_up"), k + 1)
                if k >= 4:
                    act.wait_ge(sem("r_mul"), k - 3)
                af(silu0[:, k % 4, :], bank[k % 4][:, :], ACT.Silu).then_inc(sem("r_silu"), 1)
            ln_out(1)

            loaded(act, "vecs")
            for k in range(4):
                c, half = k % 2, k // 2
                act.wait_ge(sem("f_h"), k + 1)
                af(h1T[:, c, half * HALF:(half + 1) * HALF], bank[k][:, :], ACT.Relu,
                   bias=vecs[:, 0, c:c + 1]).then_inc(sem("f_hT"), 1)
            act.wait_ge(sem("f_sub"), 1)
            af(small[:, 1, 0:64], small[:, 0, 0:64], ACT.Exp).then_inc(sem("f_e"), 1)
            for k in range(8):
                act.wait_ge(sem("f_bc"), k + 1)
                if k >= 2:
                    act.wait_ge(sem("f_vx"), k - 1)
                af(bc_s[:, k % 2, :], bank[6 + k % 2][:, :], ACT.Copy).then_inc(sem("f_bc_s"), 1)
            ln_out(2)

            for k in range(4):
                c, half = k % 2, k // 2
                act.wait_ge(sem("s_xp"), k + 1)
                af(xpT[:, c, half * HALF:(half + 1) * HALF], bank[k][:, :], ACT.Identity,
                   bias=vecs[:, 1, c:c + 1]).then_inc(sem("s_xpT"), 1)
            act.wait_ge(sem("s_pre"), 1)
            pre = bank[4][:, 0:P]
            af(small[:, 0, :], pre, ACT.Abs).then_inc(sem("s_sp"), 1)
            af(small[:, 2, :], pre, ACT.Relu)
            act.wait_ge(sem("s_sp"), 1)
            af(small[:, 0, :], small[:, 0, :], ACT.Exp, scale=-1.0).then_inc(sem("s_sp"), 1)
            act.wait_ge(sem("s_sp"), 2)
            af(small[:, 1, :], small[:, 0, :], ACT.Ln, bias=1.0).then_inc(sem("s_soft"), 1)
            act.wait_ge(sem("s_piecesT"), 1)
            for k in range(2):
                af(piecesT[:, k * HALF:(k + 1) * HALF], bank[k][0:48, :], ACT.Copy
                   ).then_inc(sem("s_piecesB"), 1)
            for r in range(2 * ST):
                s, half = r // 2, r % 2
                act.wait_ge(sem("s_bc"), r + 1)
                if s >= 4 and half == 0:
                    act.wait_ge(sem("s_u1"), s - 3)
                    act.wait_ge(sem("s_scan"), 2 * (s // 4) - 1)
                af(dl[:, s % 4, half * HALF:(half + 1) * HALF], bank[r % 4][:, :], ACT.Copy
                   ).then_inc(sem("s_bc_s"), 1)
            act.wait_ge(sem("s_z"), 8)
            for half in range(2):
                af(zT[:, half * HALF:(half + 1) * HALF], bank[6 + half][:, :], ACT.Copy
                   ).then_inc(sem("s_zT"), 1)

            for half in range(2):
                hh = slice(half * HALF, (half + 1) * HALF)
                act.wait_ge(sem("k_lat"), half + 1)
                af(keys_b[0:64, hh], bank[half][0:64, :], ACT.Copy).then_inc(sem("k_latT"), 1)
                af(keys_a[64:128, hh], bank[half][64:128, :], ACT.Copy).then_inc(sem("k_latT"), 1)
            act.wait_ge(sem("k_tok"), 1)
            af(kv_tok, bank[2][:, :].rearrange("p (i c) -> p i c", i=NT), ACT.Copy).then_inc(sem("k_tokT"), 1)
            ln_out(3)
            for half in range(2):
                act.wait_ge(sem("qc"), half + 1)
                af(qcT[:, half * HALF:(half + 1) * HALF], bank[half][0:QC, :], ACT.Copy).then_inc(sem("qcT"), 1)

            def latent_queries(u):
                if u % 16 or u >= 64:
                    return
                b = u // 16
                for p in range(NPAIR):
                    n = b * NPAIR + p
                    act.wait_ge(sem("q_l"), n + 1)
                    at = NH * (b % 2) + 2 * p
                    af(qm[0:64, at + 1, :], bank[LATQ][0:64, 0:S], ACT.Copy)
                    af(qm[64:128, at, :], bank[LATQ][64:128, 0:S], ACT.Copy).then_inc(sem("q_lat"), 1)

            def out_of4(g):
                b, p = g // 8, g % 8
                return om[:, p, b * S:(b + 1) * S], bank[(4, 6)[g % 2]][:, 0:S]

            attention("a4_", False, (0, 1), out_of4, latent_queries)
            ln_out(4)

            act.wait_ge(sem("m_sub"), 1)
            af(small[:, 1, :], small[:, 0, :], ACT.Exp).then_inc(sem("m_e"), 1)
            act.wait_ge(sem("m_piecesT"), 1)
            for k in range(2):
                af(piecesT[:, k * HALF:(k + 1) * HALF], bank[2 + k][0:48, :], ACT.Copy
                   ).then_inc(sem("m_piecesB"), 1)
            for k in range(2 * FCH):
                act.wait_ge(sem("m_g"), k + 1)
                if k >= 2:
                    act.wait_ge(sem("m_hid"), k - 1)
                af(silu1[:, k % 2, :], bank[k % 2][:, :], ACT.Silu).then_inc(sem("m_silu"), 1)

        @block.gpsimd
        def _(pool):
            step = [0]

            def link(ins):
                step[0] += 1
                ins.then_inc(sem("pool_chain"), 1)
                pool.wait_ge(sem("pool_chain"), step[0])

            def rstd_of(k):
                for half in range(2):
                    s = slice(4 * half, 4 * half + 4)
                    pool.wait_ge(sem(f"ln{k}_v"), 4 * half + 4)
                    link(pool.tensor_scalar(veps[:, s], meanvar[:, s, 1], EPS, 1.0, ALU.add, ALU.mult))
                    pool.tensor_tensor(rstd[:, s], veps[:, s], minus_half[:, s], ALU.pow
                                       ).then_inc(sem(f"ln{k}_rstd"), 1)

            def attention(n, causal_keys, extra=None):
                for u in range(2 * B * NPAIR):
                    if extra:
                        extra(u + 1)
                    keys = (u % 2 + 1) * P if causal_keys else 256
                    pool.wait_ge(sem(n + "rec"), u + 1)
                    for j in range(2):
                        pr = probs[:, u % 4, j, 0:keys]
                        last = pool.tensor_scalar(pr, pr, row_rec[:, u % 4, j:j + 1], 1.0, ALU.mult, ALU.mult)
                    last.then_inc(sem(n + "norm"), 1)

            pool.memset(v_pad, 0.0).then_inc(sem("zeroed"), 1)
            link(pool.memset(minus_half[:, :], -0.5))
            for k in range(8):
                c, half = k // 2, k % 2
                hh = slice(half * HALF, (half + 1) * HALF)
                pool.wait_ge(sem("qkv_out"), 17 + k)
                pool.tensor_tensor(kT[:, c, hh], kT[:, c, hh], probs[:, k % 2].rearrange("p a b -> p (a b)"),
                                   ALU.add).then_inc(sem("kT"), 1)
            attention("a0_", True)
            rstd_of(0)
            pool.wait_ge(sem("emask"), 4)
            for k in range(16):
                half, e = k // 8, k // 2 % 4
                hh = slice(half * HALF, (half + 1) * HALF)
                pool.wait_ge(sem("r_mul"), k + 1)
                pool.tensor_tensor(hid0[:, k % 8, hh], hid0[:, k % 8, hh], emask[e][:, hh], ALU.mult
                                   ).then_inc(sem("r_hid"), 1)
            rstd_of(1)
            rstd_of(2)
            for g in range(1, 8, 2):
                for j in range(4):
                    s = 4 * (g // 2) + j
                    pool.wait_ge(sem("s_bc_s"), 2 * s + 2)
                    if g >= 3 and j == 0:
                        pool.wait_ge(sem("s_z"), g - 1)
                    pool.tensor_tensor(hs[:, 1, j, :], dl[:, j, :], xpT[:, 1, :], ALU.mult
                                       ).then_inc(sem("s_u1"), 1)
            rstd_of(3)

            def add_queries(u):
                if u % 16 or u >= 64:
                    return
                b = u // 16
                for p in range(NPAIR):
                    n = b * NPAIR + p
                    at = NH * (b % 2) + 2 * p
                    pool.wait_ge(sem("q_mul"), n + 1)
                    if u and p == 0:
                        pool.wait_ge(sem("a4_norm"), u - 1)
                    link(pool.tensor_tensor(qm[0:64, at, :], ropes[0:64, n % 2, 0:S],
                                            ropes[0:64, n % 2, S:2 * S], ALU.add))
                    pool.tensor_tensor(qm[64:128, at + 1, :], ropes[64:128, n % 2, 0:S],
                                       ropes[64:128, n % 2, S:2 * S], ALU.add).then_inc(sem("q_add"), 1)
                    pool.wait_ge(sem("q_add"), n + 1)

            add_queries(0)
            attention("a4_", False, add_queries)
            rstd_of(4)
            rstd_of(5)


def laid_out(x):
    import numpy as np

    f = np.float32
    a = {k: np.asarray(v) for k, v in x.items()}
    o = {}

    def chunks(w):
        return w.reshape(-1, 128, w.shape[-1]).transpose(1, 0, 2)

    X = a["x"].reshape(1024, 256)
    o["x_tok"] = chunks(X)
    o["xT"] = chunks(X.T)
    head = np.arange(16)[:, None] * 16
    j = np.arange(16)[None, :]
    plain, swapped = head + j, head + (j + 8) % 16
    both = lambda l, r: np.concatenate([l, r], axis=1).ravel()
    o["wq"] = chunks(a["L0_attn_Wq"].T[:, both(plain, swapped)])
    o["wk_raw"] = chunks(a["L0_attn_Wk"].T[:, both(plain, plain)])
    o["wk_swp"] = chunks(a["L0_attn_Wk"].T[:, both(swapped, swapped)])
    o["wv"] = chunks(a["L0_attn_Wv"].T)
    wo = np.zeros((16, 32, 256), f)
    wo[:, :16] = a["L0_attn_Wo"].T.reshape(16, 16, 256)
    o["wo_pad"] = chunks(wo.reshape(512, 256))
    fr = np.arange(256, dtype=f)[:, None] * (1.0 / 10000.0 ** (np.arange(0, 16, 2, dtype=f) / 16)).astype(f)
    emb = np.concatenate([fr, fr], axis=-1)
    cos, sin = np.cos(emb).T.astype(f), np.sin(emb).T.astype(f)
    sgn = np.where(np.arange(16) < 8, -1, 1).astype(f)[:, None] * sin
    o["tab_q"] = np.tile(np.concatenate([cos, sgn]), (4, 1)) * f(0.25)
    o["tab_c"] = np.tile(cos, (8, 1))
    o["tab_s"] = np.tile(sgn, (8, 1))
    o["ident"] = np.eye(128, dtype=f)
    neg = -(np.array([1e30], f).view(np.uint32) & np.uint32(0xFFFF0000)).view(f)[0]
    k = np.arange(128)
    o["causal"] = np.where(k[None, :] > k[:, None], neg, 0).astype(f)
    o["tid"] = a["itok_BxS_13_99985"].reshape(1024).astype(np.int32)
    o["w_uqT"] = a["L1_xattn_W_uq"].reshape(96, 16, 128).transpose(2, 1, 0)
    o["w_ukT"] = a["L1_xattn_W_uk"].reshape(64, 16, 128).transpose(2, 1, 0)
    o["w_uvT"] = a["L1_xattn_W_uv"].reshape(64, 16, 128).transpose(2, 1, 0)
    o["w_o"] = a["L1_xattn_W_o"].reshape(16, 128, 256).transpose(1, 0, 2)
    o["ctxT"] = a["ctx_2048"].transpose(2, 0, 1).reshape(2, 128, 4, 256).transpose(1, 2, 0, 3)
    o["w1"] = chunks(a["L0_ffn_W1"])
    o["vT"] = chunks(a["L0_ffn_V"].reshape(512, 256).T)
    o["uw"] = chunks(a["L0_ffn_U"].transpose(0, 2, 1).reshape(512, 256))
    o["w2s"] = chunks(a["L0_ffn_W2"])
    vecs = np.zeros((128, 8, 2), f)
    vecs[:, 0] = a["L0_ffn_b1"].reshape(2, 128).T
    vecs[:, 1] = a["L1_attn_proj_in_b"].reshape(2, 128).T
    vecs[:, 2] = a["L1_attn_D_param"].reshape(2, 128).T
    o["vecs"] = vecs
    o["rows"] = np.concatenate([a["L0_ffn_b2"], a["L1_attn_proj_out_b"], np.ones(128, f)])[None]
    o["decay"] = chunks(a["L1_attn_A"])
    o["pinT"] = chunks(a["L1_attn_proj_in_w"].T)
    o["poutT"] = chunks(a["L1_attn_proj_out_w"].T)
    o["wBT"] = chunks(a["L1_attn_B_w"].T)
    cw = np.zeros((4, 32, 256), f)
    cw[:, :4] = a["L1_attn_C_w"].T.reshape(4, 4, 256).transpose(1, 0, 2)
    o["CwP"] = cw.reshape(128, 2, 128)
    onesel = np.zeros((128, 4, 32), f)
    for q in range(4):
        onesel[:, q, q] = 1
    o["onesel"] = onesel
    o["e16"] = np.tile(np.eye(16, dtype=f), (3, 1)).astype(np.uint16) * np.uint16(0x3F80)
    o["sel_e"] = np.tile(np.repeat(np.eye(16, dtype=f), 176, axis=1), (3, 1)).astype(np.uint16) * np.uint16(0x3F80)
    o["seg"] = a["itok_BxS_0_1023"].reshape(8, 128).T.astype(np.int32)
    o["wgateT"] = chunks(a["L1_ffn_gate_w"].T)
    r = np.arange(64)
    swp = (r + 32) % 64
    wqr = a["L1_xattn_W_qr"].reshape(96, 16, 64)
    o["wqr_raw"] = wqr.reshape(96, 8, 128)
    o["wqr_swp"] = wqr[:, :, swp].reshape(96, 8, 128)
    o["w_dq"] = chunks(a["L1_xattn_W_dq"])
    o["w_kvc"] = chunks(np.tile(a["L1_xattn_W_kvc"], (1, 2)))
    kr = a["L1_xattn_W_kr"]
    o["w_kr"] = np.stack([np.tile(kr, (1, 2)), np.tile(kr[:, swp], (1, 2))], axis=1)
    inv = (1.0 / 10000.0 ** (np.arange(32, dtype=f) / 32)).astype(f)
    ang = np.arange(256, dtype=f)[:, None] * inv
    c, s = np.cos(ang).T.astype(f), np.sin(ang).T.astype(f)
    o["tab_kc"] = np.concatenate([c, c, c, c])
    o["tab_ks"] = np.concatenate([-s, s, -s, s])
    scale = f(192 ** -0.5)
    o["tab_qc"] = o["tab_kc"] * scale
    o["tab_qs"] = o["tab_ks"] * scale
    o["iota4"] = np.tile(np.arange(256, dtype=f) + 4, (128, 1))
    o["reset"] = np.tile((np.arange(128) % 16 != 0).astype(f), (128, 1))
    o["gateT"] = chunks(a["L1_ffn_w_gate"].reshape(2816, 256).T)
    o["upT"] = chunks(a["L1_ffn_w_up"].reshape(2816, 256).T)
    o["downT"] = chunks(a["L1_ffn_w_down"].transpose(0, 2, 1).reshape(2816, 256))
    return {k: np.ascontiguousarray(v) for k, v in o.items()}


def kernel(**inputs):
    import concourse.bacc as bacc
    from concourse import mybir
    from concourse.bass_utils import run_bass_kernel_spmd

    arrays = laid_out(inputs)
    nc = bacc.Bacc("TRN2", target_bir_lowering=False, num_devices=1)
    d = {k: nc.dram_tensor("in_" + k, v.shape, mybir.dt.from_np(v.dtype), kind="ExternalInput").ap()
         for k, v in arrays.items()}
    out = nc.dram_tensor("out", (8, 128, 256), mybir.dt.float32, kind="ExternalOutput").ap()
    build(nc, d, out)
    r = run_bass_kernel_spmd(nc, [{"in_" + k: v for k, v in arrays.items()}], core_ids=[0])
    return r.results[0]["out"].reshape(4, 256, 256)
```

```python
def build(nc, d, out):
    import numpy as np
    from concourse import mybir
    from contextlib import ExitStack

    f32, f32r, bf16 = mybir.dt.float32, mybir.dt.float32r, mybir.dt.bfloat16
    i32, u16 = mybir.dt.int32, mybir.dt.uint16
    ALU = mybir.AluOpType
    ACT = mybir.ActivationFunctionType
    AX = mybir.AxisListType.X

    B, S, D = 4, 256, 256
    P = 128
    T = B * S
    NT = T // P
    DC = D // P
    HALF = 512
    NH = 16
    NPAIR = NH // 2
    PAD = 32
    HD0 = 16
    EPS = 1e-5
    QC, KVC = 96, 64
    MLA_SCALE = float((128 + 64) ** -0.5)
    ST = 16
    NE, FF = 16, 176
    FCH = NE * FF // P
    TOPK = 6
    GU, DN = 2 * DC * P, D
    RAW, HID = 4, 3
    NEG = -float(np.frombuffer(np.uint32(np.float32(1e30).view(np.uint32) & 0xFFFF0000).tobytes(), np.float32)[0])
    LATQ = 5
    KROPE = (3, 0, 1, 2)
    LAG = {"a0_": 3, "a4_": 3}
    RING = {"a0_": 6, "a4_": 4}
    SUMS = {"a0_": 1, "a4_": 1}
    E0, F0 = 4, 256
    PER_EXPERT = 12500 // E0

    ctx = ExitStack()
    with ctx:
        def sb(name, shape, dt=f32):
            return ctx.enter_context(nc.sbuf_tensor(name, shape, dt))

        sems = {}

        def sem(name):
            if name not in sems:
                sems[name] = ctx.enter_context(nc.semaphore(name))
            return sems[name]

        x_tok = sb("x_tok", [P, NT, D])
        xT = sb("xT", [P, DC, T])
        A = sb("A", [P, 16384])
        x_parts = sb("x_parts", [P, 2, DC, T], f32r)
        gu_parts = sb("gu_parts", [P, 2, 2, GU], f32r)
        down_parts = sb("down_parts", [P, 3, 2, DN], f32r)
        hid_parts = sb("hid_parts", [P, HID, 2, HALF], f32r)
        C = sb("C", [P, 8192])
        ctxT = sb("ctxT", [P, B, DC, 256])
        probs = sb("probs", [P, 4, 2, 256])
        probsT = sb("probsT", [P, 2, 2, 2, 256])
        ident = sb("ident", [P, P])
        ident_b = sb("ident_b", [P, P], bf16)
        fold_qk = sb("fold_qk", [P, NPAIR, P])
        qk_fold = fold_qk[0:QC]
        probs_more = fold_qk[:, :, :].rearrange("p (r j k) q -> p r j (k q)", r=2, j=2)
        vo_fold = sb("vo_fold", [P, NPAIR, D])
        probsT_more = vo_fold[:, :, :].rearrange("p (r k j) q -> p r k j q", r=2, k=2)
        neg_max = sb("neg_max", [P, 6, 2])
        row_sum = sb("row_sum", [P, 6, 2])
        row_rec = sb("row_rec", [P, 6, 2])
        stats = sb("stats", [P, NT, 6])
        meanvar = sb("meanvar", [P, NT, 2])
        veps = sb("veps", [P, NT])
        rstd = sb("rstd", [P, NT])
        minus_half = sb("minus_half", [P, NT])
        vecs = sb("vecs", [P, 8, 2])
        rows = sb("rows", [1, 8 + 256 + 128])
        small = sb("small", [P, 12, 128])
        small_b = sb("small_b", [P, 128], bf16)
        decay = sb("decay", [P, DC, ST])
        wBT = sb("wBT", [P, DC, ST])
        wgateT = sb("wgateT", [P, DC, NE])
        w2s = sb("w2s", [P, DC, 8])
        pieces = sb("pieces", [P, NT, 48])
        onesel = sb("onesel", [P, 4, 32])
        e16 = sb("e16", [48, ST], bf16)
        piecesT = sb("piecesT", [48, T], bf16)
        sel_e = sb("sel_e", [48, P], bf16)
        seg_i = sb("seg_i", [P, NT], i32)
        seg_f = sb("seg_f", [P, NT])
        top8 = sb("top8", [P, NT, 8])
        bank = [ctx.enter_context(nc.psum_tensor(f"bank{i}", [P, 512], f32)) for i in range(8)]

        def view(t, at, shape, dt=None):
            n = 1
            for k in shape[1:]:
                n *= k
            v = t[0:shape[0], at:at + n]
            if len(shape) == 3:
                v = v.rearrange("p (a b) -> p a b", a=shape[1])
            if len(shape) == 4:
                v = v.rearrange("p (a b c) -> p a b c", a=shape[1], b=shape[2])
            return v

        ctx_flat = ctxT[:, :, :, :].rearrange("p b c t -> p (b c t)")
        mask_m = ctx_flat[:, 0:1024].bitcast(bf16).rearrange("p (i k) -> p i k", i=NT)
        tab_qc = ctx_flat[:, 1024:1280]
        tab_qs = ctx_flat[:, 1280:1536]
        reset = ctx_flat[:, 1536:1664]
        distance = ctx_flat[:, 1664:1920]
        qT = view(A, 0, [P, 4, T])
        kT = view(A, 4096, [P, 4, T])
        v_pad = view(A, 8192, [P, NT, NH * PAD])
        oT = view(A, 12288, [P, 4, T])
        wq = view(C, 0, [P, DC, 512])
        wk_raw = view(C, 1024, [P, DC, 512])
        wk_swp = view(C, 2048, [P, DC, 512])
        wv = view(C, 3072, [P, DC, D])
        wo_pad = view(C, 3584, [P, 4, D])
        tab_q = view(C, 4608, [P, S])
        tab_c = view(C, 4864, [P, S])
        tab_s = view(C, 5120, [P, S])
        w1 = view(C, 5376, [P, DC, D])
        vT = view(C, 5888, [P, DC, 512])
        uw = view(C, 6912, [P, 4, D])
        causal = sb("causal", [P, P])
        causal_b = sb("causal_b", [P, P], bf16)
        w_uqT = view(A, 8192, [P, NH, QC])
        w_ukT = view(A, 9728, [P, NH, KVC])
        w_uvT = view(A, 10752, [P, NH, KVC])
        w_o = view(A, 11776, [P, NH, D])
        tid_f = view(C, 0, [P, T])
        emask = [view(C, 1024 + 512 * e, [P, 512]).bitcast(bf16) for e in range(E0)]
        tid_i = probsT[:, 0].rearrange("p a b c -> p (a b c)").bitcast(i32)
        lt_tmp = probsT[:, 1].rearrange("p a b c -> p (a b c)")
        pinT = view(C, 0, [P, DC, D])
        poutT = view(C, 512, [P, DC, D])
        CwP = view(C, 1024, [P, DC, P])
        hid0 = view(A, 0, [P, 8, T])
        silu0 = probs[:, :].rearrange("p r a b -> p r (a b)")
        h1T = view(A, 0, [P, DC, T])
        bc_s = view(A, 2048, [P, 2, HALF])
        vxa = view(A, 4096, [P, 4, T])
        xpT = view(A, 0, [P, DC, T])
        dl = view(A, 2048, [P, 4, T])
        hs = view(A, 6144, [P, 2, 4 * T]).rearrange("p r (j t) -> p r j t", j=4)
        zT = probs[:, 0:2].rearrange("p a b c -> p (a b c)")
        qm = view(A, 0, [P, 2 * NH, S])
        om = view(A, 8192, [P, NPAIR, T])
        keys_a = view(C, 0, [P, T])
        keys_b = view(C, 1024, [P, T])
        kv_tok = view(C, 2048, [P, NT, KVC])
        qcT = view(C, 2560, [QC, T])
        wqr_raw = view(C, 3584, [QC, NPAIR, P])
        wqr_swp = view(C, 4608, [QC, NPAIR, P])
        w_dq = view(C, 5632, [P, DC, QC])
        w_kvc = view(C, 5824, [P, DC, P])
        w_kr = view(C, 6080, [KVC, 2, P])
        tab_kc = view(C, 6336, [P, S])
        tab_ks = view(C, 6592, [P, S])
        iota4 = view(C, 6848, [P, 256])
        ropes = view(C, 7104, [P, 2, 512])
        cw_rows = view(A, 0, [P, T])
        silu1 = view(A, 1024, [P, 2, HALF])
        hid1 = view(A, 2048, [P, 2, HALF])
        raw = [view(C, (GU + DN) * r, [P, GU + DN]) for r in range(RAW)]

        def bc(ap, n, dim=1):
            v = ap.unsqueeze(dim)
            shape = list(v.shape)
            shape[dim] = n
            return v.broadcast_to(shape)

        LOADS = {
            "ld_first": ("xT", "wq", "tab_q"), "ld_keys": ("wk_raw", "wk_swp", "tab_c", "tab_s", "wv"),
            "ld_const": ("ident", "causal", "x_tok", "tid"),
            "ld_out": ("wo_pad",), "ld_fold": ("w_uqT", "w_ukT", "w_uvT", "w_o"), "ld_ctx": ("ctxT",),
            "ld_ffn": ("w1", "vT", "uw", "w2s", "vecs", "rows", "wBT", "onesel", "e16", "seg", "wgateT", "sel_e"),
            "ld_decay": ("decay",), "ld_scan": ("pinT", "poutT", "CwP"),
            "ld_latent": ("wqr_raw", "wqr_swp", "w_dq", "w_kvc", "w_kr", "tab_kc", "tab_ks", "iota4"),
            "ld_tabs": ("tab_qc", "tab_qs", "reset"), 
        }
        GROUP = {name: g for g, names in LOADS.items() for name in names}

        def loaded(eng, *names):
            for g in sorted({GROUP[n] for n in names}):
                eng.wait_ge(sem(g), 16 * len(LOADS[g]))

        AT_ONCE = {"a0_": 2, "a4_": 1}

        def pT_slot(n, g):
            g %= 2 * AT_ONCE[n]
            return probsT[:, g] if g < 2 else probsT_more[:, g - 2]

        def probs_slot(n, u):
            r = u % RING[n]
            return probs[:, r] if r < 4 else probs_more[:, r - 4]

        def copy_probs(eng, n, v, causal_keys, copy, which):
            g, kcs = v // 2, 1 + v % 2 if causal_keys else 2
            G = g // AT_ONCE[n]
            eng.wait_ge(sem(n + "tr"), v + 1)
            if G >= 2:
                eng.wait_ge(sem(n + "av"), G - 1)
            src = bank[2 + v % 2][:, 0:kcs * 256].rearrange("p (k j q) -> p k j q", k=kcs, j=2)
            copy(pT_slot(n, g)[:, 0:kcs, :, (v % 2) * P:(v % 2 + 1) * P], src
                 ).then_inc(sem(n + "pT" + which), 1)

        def group_at(n, step):
            G, r = divmod(step, 2 * AT_ONCE[n])
            return G if r == 0 and 0 <= G < B * NPAIR // AT_ONCE[n] else None

        def q_banks(n):
            return (bank[(7, 6)[n % 2]], bank[(LATQ, 4)[n % 2]]) if n < NPAIR else (bank[7], bank[LATQ])

        def next_pair(u):
            return NPAIR * (u // 16 + 1) + u % 16 // 2 if u % 2 and u < 16 * (B - 1) else None

        block = ctx.enter_context(nc.Block())

        @block.sync
        def _(sp):
            def load(name, dst, src=None):
                sp.dma_start(dst, d[name] if src is None else src).then_inc(sem(GROUP[name]), 16)

            load("xT", xT[:, :, :])
            load("wq", wq)
            load("tab_q", tab_q)
            load("wk_raw", wk_raw)
            load("wk_swp", wk_swp)
            load("tab_c", tab_c)
            load("tab_s", tab_s)
            load("wv", wv)
            load("ident", ident[:, :])
            load("causal", causal[:, :])
            load("x_tok", x_tok[:, :, :])
            load("tid", tid_i, d["tid"].partition_broadcast(P))
            load("wo_pad", wo_pad)
            load("ctxT", ctxT[:, :, :, :])
            load("w1", w1)
            load("vT", vT)
            load("uw", uw)
            load("w2s", w2s[:, :, :])
            load("vecs", vecs[:, :, :])
            load("rows", rows[:, :])
            load("decay", decay[:, :, :])
            load("wBT", wBT[:, :, :])
            load("onesel", onesel[:, :, :])
            load("e16", e16[:, :].bitcast(u16))
            load("seg", seg_i[:, :])
            load("wgateT", wgateT[:, :, :])
            load("sel_e", sel_e[:, :].bitcast(u16))
            sp.wait_ge(sem("fin0"), NT)
            load("w_uqT", w_uqT)
            load("w_ukT", w_ukT)
            load("w_uvT", w_uvT)
            load("w_o", w_o)
            sp.wait_ge(sem("fin1"), NT)
            load("pinT", pinT)
            load("poutT", poutT)
            load("CwP", CwP)
            sp.wait_ge(sem("fin2"), NT)
            load("wqr_raw", wqr_raw)
            load("wqr_swp", wqr_swp)
            load("w_dq", w_dq)
            load("w_kvc", w_kvc)
            load("w_kr", w_kr)
            load("tab_kc", tab_kc)
            load("tab_ks", tab_ks)
            load("iota4", iota4)
            sp.wait_ge(sem("fin3"), NT)
            sp.wait_ge(sem("k_tok"), 1)
            load("tab_qc", tab_qc)
            load("tab_qs", tab_qs)
            load("reset", reset)
            sp.wait_ge(sem("fin4"), 1)
            for c in range(FCH):
                if c >= RAW:
                    sp.wait_ge(sem("m_w"), c - RAW + 1)
                sp.dma_start(raw[c % RAW], d["experts"][c]).then_inc(sem(f"ld_raw{c % RAW}"), 16)
            for i in range(NT):
                sp.wait_ge(sem("ln5_x"), i + 1)
                sp.dma_start(out[i], x_tok[:, i, :]).then_inc(sem("stored"), 16)
            sp.wait_ge(sem("stored"), 16 * NT)

        @block.tensor
        def _(pe):
            mm = pe.matmul

            def ln_transposes(k, half):
                for q in (2 * half, 2 * half + 1):
                    pe.wait_ge(sem(f"ln{k}_x"), 2 * q + 2)
                    if q >= 2:
                        pe.wait_ge(sem(f"ln{k}_xT"), q - 1)
                    for j in range(2):
                        for c in range(DC):
                            o = (2 * j + c) * P
                            last = pe.transpose(bank[4 + q % 2][:, o:o + P],
                                                x_tok[:, 2 * q + j, c * P:(c + 1) * P], ident[:, :])
                    last.then_inc(sem(f"ln{k}_t"), 1)

            def final(k, tiles, emit):
                for i in tiles:
                    if i >= 2:
                        pe.wait_ge(sem(f"ln{k}_r"), i - 1)
                    emit(i, bank[6 + i % 2][:, 0:D]).then_inc(sem(f"fin{k}"), 1)

            def close(k, emit):
                final(k, range(6), emit)
                ln_transposes(k, 0)
                final(k, range(6, NT), emit)

            def proj(o, w, col, half, m=P):
                for c in range(DC):
                    last = mm(o, w[:, c, col:col + m], xT[:, c, half * HALF:(half + 1) * HALF],
                              start=(c == 0), stop=(c == DC - 1))
                return last

            def attention(n, scores, apply, causal_keys, ring, filler=None):
                U = 2 * B * NPAIR
                for u in range(U + LAG[n] + 2 + 2 * AT_ONCE[n]):
                    if u < U:
                        if u >= len(ring):
                            pe.wait_ge(sem(n + "exp"), u - len(ring) + 1)
                        scores(u, bank[ring[u % len(ring)]]).then_inc(sem(n + "sc"), 1)
                    if filler:
                        filler(u)
                    v = u - LAG[n]
                    if 0 <= v < U:
                        pe.wait_ge(sem(n + "norm"), v + 1)
                        if v >= 2:
                            pe.wait_ge(sem(n + "pT" + "ad"[v % 2]), v // 2)
                        for kc in range(1 + v % 2 if causal_keys else 2):
                            for j in range(2):
                                o = (2 * kc + j) * P
                                last = pe.transpose(bank[2 + v % 2][:, o:o + P],
                                                    probs_slot(n, v)[:, j, kc * P:(kc + 1) * P], ident[:, :])
                        last.then_inc(sem(n + "tr"), 1)
                    G = group_at(n, u - LAG[n] - 1 - 2 * AT_ONCE[n])
                    if G is not None:
                        pe.wait_ge(sem(n + "pTa"), AT_ONCE[n] * (G + 1))
                        pe.wait_ge(sem(n + "pTd"), AT_ONCE[n] * (G + 1))
                        if G >= 2:
                            pe.wait_ge(sem(n + "oT"), G - 1)
                        apply(G, bank[(4, 6)[G % 2]]).then_inc(sem(n + "av"), 1)

            loaded(pe, "xT", "wq", "wk_raw", "wk_swp", "wv")
            n = 0
            for w in (wq, wk_raw, wk_swp):
                for c in range(4):
                    for half in range(2):
                        if n >= 4:
                            pe.wait_ge(sem("qkv_out"), n - 3)
                        proj(bank[n % 4][:, :], w, c * P, half).then_inc(sem("qkv"), 1)
                        n += 1
            for i in range(NT):
                if i >= 2:
                    pe.wait_ge(sem("v_out"), i - 1)
                for c in range(DC):
                    last = mm(bank[4 + i % 2][:, 0:D], xT[:, c, i * P:(i + 1) * P], wv[:, c, :],
                              start=(c == 0), stop=(c == DC - 1))
                last.then_inc(sem("v"), 1)

            pe.wait_ge(sem("kT"), 8)
            pe.wait_ge(sem("qkv_out"), 24)
            pe.wait_ge(sem("v_out"), NT)
            pe.wait_ge(sem("const_b"), 2)
            loaded(pe, "ident")

            def scores0(u, o):
                b, p, qt = u // 16, u // 2 % 8, u % 2
                o3 = o[:, :].rearrange("p (j k) -> p j k", j=2)
                for j in range(2):
                    r, c = PAD * (p % 4), 2 * (p // 4) + j
                    mm(o3[:, j, 0:(qt + 1) * P], qT[r:r + PAD, c, b * S + qt * P:b * S + (qt + 1) * P],
                       kT[r:r + PAD, c, b * S:b * S + (qt + 1) * P],
                       start=(j == 0), stop=False, skip_group_check=True)
                return mm(o3[:, :, qt * P:(qt + 1) * P], ident_b[:, :], bc(causal_b[:, :], 2),
                          start=False, stop=True, skip_group_check=True)

            def apply0(G, o):
                b, p = G // 4, 2 * (G % 4)
                for j in range(2):
                    for kc in range(2):
                        for i in range(2):
                            r = PAD * ((p + i) % 4)
                            h = 4 * (2 * (p // 4) + j) + (p + i) % 4
                            last = mm(o[r:r + PAD, j * S + kc * P:(j + 1) * S],
                                      v_pad[:, 2 * b + kc, PAD * h:PAD * h + PAD],
                                      pT_slot("a0_", 2 * G + i)[:, kc, j, kc * P:S], start=(kc == 0),
                                      stop=(kc == 1), skip_group_check=True)
                return last

            def keep_clock(u):
                for _ in range(1 if u >= LAG["a0_"] + 2 else 6):
                    mm(bank[7][:, :], ident_b[:, :], bc(ident_b[:, :], 4), start=True, stop=True)

            attention("a0_", scores0, apply0, True, (0, 1, 5), keep_clock)
            pe.wait_ge(sem("a0_oT"), B * NPAIR // 2)
            loaded(pe, "wo_pad")

            def out0(i, o):
                for c in range(4):
                    last = mm(o, oT[:, c, i * P:(i + 1) * P], wo_pad[:, c, :], start=(c == 0), stop=(c == 3))
                return last

            close(0, out0)

            loaded(pe, "ctxT")
            for k in range(16):
                half, e, fc = k // 8, k // 2 % 4, k % 2
                if k == 8:
                    ln_transposes(0, 1)
                pe.wait_ge(sem("ln0_xT"), 2 * (half + 1))
                if k >= 4:
                    pe.wait_ge(sem("r_mul"), k - 3)
                proj(bank[k % 4][:, :], ctxT[:, e], fc * P, half).then_inc(sem("r_up"), 1)

            def out1(i, o):
                pe.wait_ge(sem("r_hid"), 8 * (i // 4 + 1))
                for k in range(8):
                    last = mm(o, hid0[:, k, i * P:(i + 1) * P], ctxT[:, k // 2, k % 2, :],
                              start=(k == 0), stop=(k == 7))
                return last

            close(1, out1)

            loaded(pe, "w1", "w2s", "vT", "uw", "rows")

            def hidden(half):
                for c in range(DC):
                    k = 2 * half + c
                    pe.wait_ge(sem("ln1_xT"), 2 * (half + 1))
                    if half:
                        pe.wait_ge(sem("f_hT"), c + 1)
                    proj(bank[c][:, :], w1, c * P, half).then_inc(sem("f_h"), 1)

            def low_rank(k):
                if k in (2, 3):
                    pe.wait_ge(sem("f_hT"), k + 1)
                if k >= 4:
                    pe.wait_ge(sem("f_vx"), k - 3)
                proj(bank[(2 + k) % 4][:, :], vT, (k % 4) * P, k // 4).then_inc(sem("f_v"), 1)

            def mixing(k):
                c, half = k % 4, k // 4
                pe.wait_ge(sem("f_alpha"), 1)
                if k >= 2:
                    pe.wait_ge(sem("f_bc_s"), k - 1)
                for i in range(4):
                    for j in range(2):
                        at = 8 * (4 * half + i) + 2 * c + j
                        last = mm(bank[6 + k % 2][64 * j:64 * j + 64, i * P:(i + 1) * P],
                                  small[:, 5, at:at + 1].broadcast_to([P, 64]), ident[:, :],
                                  start=True, stop=True, skip_group_check=True)
                last.then_inc(sem("f_bc"), 1)

            def fold(f):
                o = bank[6 + f % 2]
                if f >= 2:
                    pe.wait_ge(sem("fold_out"), f - 1)
                for p in range(4 * f, 4 * f + 4) if f < 2 else range(2 * f - 4, 2 * f - 2):
                    for j in range(2):
                        h = 2 * p + j
                        if f < 2:
                            at = (p % 4) * P + (1 - j) * KVC
                            last = mm(o[0:QC, at:at + KVC], w_uqT[:, h, :], w_ukT[:, h, :],
                                      start=True, stop=True)
                        else:
                            last = mm(o[KVC * j:KVC * j + KVC, (p % 2) * D:(p % 2 + 1) * D],
                                      w_uvT[:, h, :], w_o[:, h, :], start=True, stop=True)
                last.then_inc(sem("fold"), 1)

            hidden(0)
            low_rank(0)
            low_rank(1)
            ln_transposes(1, 1)
            hidden(1)
            pe.wait_ge(sem("f_hT"), 4)
            for i in range(NT):
                o = bank[4][:, 8 * i:8 * i + 8]
                for c in range(DC):
                    mm(o, h1T[:, c, i * P:(i + 1) * P], w2s[:, c, :], start=(c == 0), stop=False)
                last = mm(o, rows[0:1, 264:264 + P], rows[0:1, 0:8], start=False, stop=True)
            last.then_inc(sem("f_lg"), 1)
            low_rank(2)
            low_rank(3)
            loaded(pe, "w_uqT", "w_ukT", "w_uvT", "w_o")
            for f in range(6):
                fold(f)
            pe.wait_ge(sem("fold_out"), 6)
            for k in range(8):
                mixing(k)
                if k < 4:
                    low_rank(k + 4)

            def out2(i, o):
                pe.wait_ge(sem("f_vx"), 4 * (i // 4 + 1))
                pe.wait_ge(sem("f_bc_s"), 8)
                for c in range(4):
                    last = mm(o, vxa[:, c, i * P:(i + 1) * P], uw[:, c, :], start=(c == 0), stop=(c == 3))
                return last

            close(2, out2)

            loaded(pe, "pinT", "wBT", "CwP", "onesel", "e16", "poutT")
            for k in range(4):
                c, half = k % 2, k // 2
                if k == 2:
                    ln_transposes(2, 1)
                pe.wait_ge(sem("ln2_xT"), 2 * (half + 1))
                proj(bank[k][:, :], pinT, c * P, half).then_inc(sem("s_xp"), 1)
            pe.wait_ge(sem("s_xpT"), 4)
            for i in range(NT):
                for c in range(DC):
                    last = mm(bank[4][:, ST * i:ST * i + ST], xpT[:, c, i * P:(i + 1) * P], wBT[:, c, :],
                              start=(c == 0), stop=(c == DC - 1))
            last.then_inc(sem("s_pre"), 1)

            def pieces_transposed(n):
                pe.wait_ge(sem(n + "pieces"), 1)
                for i in range(NT):
                    last = pe.transpose(bank[i // 4][0:48, (i % 4) * P:(i % 4 + 1) * P],
                                        pieces[:, i, :], ident[:, :])
                last.then_inc(sem(n + "piecesT"), 1)
                pe.wait_ge(sem(n + "piecesB"), 2)

            pieces_transposed("s_")

            def step_sizes(q):
                for s in range(4 * q, 4 * q + 4):
                    for half in range(2):
                        r = 2 * s + half
                        if r >= 4:
                            pe.wait_ge(sem("s_bc_s"), r - 3)
                        mm(bank[r % 4][:, :], e16[:, s:s + 1].broadcast_to([48, P]),
                           piecesT[:, half * HALF:(half + 1) * HALF], start=True, stop=True
                           ).then_inc(sem("s_bc"), 1)

            def state_sums(g):
                pe.wait_ge(sem("s_scan"), g + 1)
                for half in range(2):
                    for j in range(4):
                        last = mm(bank[6 + half][32 * j:32 * j + 32, :], onesel[:, g // 2, :],
                                  hs[:, g % 2, j, half * HALF:(half + 1) * HALF],
                                  start=(g == 0), stop=(g == 7), skip_group_check=True)
                last.then_inc(sem("s_z"), 1)

            step_sizes(0)
            for q in range(1, 4):
                step_sizes(q)
                state_sums(2 * q - 2)
                state_sums(2 * q - 1)
            state_sums(6)
            state_sums(7)
            pe.wait_ge(sem("s_zT"), 2)
            for k in range(4):
                c, half = k % 2, k // 2
                mm(bank[k][:, :], CwP[:, c, :], zT[:, half * HALF:(half + 1) * HALF],
                   start=True, stop=True).then_inc(sem("s_y"), 1)

            def out3(i, o):
                pe.wait_ge(sem("s_yT"), 2 * (i // 4 + 1))
                for c in range(DC):
                    mm(o, xpT[:, c, i * P:(i + 1) * P], poutT[:, c, :], start=(c == 0), stop=False)
                return mm(o, rows[0:1, 264:264 + P], rows[0:1, 8:264], start=False, stop=True)

            close(3, out3)

            loaded(pe, "w_kvc", "w_kr", "w_dq")
            for half in range(2):
                for c in range(DC):
                    last = mm(bank[half][:, :], w_kvc[:, c, :],
                              ctxT[:, 2 * half:2 * half + 2, c, :], start=(c == 0), stop=(c == DC - 1))
                last.then_inc(sem("k_lat"), 1)
            for i in range(NT):
                for c in range(DC):
                    last = mm(bank[2][:, KVC * i:KVC * i + KVC],
                              ctxT[:, i // 2, c, (i % 2) * P:(i % 2 + 1) * P], w_kvc[:, c, 0:KVC],
                              start=(c == 0), stop=(c == DC - 1))
            last.then_inc(sem("k_tok"), 1)
            for half in range(2):
                pe.wait_ge(sem("k_latT"), 2 * (half + 1))
                if half:
                    pe.wait_ge(sem("k_tokT"), 1)
                for r in range(2):
                    mm(bank[KROPE[2 * half + r]][:, :], w_kr[:, r, :],
                       keys_b[0:KVC, half * HALF:(half + 1) * HALF], start=True, stop=True
                       ).then_inc(sem("k_rope"), 1)
            ln_transposes(3, 1)
            pe.wait_ge(sem("k_mul"), 4)
            for half in range(2):
                pe.wait_ge(sem("ln3_xT"), 2 * (half + 1))
                for c in range(DC):
                    last = mm(bank[half][0:QC, :], w_dq[:, c, :], xT[:, c, half * HALF:(half + 1) * HALF],
                              start=(c == 0), stop=(c == DC - 1))
                last.then_inc(sem("qc"), 1)
            loaded(pe, "wqr_raw", "wqr_swp")
            pe.wait_ge(sem("qcT"), 2)
            pe.wait_ge(sem("k_add"), 4)
            pe.wait_ge(sem("k_tokT"), 1)
            pe.wait_ge(sem("mask"), NT)

            def query_pair(n):
                rhs = qcT[:, n // NPAIR * S:(n // NPAIR + 1) * S]
                p = n % NPAIR
                rope, lat = q_banks(n)
                if n >= 2:
                    ahead = 1 if n >= NPAIR else 2
                    pe.wait_ge(sem("q_mul"), n + 1 - ahead)
                    pe.wait_ge(sem("q_lat"), n + 1 - ahead)
                mm(rope[:, 0:S], wqr_raw[:, p, :], rhs, start=True, stop=True)
                mm(rope[:, S:2 * S], wqr_swp[:, p, :], rhs, start=True, stop=True
                   ).then_inc(sem("q_rope"), 1)
                mm(lat[:, 0:S], qk_fold[:, p, :], rhs, start=True, stop=True).then_inc(sem("q_l"), 1)

            def next_queries(u):
                n = next_pair(u)
                if n:
                    query_pair(n)

            def scores4(u, o):
                b, p, qt = u // 16, u // 2 % 8, u % 2
                if u % 16 == 0:
                    pe.wait_ge(sem("q_add"), NPAIR * (b + 1))
                    pe.wait_ge(sem("q_lat"), NPAIR * (b + 1))
                o3 = o[:, :].rearrange("p (j k) -> p j k", j=2)
                for j in range(2):
                    mm(o3[:, j, :], qm[:, NH * (b % 2) + 2 * p + j, qt * P:(qt + 1) * P],
                       (keys_a, keys_b)[j][:, b * S:(b + 1) * S], start=(j == 0), stop=False,
                       skip_group_check=True)
                return mm(o3, ident_b[:, :], bc(mask_m[:, 2 * b + qt, :], 2), start=False, stop=True,
                          skip_group_check=True)

            def apply4(g, o):
                b = g // 8
                for kc in range(2):
                    for j in range(2):
                        last = mm(o[KVC * j:KVC * j + KVC, 0:S], kv_tok[:, 2 * b + kc, :],
                                  probsT[:, g % 2, kc, j, :], start=(kc == 0), stop=(kc == 1),
                                  skip_group_check=True)
                return last

            for n in range(NPAIR):
                query_pair(n)
            attention("a4_", scores4, apply4, False, (0, 1), next_queries)
            pe.wait_ge(sem("a4_oT"), B * NPAIR)

            def out4(i, o):
                for p in range(NPAIR):
                    last = mm(o, om[:, p, i * P:(i + 1) * P], vo_fold[:, p, :], start=(p == 0),
                              stop=(p == NPAIR - 1))
                return last

            close(4, out4)
            ln_transposes(4, 1)

            loaded(pe, "wgateT", "sel_e")

            def product3(o, left, right, first, last):
                for n, (l, r) in enumerate(((0, 0), (1, 0), (0, 1))):
                    ins = mm(o, left[l], right[r], start=first and n == 0, stop=last and n == 2,
                             skip_group_check=True)
                return ins

            def gate_up(k):
                c, half = k // 2, k % 2
                hh = slice(half * HALF, (half + 1) * HALF)
                pe.wait_ge(sem("m_w"), c + 1)
                if k >= 2:
                    pe.wait_ge(sem("m_silu"), k - 1)
                    pe.wait_ge(sem("m_mul"), k - 1)
                for w, name in enumerate(("m_g", "m_u")):
                    for dc in range(DC):
                        at = (DC * w + dc) * P
                        last = product3(bank[2 * w + k % 2][:, :],
                                        [gu_parts[:, c % 2, r, at:at + P] for r in range(2)],
                                        [x_parts[:, r, dc, hh] for r in range(2)], dc == 0, dc == DC - 1)
                    last.then_inc(sem(name), 1)

            def down(k):
                c, half = k // 2, k % 2
                pe.wait_ge(sem("m_lo"), k + 1)
                for i in range(4):
                    last = product3(bank[4 + 2 * half + i // 2][:, (i % 2) * D:(i % 2 + 1) * D],
                                    [hid_parts[:, k % HID, r, i * P:(i + 1) * P] for r in range(2)],
                                    [down_parts[:, c % 3, r, :] for r in range(2)],
                                    c == 0 and i % 2 == 0, c == FCH - 1)
                    if c == FCH - 1:
                        last.then_inc(sem("fin5"), 1)
                if c < FCH - 1:
                    last.then_inc(sem("m_down"), 1)

            pe.wait_ge(sem("ln4_xT"), 4)
            for i in range(NT):
                for c in range(DC):
                    last = mm(bank[6][:, NE * i:NE * i + NE], xT[:, c, i * P:(i + 1) * P], wgateT[:, c, :],
                              start=(c == 0), stop=(c == DC - 1))
            last.then_inc(sem("m_lg"), 1)
            for k in range(2):
                pe.wait_ge(sem("x_lo"), k + 1)
                gate_up(k)
            pe.wait_ge(sem("m_pieces"), 1)
            for i in range(NT):
                last = pe.transpose(bank[4 + i // 4][0:48, (i % 4) * P:(i % 4 + 1) * P],
                                    pieces[:, i, :], ident[:, :])
            last.then_inc(sem("m_piecesT"), 1)
            for half in range(2):
                pe.wait_ge(sem("m_piecesB"), half + 1)
                mm(bank[6 + half][:, :], sel_e[:, :], piecesT[:, half * HALF:(half + 1) * HALF],
                   start=True, stop=True).then_inc(sem("m_cw"), 1)
            for k in range(2, 2 * FCH + 2):
                if k < 2 * FCH:
                    gate_up(k)
                if k == 2:
                    pe.wait_ge(sem("cw_rows"), 2)
                down(k - 2)

        @block.vector
        def _(dve):
            tt, ts, stt, cp = dve.tensor_tensor, dve.tensor_scalar, dve.scalar_tensor_tensor, dve.tensor_copy
            chain = [0]

            def link(ins):
                chain[0] += 1
                ins.then_inc(sem("dve_chain"), 1)
                dve.wait_ge(sem("dve_chain"), chain[0])

            def norm(k, scale, place):

                def residual(i):
                    dve.wait_ge(sem(f"fin{k}"), i + 1)
                    if i == 0:
                        if k == 0:
                            loaded(dve, "x_tok")
                        else:
                            dve.wait_ge(sem(f"ln{k-1}_t"), 4)
                    stt(x_tok[:, i, :], x_tok[:, i, :], scale, place(i), ALU.mult, ALU.add
                        ).then_inc(sem(f"ln{k}_r"), 1)
                    dve.wait_ge(sem(f"ln{k}_r"), i + 1)
                    link(dve.bn_stats(stats[:, i, :], x_tok[:, i, :]))
                    dve.bn_aggr(meanvar[:, i, :], stats[:, i, :]).then_inc(sem(f"ln{k}_v"), 1)

                def normalise(i):
                    dve.wait_ge(sem(f"ln{k}_v"), i + 1)
                    dve.wait_ge(sem(f"ln{k}_rstd"), i // 4 + 1)
                    ts(x_tok[:, i, :], x_tok[:, i, :], meanvar[:, i, 0:1], rstd[:, i:i + 1],
                       ALU.subtract, ALU.mult).then_inc(sem(f"ln{k}_x"), 1)

                for i in range(6):
                    residual(i)
                for i in range(4):
                    normalise(i)
                for i in range(6, NT):
                    residual(i)
                for i in range(4, NT):
                    normalise(i)

            fin_bank = lambda i: bank[6 + i % 2][:, 0:D]

            def softmax_small(n, lg, w, e_row):
                sh = lambda r: small[:, r, 0:NT * w].rearrange("p (i w) -> p i w", w=w)
                col = small[:, 11, 0:NT]
                link(dve.tensor_reduce(col, lg, axis=AX, op=ALU.max, negate=True))
                tt(sh(0), lg, bc(col, w, 2), ALU.add).then_inc(sem(n + "sub"), 1)
                dve.wait_ge(sem(n + "e"), 1)
                link(dve.tensor_reduce(small[:, 11, 8:16], sh(1), axis=AX, op=ALU.add))
                link(dve.reciprocal(small[:, 11, 16:24], small[:, 11, 8:16]))
                return tt(sh(e_row), sh(1), bc(small[:, 11, 16:24], w, 2), ALU.mult)

            def split(n, row):
                src = small[:, row, :].rearrange("p (i w) -> p i w", w=16)
                cur = src
                b3 = small_b[:, :].rearrange("p (i w) -> p i w", w=16)
                rest = small[:, 10, :].rearrange("p (i w) -> p i w", w=16)
                for j in range(2):
                    link(cp(b3, cur))
                    link(cp(pieces[:, :, 16 * j:16 * j + 16], b3))
                    link(tt(rest, cur, pieces[:, :, 16 * j:16 * j + 16], ALU.subtract))
                    cur = rest
                cp(pieces[:, :, 32:48], rest).then_inc(sem(n + "pieces"), 1)

            def attention(n, causal_keys, ring, extra=None):
                U = 2 * B * NPAIR
                for u in range(U + LAG[n] + 2):
                    v = u - LAG[n] - 1
                    if 0 <= v < U and v % 2 == 1:
                        copy_probs(dve, n, v, causal_keys, lambda o, i: cp(o, i), "d")
                    if u < U:
                        keys = (u % 2 + 1) * P if causal_keys else 256
                        s3 = bank[ring[u % len(ring)]][:, :].rearrange("p (j k) -> p j k", j=2)
                        dve.wait_ge(sem(n + "sc"), u + 1)
                        dve.tensor_reduce(neg_max[:, u % RING[n], :], s3[:, :, 0:keys], axis=AX, op=ALU.max,
                                          negate=True).then_inc(sem(n + "max"), 1)
                    v = u - SUMS[n]
                    if 0 <= v < U:
                        dve.wait_ge(sem(n + "exp"), v + 1)
                        if v >= RING[n]:
                            dve.wait_ge(sem(n + "norm"), v - RING[n] + 1)
                        dve.reciprocal(row_rec[:, v % RING[n], :], row_sum[:, v % RING[n], :]).then_inc(sem(n + "rec"), 1)
                    if extra:
                        extra(u)

            loaded(dve, "ident", "causal")
            cp(ident_b[:, :], ident[:, :]).then_inc(sem("const_b"), 1)
            cp(causal_b[:, :], causal[:, :]).then_inc(sem("const_b"), 1)

            loaded(dve, "tab_q", "tab_c", "tab_s")
            n = 0
            for w in range(3):
                for c in range(4):
                    for half in range(2):
                        src = bank[n % 4][:, :].rearrange("p (b s) -> p b s", b=2)
                        hh = slice(half * HALF, (half + 1) * HALF)
                        dve.wait_ge(sem("qkv"), n + 1)
                        if w == 0:
                            dst, tab = qT[:, c, hh], tab_q
                        elif w == 1:
                            dst, tab = kT[:, c, hh], tab_c
                        else:
                            r = (c * 2 + half) % 2
                            if c * 2 + half >= 2:
                                dve.wait_ge(sem("kT"), c * 2 + half - 1)
                            dst, tab = probs[:, r].rearrange("p a b -> p (a b)"), tab_s
                        tt(dst.rearrange("p (b s) -> p b s", b=2), src, bc(tab, 2), ALU.mult
                           ).then_inc(sem("qkv_out"), 1)
                        n += 1
            loaded(dve, "tid")
            link(cp(tid_f, tid_i))
            ts(emask[0], tid_f, float(PER_EXPERT), None, ALU.is_lt).then_inc(sem("emask"), 1)
            for e in (1, 2):
                link(ts(lt_tmp, tid_f, float(PER_EXPERT * (e + 1)), None, ALU.is_lt))
                stt(emask[e], tid_f, float(PER_EXPERT * e), lt_tmp, ALU.is_ge, ALU.mult).then_inc(sem("emask"), 1)
                dve.wait_ge(sem("emask"), e + 1)
            ts(emask[3], tid_f, float(PER_EXPERT * 3), None, ALU.is_ge).then_inc(sem("emask"), 1)

            attention("a0_", True, (0, 1, 5))
            norm(0, 1.0, fin_bank)

            for k in range(16):
                half = k // 8
                dve.wait_ge(sem("r_silu"), k + 1)
                tt(hid0[:, k % 8, half * HALF:(half + 1) * HALF], silu0[:, k % 4, :], bank[k % 4][:, :],
                   ALU.mult).then_inc(sem("r_mul"), 1)
            norm(1, 1.0, fin_bank)

            dve.wait_ge(sem("f_lg"), 1)
            softmax_small("f_", bank[4][:, 0:64].rearrange("p (i w) -> p i w", w=8), 8, 5
                          ).then_inc(sem("f_alpha"), 1)
            for k in range(8):
                c, half = k % 4, k // 4
                dve.wait_ge(sem("f_v"), k + 1)
                dve.wait_ge(sem("f_bc_s"), k + 1)
                tt(vxa[:, c, half * HALF:(half + 1) * HALF], bc_s[:, k % 2, :], bank[(2 + k) % 4][:, :],
                   ALU.mult).then_inc(sem("f_vx"), 1)
            norm(2, 1.0, fin_bank)

            dve.wait_ge(sem("decayed"), 1)
            dve.wait_ge(sem("s_soft"), 1)
            link(tt(small[:, 3, :], small[:, 2, :], small[:, 1, :], ALU.add))
            split("s_", 3)
            for g in range(8):
                c = g % 2
                for j in range(4):
                    s = 4 * (g // 2) + j
                    u_s = hs[:, g % 2, j, :]
                    if c == 0:
                        dve.wait_ge(sem("s_bc_s"), 2 * s + 2)
                        if g >= 2:
                            dve.wait_ge(sem("s_z"), g - 1)
                        link(tt(u_s, dl[:, j, :], xpT[:, 0, :], ALU.mult))
                    else:
                        dve.wait_ge(sem("s_u1"), s + 1)
                    for b in range(B):
                        col = hs[:, g % 2, j, b * S:(b + 1) * S]
                        last = dve.tensor_tensor_scan(col, decay[:, c, s:s + 1].broadcast_to([P, S]), col,
                                                      0.0, ALU.mult, ALU.add)
                last.then_inc(sem("s_scan"), 1)
            for k in range(4):
                c, half = k % 2, k // 2
                hh = slice(half * HALF, (half + 1) * HALF)
                dve.wait_ge(sem("s_y"), k + 1)
                stt(xpT[:, c, hh], xpT[:, c, hh], vecs[:, 2, c:c + 1], bank[k][:, :], ALU.mult, ALU.add
                    ).then_inc(sem("s_yT"), 1)
            norm(3, 2.0, fin_bank)

            loaded(dve, "tab_kc", "tab_ks", "iota4", "seg")
            for half in range(2):
                for r in range(2):
                    n = 2 * half + r
                    dve.wait_ge(sem("k_rope"), n + 1)
                    if half == 1 and r == 0:
                        dve.wait_ge(sem("k_add"), 2)
                    src = bank[KROPE[n]][:, :].rearrange("p (b s) -> p b s", b=2)
                    tt(ropes[:, r, :].rearrange("p (b s) -> p b s", b=2), src, bc((tab_kc, tab_ks)[r], 2),
                       ALU.mult).then_inc(sem("k_mul"), 1)
                dve.wait_ge(sem("k_mul"), 2 * half + 2)
                hh = slice(half * HALF, (half + 1) * HALF)
                tt(keys_a[0:64, hh], ropes[0:64, 0, :], ropes[0:64, 1, :], ALU.add).then_inc(sem("k_add"), 1)
                tt(keys_b[64:128, hh], ropes[64:128, 0, :], ropes[64:128, 1, :], ALU.add).then_inc(sem("k_add"), 1)
            link(cp(seg_f[:, :], seg_i[:, :]))
            dve.wait_ge(sem("k_tok"), 1)
            for i in range(NT):
                link(ts(distance, iota4, seg_f[:, i:i + 1], None, ALU.subtract))
                link(tt(distance, distance, distance, ALU.mult))
                ts(mask_m[:, i, :], distance, 16.0, NEG, ALU.is_gt, ALU.mult).then_inc(sem("mask"), 1)
                dve.wait_ge(sem("mask"), i + 1)

            def rotate_pair(n):
                rope = q_banks(n)[0]
                dve.wait_ge(sem("q_rope"), n + 1)
                if n >= 2:
                    dve.wait_ge(sem("q_add"), n - 1)
                tt(ropes[:, n % 2, 0:S], rope[:, 0:S], tab_qc, ALU.mult)
                tt(ropes[:, n % 2, S:2 * S], rope[:, S:2 * S], tab_qs, ALU.mult).then_inc(sem("q_mul"), 1)

            def rotate_next(u):
                if next_pair(u):
                    rotate_pair(next_pair(u))

            loaded(dve, "tab_qc", "tab_qs")
            for n in range(NPAIR):
                rotate_pair(n)
            attention("a4_", False, (0, 1), rotate_next)
            norm(4, 1.0, fin_bank)

            dve.wait_ge(sem("m_lg"), 1)
            link(softmax_small("m_", bank[6][:, 0:128].rearrange("p (i w) -> p i w", w=16), 16, 3))
            sc3 = small[:, 3, :].rearrange("p (i w) -> p i w", w=16)
            r3 = lambda r: small[:, r, :].rearrange("p (i w) -> p i w", w=16)
            for i in range(NT):
                last = dve.max(top8[:, i, :], sc3[:, i, :])
            link(last)
            thr = top8[:, :, TOPK - 1].unsqueeze(2).broadcast_to([P, NT, NE])
            link(tt(r3(4), sc3, thr, ALU.is_gt))
            link(tt(r3(5), sc3, thr, ALU.is_equal))
            link(dve.tensor_reduce(small[:, 11, 24:32], r3(4), axis=AX, op=ALU.add))
            loaded(dve, "reset")
            link(dve.tensor_tensor_scan(small[:, 6, :], reset[:, :], small[:, 5, :], 0.0, ALU.mult, ALU.add))
            link(tt(r3(7), r3(6), bc(small[:, 11, 24:32], NE, 2), ALU.add))
            link(stt(small[:, 8, :], small[:, 7, :], float(TOPK), small[:, 5, :], ALU.is_le, ALU.mult))
            link(tt(small[:, 9, :], small[:, 8, :], small[:, 4, :], ALU.add))
            link(tt(small[:, 9, :], small[:, 9, :], small[:, 3, :], ALU.mult))
            split("m_", 9)
            def low_part(k):
                dve.wait_ge(sem("m_hi"), k + 1)
                tt(hid_parts[:, k % HID, 1, :], hid1[:, k % 2, :], hid_parts[:, k % HID, 0, :].bitcast(f32),
                   ALU.subtract).then_inc(sem("m_lo"), 1)

            for k in range(2 * FCH):
                half = k % 2
                dve.wait_ge(sem("m_silu"), k + 1)
                dve.wait_ge(sem("m_u"), k + 1)
                if k >= 2:
                    dve.wait_ge(sem("m_lo"), k - 1)
                tt(hid1[:, k % 2, :], silu1[:, k % 2, :], bank[2 + k % 2][:, :], ALU.mult
                   ).then_inc(sem("m_mul"), 1)
                if k < 2:
                    dve.wait_ge(sem("cw_rows"), k + 1)
                dve.wait_ge(sem("m_mul"), k + 1)
                tt(hid1[:, k % 2, :], hid1[:, k % 2, :], cw_rows[:, half * HALF:(half + 1) * HALF], ALU.mult
                   ).then_inc(sem("m_hid"), 1)
                if k:
                    low_part(k - 1)
            low_part(2 * FCH - 1)
            dve.wait_ge(sem("ln4_t"), 4)
            for i in range(NT):
                dve.wait_ge(sem("fin5"), i // 2 * 2 + 2)
                stt(x_tok[:, i, :], x_tok[:, i, :], 1.0,
                    bank[4 + i // 2][:, (i % 2) * D:(i % 2 + 1) * D], ALU.mult, ALU.add
                    ).then_inc(sem("ln5_r"), 1)
            for i in range(NT):
                dve.wait_ge(sem("ln5_r"), i + 1)
                link(dve.bn_stats(stats[:, i, :], x_tok[:, i, :]))
                dve.bn_aggr(meanvar[:, i, :], stats[:, i, :]).then_inc(sem("ln5_v"), 1)
            for i in range(NT):
                dve.wait_ge(sem("ln5_v"), i + 1)
                dve.wait_ge(sem("ln5_rstd"), i // 4 + 1)
                ts(x_tok[:, i, :], x_tok[:, i, :], meanvar[:, i, 0:1], rstd[:, i:i + 1],
                   ALU.subtract, ALU.mult).then_inc(sem("ln5_x"), 1)

        @block.scalar
        def _(act):
            af = act.activation

            def ln_out(k, half):
                for q in (2 * half, 2 * half + 1):
                    act.wait_ge(sem(f"ln{k}_t"), q + 1)
                    src = bank[4 + q % 2][:, :].rearrange("p (i c t) -> p i c t", i=2, c=2)
                    dst = xT[:, :, q * 2 * P:(q + 1) * 2 * P].rearrange("p c (i t) -> p i c t", i=2)
                    af(dst, src, ACT.Copy).then_inc(sem(f"ln{k}_xT"), 1)

            def attention(n, causal_keys, ring, out_of, extra=None):
                U = 2 * B * NPAIR
                for u in range(U + LAG[n] + 3 + 2 * AT_ONCE[n]):
                    v = u - LAG[n] - 1
                    if 0 <= v < U and v % 2 == 0:
                        copy_probs(act, n, v, causal_keys, lambda o, i: af(o, i, ACT.Copy), "a")
                    if u < U:
                        keys = (u % 2 + 1) * P if causal_keys else 256
                        act.wait_ge(sem(n + "max"), u + 1)
                        if u >= RING[n]:
                            act.wait_ge(sem(n + "tr"), u - RING[n] + 1)
                            act.wait_ge(sem(n + "rec"), u - RING[n] + 1)
                        for j in range(2):
                            last = af(probs_slot(n, u)[:, j, 0:keys],
                                      bank[ring[u % len(ring)]][:, j * 256:j * 256 + keys], ACT.Exp,
                                      bias=neg_max[:, u % RING[n], j:j + 1],
                                      accum_out=row_sum[:, u % RING[n], j:j + 1])
                        last.then_inc(sem(n + "exp"), 1)
                    G = group_at(n, u - LAG[n] - 2 - 2 * AT_ONCE[n])
                    if G is not None:
                        act.wait_ge(sem(n + "av"), G + 1)
                        dst, src = out_of(G)
                        af(dst, src, ACT.Copy).then_inc(sem(n + "oT"), 1)
                    if extra:
                        extra(u)

            loaded(act, "decay")
            af(decay[:, :, :], decay[:, :, :], ACT.Sigmoid).then_inc(sem("decayed"), 1)
            act.wait_ge(sem("zeroed"), 1)
            for i in range(NT):
                act.wait_ge(sem("v"), i + 1)
                af(v_pad[:, i, :].rearrange("p (h w) -> p h w", w=PAD)[:, :, 0:HD0],
                   bank[4 + i % 2][:, 0:D].rearrange("p (h w) -> p h w", w=HD0), ACT.Copy
                   ).then_inc(sem("v_out"), 1)

            def out_of0(G):
                b, p = G // 4, 2 * (G % 4)
                r, c = PAD * (p % 4), 2 * (p // 4)
                return (oT[r:r + 2 * PAD, c:c + 2, b * S:(b + 1) * S],
                        bank[(4, 6)[G % 2]][r:r + 2 * PAD, :].rearrange("p (j q) -> p j q", j=2))

            attention("a0_", True, (0, 1, 5), out_of0)
            ln_out(0, 0)

            for k in range(16):
                if k == 8:
                    ln_out(0, 1)
                act.wait_ge(sem("r_up"), k + 1)
                if k >= 4:
                    act.wait_ge(sem("r_mul"), k - 3)
                af(silu0[:, k % 4, :], bank[k % 4][:, :], ACT.Silu).then_inc(sem("r_silu"), 1)
            ln_out(1, 0)

            loaded(act, "vecs")
            for k in range(4):
                c, half = k % 2, k // 2
                if k == 2:
                    ln_out(1, 1)
                act.wait_ge(sem("f_h"), k + 1)
                af(h1T[:, c, half * HALF:(half + 1) * HALF], bank[c][:, :], ACT.Relu,
                   bias=vecs[:, 0, c:c + 1]).then_inc(sem("f_hT"), 1)
            act.wait_ge(sem("f_sub"), 1)
            af(small[:, 1, 0:64], small[:, 0, 0:64], ACT.Exp).then_inc(sem("f_e"), 1)
            for f in range(6):
                act.wait_ge(sem("fold"), f + 1)
                o = bank[6 + f % 2]
                if f < 2:
                    af(qk_fold[:, 4 * f:4 * f + 4, :], o[0:QC, :].rearrange("p (a b) -> p a b", a=4),
                       ACT.Copy, scale=MLA_SCALE).then_inc(sem("fold_out"), 1)
                else:
                    af(vo_fold[:, 2 * f - 4:2 * f - 2, :], o[:, :].rearrange("p (a b) -> p a b", a=2),
                       ACT.Copy).then_inc(sem("fold_out"), 1)
            for k in range(8):
                act.wait_ge(sem("f_bc"), k + 1)
                if k >= 2:
                    act.wait_ge(sem("f_vx"), k - 1)
                af(bc_s[:, k % 2, :], bank[6 + k % 2][:, :], ACT.Copy).then_inc(sem("f_bc_s"), 1)
            ln_out(2, 0)

            for k in range(4):
                c, half = k % 2, k // 2
                if k == 2:
                    ln_out(2, 1)
                act.wait_ge(sem("s_xp"), k + 1)
                af(xpT[:, c, half * HALF:(half + 1) * HALF], bank[k][:, :], ACT.Identity,
                   bias=vecs[:, 1, c:c + 1]).then_inc(sem("s_xpT"), 1)
            act.wait_ge(sem("s_pre"), 1)
            pre = bank[4][:, 0:P]
            af(small[:, 0, :], pre, ACT.Abs).then_inc(sem("s_sp"), 1)
            af(small[:, 2, :], pre, ACT.Relu)
            act.wait_ge(sem("s_sp"), 1)
            af(small[:, 0, :], small[:, 0, :], ACT.Exp, scale=-1.0).then_inc(sem("s_sp"), 1)
            act.wait_ge(sem("s_sp"), 2)
            af(small[:, 1, :], small[:, 0, :], ACT.Ln, bias=1.0).then_inc(sem("s_soft"), 1)
            act.wait_ge(sem("s_piecesT"), 1)
            for k in range(2):
                af(piecesT[:, k * HALF:(k + 1) * HALF], bank[k][0:48, :], ACT.Copy
                   ).then_inc(sem("s_piecesB"), 1)
            for r in range(2 * ST):
                s, half = r // 2, r % 2
                act.wait_ge(sem("s_bc"), r + 1)
                if s >= 4 and half == 0:
                    act.wait_ge(sem("s_u1"), s - 3)
                    act.wait_ge(sem("s_scan"), 2 * (s // 4) - 1)
                af(dl[:, s % 4, half * HALF:(half + 1) * HALF], bank[r % 4][:, :], ACT.Copy
                   ).then_inc(sem("s_bc_s"), 1)
            act.wait_ge(sem("s_z"), 8)
            for half in range(2):
                af(zT[:, half * HALF:(half + 1) * HALF], bank[6 + half][:, :], ACT.Copy
                   ).then_inc(sem("s_zT"), 1)

            ln_out(3, 0)
            for half in range(2):
                hh = slice(half * HALF, (half + 1) * HALF)
                act.wait_ge(sem("k_lat"), half + 1)
                af(keys_b[0:64, hh], bank[half][0:64, :], ACT.Copy).then_inc(sem("k_latT"), 1)
                af(keys_a[64:128, hh], bank[half][64:128, :], ACT.Copy).then_inc(sem("k_latT"), 1)
            act.wait_ge(sem("k_tok"), 1)
            af(kv_tok, bank[2][:, :].rearrange("p (i c) -> p i c", i=NT), ACT.Copy).then_inc(sem("k_tokT"), 1)
            ln_out(3, 1)
            for half in range(2):
                act.wait_ge(sem("qc"), half + 1)
                af(qcT[:, half * HALF:(half + 1) * HALF], bank[half][0:QC, :], ACT.Copy).then_inc(sem("qcT"), 1)

            def latent_pair(n):
                lat = q_banks(n)[1]
                at = NH * (n // NPAIR % 2) + 2 * (n % NPAIR)
                act.wait_ge(sem("q_l"), n + 1)
                af(qm[0:64, at + 1, :], lat[0:64, 0:S], ACT.Copy)
                af(qm[64:128, at, :], lat[64:128, 0:S], ACT.Copy).then_inc(sem("q_lat"), 1)

            def latent_next(u):
                if next_pair(u):
                    latent_pair(next_pair(u))

            def out_of4(g):
                b, p = g // 8, g % 8
                return om[:, p, b * S:(b + 1) * S], bank[(4, 6)[g % 2]][:, 0:S]

            for n in range(NPAIR):
                latent_pair(n)
            attention("a4_", False, (0, 1), out_of4, latent_next)
            for half in range(2):
                ln_out(4, half)
                act.wait_ge(sem("ln4_xT"), 2 * half + 2)
                hh = slice(half * HALF, (half + 1) * HALF)
                af(x_parts[:, 0, :, hh], xT[:, :, hh], ACT.Copy).then_inc(sem("x_hi"), 1)

            act.wait_ge(sem("m_sub"), 1)
            af(small[:, 1, :], small[:, 0, :], ACT.Exp).then_inc(sem("m_e"), 1)

            def silu(k):
                act.wait_ge(sem("m_g"), k + 1)
                if k >= 2:
                    act.wait_ge(sem("m_mul"), k - 1)
                af(silu1[:, k % 2, :], bank[k % 2][:, :], ACT.Silu).then_inc(sem("m_silu"), 1)

            def high_part(k):
                act.wait_ge(sem("m_hid"), k + 1)
                if k >= HID:
                    act.wait_ge(sem("m_down"), k - HID + 1)
                af(hid_parts[:, k % HID, 0, :], hid1[:, k % 2, :], ACT.Copy).then_inc(sem("m_hi"), 1)

            silu(0)
            silu(1)
            act.wait_ge(sem("m_piecesT"), 1)
            for half in range(2):
                af(piecesT[:, half * HALF:(half + 1) * HALF], bank[4 + half][0:48, :], ACT.Copy
                   ).then_inc(sem("m_piecesB"), 1)
            for half in range(2):
                act.wait_ge(sem("m_cw"), half + 1)
                af(cw_rows[:, half * HALF:(half + 1) * HALF], bank[6 + half][:, :], ACT.Copy
                   ).then_inc(sem("cw_rows"), 1)
            for k in range(2 * FCH):
                high_part(k)
                if k + 2 < 2 * FCH:
                    silu(k + 2)

        @block.gpsimd
        def _(pool):
            step = [0]

            def link(ins):
                step[0] += 1
                ins.then_inc(sem("pool_chain"), 1)
                pool.wait_ge(sem("pool_chain"), step[0])

            def rstd_of(k):
                for half in range(2):
                    s = slice(4 * half, 4 * half + 4)
                    pool.wait_ge(sem(f"ln{k}_v"), 4 * half + 4)
                    link(pool.tensor_scalar(veps[:, s], meanvar[:, s, 1], EPS, 1.0, ALU.add, ALU.mult))
                    pool.tensor_tensor(rstd[:, s], veps[:, s], minus_half[:, s], ALU.pow
                                       ).then_inc(sem(f"ln{k}_rstd"), 1)

            def attention(n, causal_keys, extra=None):
                for u in range(2 * B * NPAIR):
                    if extra:
                        extra(u)
                    keys = (u % 2 + 1) * P if causal_keys else 256
                    pool.wait_ge(sem(n + "rec"), u + 1)
                    for j in range(2):
                        pr = probs_slot(n, u)[:, j, 0:keys]
                        last = pool.tensor_scalar(pr, pr, row_rec[:, u % RING[n], j:j + 1], 1.0, ALU.mult, ALU.mult)
                    last.then_inc(sem(n + "norm"), 1)

            pool.memset(v_pad, 0.0).then_inc(sem("zeroed"), 1)
            link(pool.memset(minus_half[:, :], -0.5))
            for k in range(8):
                c, half = k // 2, k % 2
                hh = slice(half * HALF, (half + 1) * HALF)
                pool.wait_ge(sem("qkv_out"), 17 + k)
                pool.tensor_tensor(kT[:, c, hh], kT[:, c, hh], probs[:, k % 2].rearrange("p a b -> p (a b)"),
                                   ALU.add).then_inc(sem("kT"), 1)
            attention("a0_", True)
            rstd_of(0)
            pool.wait_ge(sem("emask"), 4)
            for k in range(16):
                half, e = k // 8, k // 2 % 4
                hh = slice(half * HALF, (half + 1) * HALF)
                pool.wait_ge(sem("r_mul"), k + 1)
                pool.tensor_tensor(hid0[:, k % 8, hh], hid0[:, k % 8, hh], emask[e][:, hh], ALU.mult
                                   ).then_inc(sem("r_hid"), 1)
            rstd_of(1)
            rstd_of(2)
            for g in range(1, 8, 2):
                for j in range(4):
                    s = 4 * (g // 2) + j
                    pool.wait_ge(sem("s_bc_s"), 2 * s + 2)
                    if g >= 3 and j == 0:
                        pool.wait_ge(sem("s_z"), g - 1)
                    pool.tensor_tensor(hs[:, 1, j, :], dl[:, j, :], xpT[:, 1, :], ALU.mult
                                       ).then_inc(sem("s_u1"), 1)
            rstd_of(3)

            def add_pair(n):
                at = NH * (n // NPAIR % 2) + 2 * (n % NPAIR)
                pool.wait_ge(sem("q_mul"), n + 1)
                link(pool.tensor_tensor(qm[0:64, at, :], ropes[0:64, n % 2, 0:S],
                                        ropes[0:64, n % 2, S:2 * S], ALU.add))
                pool.tensor_tensor(qm[64:128, at + 1, :], ropes[64:128, n % 2, 0:S],
                                   ropes[64:128, n % 2, S:2 * S], ALU.add).then_inc(sem("q_add"), 1)
                pool.wait_ge(sem("q_add"), n + 1)

            def add_next(u):
                if next_pair(u):
                    pool.wait_ge(sem("a4_norm"), u)
                    add_pair(next_pair(u))

            for n in range(NPAIR):
                add_pair(n)
            attention("a4_", False, add_next)
            rstd_of(4)

            def split_weights(c):
                w = raw[c % RAW]
                pool.wait_ge(sem(f"ld_raw{c % RAW}"), 16 * (c // RAW + 1))
                for words, parts, r in ((slice(0, GU), gu_parts, c % 2), (slice(GU, GU + DN), down_parts, c % 3)):
                    if parts is gu_parts and c >= 2:
                        pool.wait_ge(sem("m_u"), 2 * c - 2)
                    if parts is down_parts and c >= 3:
                        pool.wait_ge(sem("m_down"), 2 * c - 4)
                    link(pool.tensor_copy(parts[:, r, 0, :], w[:, words]))
                    last = pool.tensor_tensor(parts[:, r, 1, :], w[:, words], parts[:, r, 0, :].bitcast(f32),
                                              ALU.subtract)
                last.then_inc(sem("m_w"), 1)

            split_weights(0)
            for half in range(2):
                hh = slice(half * HALF, (half + 1) * HALF)
                pool.wait_ge(sem("x_hi"), half + 1)
                pool.tensor_tensor(x_parts[:, 1, :, hh], xT[:, :, hh], x_parts[:, 0, :, hh].bitcast(f32),
                                   ALU.subtract).then_inc(sem("x_lo"), 1)
            for c in range(1, FCH):
                split_weights(c)
            rstd_of(5)


def laid_out(x):
    import numpy as np

    f = np.float32
    a = {k: np.asarray(v) for k, v in x.items()}
    o = {}

    def chunks(w):
        return w.reshape(-1, 128, w.shape[-1]).transpose(1, 0, 2)

    X = a["x"].reshape(1024, 256)
    o["x_tok"] = chunks(X)
    o["xT"] = chunks(X.T)
    head = np.arange(16)[:, None] * 16
    j = np.arange(16)[None, :]
    plain, swapped = head + j, head + (j + 8) % 16
    both = lambda l, r: np.concatenate([l, r], axis=1).ravel()
    o["wq"] = chunks(a["L0_attn_Wq"].T[:, both(plain, swapped)])
    o["wk_raw"] = chunks(a["L0_attn_Wk"].T[:, both(plain, plain)])
    o["wk_swp"] = chunks(a["L0_attn_Wk"].T[:, both(swapped, swapped)])
    o["wv"] = chunks(a["L0_attn_Wv"].T)
    wo = np.zeros((16, 32, 256), f)
    wo[:, :16] = a["L0_attn_Wo"].T.reshape(16, 16, 256)
    o["wo_pad"] = chunks(wo.reshape(512, 256))
    fr = np.arange(256, dtype=f)[:, None] * (1.0 / 10000.0 ** (np.arange(0, 16, 2, dtype=f) / 16)).astype(f)
    emb = np.concatenate([fr, fr], axis=-1)
    cos, sin = np.cos(emb).T.astype(f), np.sin(emb).T.astype(f)
    sgn = np.where(np.arange(16) < 8, -1, 1).astype(f)[:, None] * sin
    o["tab_q"] = np.tile(np.concatenate([cos, sgn]), (4, 1)) * f(0.25)
    o["tab_c"] = np.tile(cos, (8, 1))
    o["tab_s"] = np.tile(sgn, (8, 1))
    o["ident"] = np.eye(128, dtype=f)
    neg = -(np.array([1e30], f).view(np.uint32) & np.uint32(0xFFFF0000)).view(f)[0]
    k = np.arange(128)
    o["causal"] = np.where(k[None, :] > k[:, None], neg, 0).astype(f)
    o["tid"] = a["itok_BxS_13_99985"].reshape(1024).astype(np.int32)
    o["w_uqT"] = a["L1_xattn_W_uq"].reshape(96, 16, 128).transpose(2, 1, 0)
    o["w_ukT"] = a["L1_xattn_W_uk"].reshape(64, 16, 128).transpose(2, 1, 0)
    o["w_uvT"] = a["L1_xattn_W_uv"].reshape(64, 16, 128).transpose(2, 1, 0)
    o["w_o"] = a["L1_xattn_W_o"].reshape(16, 128, 256).transpose(1, 0, 2)
    o["ctxT"] = a["ctx_2048"].transpose(2, 0, 1).reshape(2, 128, 4, 256).transpose(1, 2, 0, 3)
    o["w1"] = chunks(a["L0_ffn_W1"])
    o["vT"] = chunks(a["L0_ffn_V"].reshape(512, 256).T)
    o["uw"] = chunks(a["L0_ffn_U"].transpose(0, 2, 1).reshape(512, 256))
    o["w2s"] = chunks(a["L0_ffn_W2"])
    vecs = np.zeros((128, 8, 2), f)
    vecs[:, 0] = a["L0_ffn_b1"].reshape(2, 128).T
    vecs[:, 1] = a["L1_attn_proj_in_b"].reshape(2, 128).T
    vecs[:, 2] = a["L1_attn_D_param"].reshape(2, 128).T
    o["vecs"] = vecs
    o["rows"] = np.concatenate([a["L0_ffn_b2"], a["L1_attn_proj_out_b"], np.ones(128, f)])[None]
    o["decay"] = chunks(a["L1_attn_A"])
    o["pinT"] = chunks(a["L1_attn_proj_in_w"].T)
    o["poutT"] = chunks(a["L1_attn_proj_out_w"].T)
    o["wBT"] = chunks(a["L1_attn_B_w"].T)
    cw = np.zeros((4, 32, 256), f)
    cw[:, :4] = a["L1_attn_C_w"].T.reshape(4, 4, 256).transpose(1, 0, 2)
    o["CwP"] = cw.reshape(128, 2, 128)
    onesel = np.zeros((128, 4, 32), f)
    for q in range(4):
        onesel[:, q, q] = 1
    o["onesel"] = onesel
    o["e16"] = np.tile(np.eye(16, dtype=f), (3, 1)).astype(np.uint16) * np.uint16(0x3F80)
    o["sel_e"] = np.tile(np.repeat(np.eye(16, dtype=f), 8, axis=1), (3, 1)).astype(np.uint16) * np.uint16(0x3F80)
    o["seg"] = a["itok_BxS_0_1023"].reshape(8, 128).T.astype(np.int32)
    o["wgateT"] = chunks(a["L1_ffn_gate_w"].T)
    r = np.arange(64)
    swp = (r + 32) % 64
    wqr = a["L1_xattn_W_qr"].reshape(96, 16, 64)
    o["wqr_raw"] = wqr.reshape(96, 8, 128)
    o["wqr_swp"] = wqr[:, :, swp].reshape(96, 8, 128)
    o["w_dq"] = chunks(a["L1_xattn_W_dq"])
    o["w_kvc"] = chunks(np.tile(a["L1_xattn_W_kvc"], (1, 2)))
    kr = a["L1_xattn_W_kr"]
    o["w_kr"] = np.stack([np.tile(kr, (1, 2)), np.tile(kr[:, swp], (1, 2))], axis=1)
    inv = (1.0 / 10000.0 ** (np.arange(32, dtype=f) / 32)).astype(f)
    ang = np.arange(256, dtype=f)[:, None] * inv
    c, s = np.cos(ang).T.astype(f), np.sin(ang).T.astype(f)
    o["tab_kc"] = np.concatenate([c, c, c, c])
    o["tab_ks"] = np.concatenate([-s, s, -s, s])
    scale = f(192 ** -0.5)
    o["tab_qc"] = o["tab_kc"] * scale
    o["tab_qs"] = o["tab_ks"] * scale
    o["iota4"] = np.tile(np.arange(256, dtype=f) + 4, (128, 1))
    o["reset"] = np.tile((np.arange(128) % 16 != 0).astype(f), (128, 1))


    def by_chunk(w):
        return w.reshape(16, 22, 8, 256).transpose(1, 0, 2, 3).reshape(22, 128, 256)

    def transposed(w):
        return by_chunk(w).reshape(22, 128, 2, 128).transpose(0, 3, 2, 1).reshape(22, 128, 256)

    o["experts"] = np.concatenate([transposed(a["L1_ffn_w_gate"]), transposed(a["L1_ffn_w_up"]),
                                   by_chunk(a["L1_ffn_w_down"].transpose(0, 2, 1))], axis=2)
    return {k: np.ascontiguousarray(v) for k, v in o.items()}


def kernel(**inputs):
    import concourse.bacc as bacc
    from concourse import mybir
    from concourse.bass_utils import run_bass_kernel_spmd

    arrays = laid_out(inputs)
    nc = bacc.Bacc("TRN2", target_bir_lowering=False, num_devices=1)
    d = {k: nc.dram_tensor("in_" + k, v.shape, mybir.dt.from_np(v.dtype), kind="ExternalInput").ap()
         for k, v in arrays.items()}
    out = nc.dram_tensor("out", (8, 128, 256), mybir.dt.float32, kind="ExternalOutput").ap()
    build(nc, d, out)
    r = run_bass_kernel_spmd(nc, [{"in_" + k: v for k, v in arrays.items()}], core_ids=[0])
    return r.results[0]["out"].reshape(4, 256, 256)
```

```python
def build(nc, d, out):
    import numpy as np
    from concourse import mybir
    from contextlib import ExitStack

    f32, f32r, bf16 = mybir.dt.float32, mybir.dt.float32r, mybir.dt.bfloat16
    i32, u16 = mybir.dt.int32, mybir.dt.uint16
    ALU = mybir.AluOpType
    ACT = mybir.ActivationFunctionType
    AX = mybir.AxisListType.X

    B, S, D = 4, 256, 256
    P = 128
    T = B * S
    NT = T // P
    DC = D // P
    HALF = 512
    NH = 16
    NPAIR = NH // 2
    PAD = 32
    HD0 = 16
    EPS = 1e-5
    QC, KVC = 96, 64
    MLA_SCALE = float((128 + 64) ** -0.5)
    ST = 16
    NE, FF = 16, 176
    FCH = NE * FF // P
    TOPK = 6
    GU, DN = 2 * DC * P, D
    RAW, HID = 4, 3
    NEG = -float(np.frombuffer(np.uint32(np.float32(1e30).view(np.uint32) & 0xFFFF0000).tobytes(), np.float32)[0])
    LATQ = 5
    KROPE = (3, 0, 1, 2)
    LAG = {"a0_": 3, "a4_": 4}
    RING = {"a0_": 5, "a4_": 5}
    SUMS = {"a0_": 1, "a4_": 1}
    E0, F0 = 4, 256
    PER_EXPERT = 12500 // E0

    ctx = ExitStack()
    with ctx:
        def sb(name, shape, dt=f32):
            return ctx.enter_context(nc.sbuf_tensor(name, shape, dt))

        sems = {}

        def sem(name):
            if name not in sems:
                sems[name] = ctx.enter_context(nc.semaphore(name))
            return sems[name]

        x_tok = sb("x_tok", [P, NT, D])
        xT = sb("xT", [P, DC, T])
        A = sb("A", [P, 16384])
        parts = sb("parts", [P, 10752], f32r)
        C = sb("C", [P, 8192])
        ctxT = sb("ctxT", [P, B, DC, 256])
        probs = sb("probs", [P, 5, 2, 256])
        probsT = sb("probsT", [P, 2, 2, 2, 256])
        ident = sb("ident", [P, P])
        ident_b = sb("ident_b", [P, P], bf16)
        qk_fold = sb("qk_fold", [QC, NPAIR, P])
        vo_fold = sb("vo_fold", [P, NPAIR, D])
        probsT_more = vo_fold[:, :, :].rearrange("p (r k j) q -> p r k j q", r=2, k=2)
        neg_max = sb("neg_max", [P, 6, 2])
        row_sum = sb("row_sum", [P, 6, 2])
        row_rec = sb("row_rec", [P, 6, 2])
        stats = sb("stats", [P, NT, 6])
        meanvar = sb("meanvar", [P, NT, 2])
        veps = sb("veps", [P, NT])
        rstd = sb("rstd", [P, NT])
        minus_half = sb("minus_half", [P, NT])
        vecs = sb("vecs", [P, 8, 2])
        rows = sb("rows", [1, 8 + 256 + 128])
        small = sb("small", [P, 12, 128])
        small_b = sb("small_b", [P, 128], bf16)
        decay = sb("decay", [P, DC, ST])
        wBT = sb("wBT", [P, DC, ST])
        wgateT = sb("wgateT", [P, DC, NE])
        w2s = sb("w2s", [P, DC, 8])
        pieces = sb("pieces", [P, NT, 48])
        onesel = sb("onesel", [P, 4, 32])
        piecesT = sb("piecesT", [48, T], bf16)
        sel_e = sb("sel_e", [48, P], bf16)
        seg_i = sb("seg_i", [P, NT], i32)
        seg_f = sb("seg_f", [P, NT])
        top8 = sb("top8", [P, NT, 8])
        bank = [ctx.enter_context(nc.psum_tensor(f"bank{i}", [P, 512], f32)) for i in range(8)]

        def view(t, at, shape, dt=None):
            n = 1
            for k in shape[1:]:
                n *= k
            v = t[0:shape[0], at:at + n]
            if len(shape) == 3:
                v = v.rearrange("p (a b) -> p a b", a=shape[1])
            if len(shape) == 4:
                v = v.rearrange("p (a b c) -> p a b c", a=shape[1], b=shape[2])
            return v

        ctx_flat = ctxT[:, :, :, :].rearrange("p b c t -> p (b c t)")
        mask_m = ctx_flat[:, 0:1024].bitcast(bf16).rearrange("p (i k) -> p i k", i=NT)
        tab_qc = ctx_flat[:, 1024:1280]
        tab_qs = ctx_flat[:, 1280:1536]
        reset = ctx_flat[:, 1536:1664]
        distance = ctx_flat[:, 1664:1920]
        qT = view(A, 0, [P, 4, T])
        kT = view(A, 4096, [P, 4, T])
        v_pad = view(A, 8192, [P, NT, NH * PAD])
        oT = view(A, 12288, [P, 4, T])
        wq = view(C, 0, [P, DC, 512])
        wk_raw = view(C, 1024, [P, DC, 512])
        wk_swp = view(C, 2048, [P, DC, 512])
        wv = view(C, 3072, [P, DC, D])
        wo_pad = view(C, 3584, [P, 4, D])
        tab_q = view(C, 4608, [P, S])
        tab_c = view(C, 4864, [P, S])
        tab_s = view(C, 5120, [P, S])
        w1 = view(C, 5376, [P, DC, D])
        vT = view(C, 5888, [P, DC, 512])
        uw = view(C, 6912, [P, 4, D])
        causal = sb("causal", [P, P])
        causal_b = sb("causal_b", [P, P], bf16)
        w_uqT = view(A, 8192, [P, NH, QC])
        w_ukT = view(A, 9728, [P, NH, KVC])
        w_uvT = view(A, 10752, [P, NH, KVC])
        w_o = view(A, 11776, [P, NH, D])
        tid_f = view(C, 0, [P, T])
        emask = [view(C, 1024 + 512 * e, [P, 512]).bitcast(bf16) for e in range(E0)]
        tid_i = probsT[:, 0].rearrange("p a b c -> p (a b c)").bitcast(i32)
        lt_tmp = probsT[:, 1].rearrange("p a b c -> p (a b c)")
        pinT = view(C, 0, [P, DC, D])
        poutT = view(C, 512, [P, DC, D])
        CwP = view(C, 1024, [P, DC, P])
        hid0 = view(A, 0, [P, 8, T])
        silu0 = probs[:, 0:4].rearrange("p r a b -> p r (a b)")
        h1T = view(A, 0, [P, DC, T])
        bc_s = view(A, 2048, [P, 2, HALF])
        vxa = view(A, 4096, [P, 4, T])
        xpT = view(A, 0, [P, DC, T])
        x_p = view(A, 2048, [P, NT, D])
        scaled = view(A, 4096, [P, 4, 1024]).rearrange("p r (i d) -> p r i d", i=4)
        hs = view(A, 8192, [P, 2, 4096]).rearrange("p h (c j t) -> p h c j t", c=DC, j=4)
        zT = probs[:, 0:2].rearrange("p a b c -> p (a b c)")
        qm = view(A, 0, [P, 2 * NH, S])
        om = view(A, 8192, [P, NPAIR, T])
        keys_a = view(C, 0, [P, T])
        keys_b = view(C, 1024, [P, T])
        kv_tok = view(C, 2048, [P, NT, KVC])
        wqr_raw = view(C, 3584, [QC, NPAIR, P])
        wqr_swp = view(C, 4608, [QC, NPAIR, P])
        w_dq = view(C, 5632, [P, DC, QC])
        w_kvc = view(C, 5824, [P, DC, P])
        w_kr = view(C, 6080, [KVC, 2, P])
        tab_kc = view(C, 6336, [P, S])
        tab_ks = view(C, 6592, [P, S])
        iota4 = view(C, 6848, [P, 256])
        ropes = view(C, 7104, [P, 2, 512])
        wqr_raw_parts = view(parts, 0, [QC, 2, NPAIR, P])
        wqr_swp_parts = view(parts, 2048, [QC, 2, NPAIR, P])
        qk_parts = view(parts, 4096, [QC, 2, NPAIR, P])
        qc_parts = view(parts, 6144, [QC, 2, T])
        x0_parts = view(parts, 6144, [P, 2, DC, T])
        qkv_parts = [view(parts, 2048 * w, [P, 2, DC, 512]) for w in range(3)]
        SPLIT0 = ([("wq", wq, qkv_parts[0])]
                  + [(f"xT{h}", xT[:, :, h * HALF:(h + 1) * HALF], x0_parts[:, :, :, h * HALF:(h + 1) * HALF])
                     for h in range(2)]
                  + [("wk_raw", wk_raw, qkv_parts[1]), ("wk_swp", wk_swp, qkv_parts[2])])
        QC_AT, X_AT = len(SPLIT0), len(SPLIT0) + 2
        x_parts = view(parts, 0, [P, 2, DC, T])
        gu_parts = view(parts, 4096, [P, 2, 2, GU])
        down_parts = view(parts, 6144, [P, 3, 2, DN])
        hid_parts = view(parts, 7680, [P, HID, 2, HALF])
        cw_rows = view(A, 0, [P, T])
        silu1 = view(A, 1024, [P, 2, HALF])
        hid1 = view(A, 2048, [P, 2, HALF])
        raw = [view(C, (GU + DN) * r, [P, GU + DN]) for r in range(RAW)]

        def bc(ap, n, dim=1):
            v = ap.unsqueeze(dim)
            shape = list(v.shape)
            shape[dim] = n
            return v.broadcast_to(shape)

        LOADS = {
            "ld_first": ("wq", "tab_q"), "ld_keys": ("wk_raw", "wk_swp", "tab_c", "tab_s", "wv"),
            "ld_const": ("ident", "causal", "x_tok", "tid", "decay"),
            "ld_out": ("wo_pad",), "ld_fold": ("w_uqT", "w_ukT", "w_uvT", "w_o"), "ld_ctx": ("ctxT",),
            "ld_ffn": ("w1", "vT", "uw", "w2s", "vecs", "rows", "wBT", "onesel", "seg", "wgateT", "sel_e"),
            "ld_scan": ("pinT", "poutT", "CwP"),
            "ld_latent": ("wqr_raw", "wqr_swp", "w_dq", "w_kvc", "w_kr", "tab_kc", "tab_ks", "iota4"),
            "ld_tabs": ("tab_qc", "tab_qs", "reset"),
        }
        GROUP = {name: g for g, names in LOADS.items() for name in names}

        def loaded(eng, *names):
            for g in sorted({GROUP[n] for n in names}):
                eng.wait_ge(sem(g), 16 * len(LOADS[g]))

        def scan_unit(n):
            q, half, j = n // 8, n // 4 % 2, n % 4
            return q, half, j

        SCAN_UNITS = 2 * ST

        def scale_tokens(eng, n, tiles, scale_op, done):
            q, half, j = scan_unit(n)
            if n >= 4:
                eng.wait_ge(sem("s_uT"), 2 * (n - 3))
            for i in tiles:
                at = ST * (4 * half + i) + 4 * q + j
                last = scale_op(scaled[:, n % 4, i, :], x_p[:, 4 * half + i, :], small[:, 3, at:at + 1])
            last.then_inc(sem(done), 1)

        QKV = ([(0, c, half) for half in range(2) for c in range(4)]
               + [(w, c, half) for w in (1, 2) for c in range(4) for half in range(2)])
        AT_ONCE = {"a0_": 2, "a4_": 1}

        def pT_slot(n, g):
            g %= 2 * AT_ONCE[n]
            return probsT[:, g] if g < 2 else probsT_more[:, g - 2]

        def probs_slot(n, u):
            return probs[:, u % RING[n]]

        def copy_probs(eng, n, v, causal_keys, copy, which):
            g, kcs = v // 2, 1 + v % 2 if causal_keys else 2
            G = g // AT_ONCE[n]
            eng.wait_ge(sem(n + "tr"), v + 1)
            if G >= 2:
                eng.wait_ge(sem(n + "av"), G - 1)
            src = bank[2 + v % 2][:, 0:kcs * 256].rearrange("p (k j q) -> p k j q", k=kcs, j=2)
            copy(pT_slot(n, g)[:, 0:kcs, :, (v % 2) * P:(v % 2 + 1) * P], src
                 ).then_inc(sem(n + "pT" + which), 1)

        def group_at(n, step):
            G, r = divmod(step, 2 * AT_ONCE[n])
            return G if r == 0 and 0 <= G < B * NPAIR // AT_ONCE[n] else None

        FIRST = 3
        QUERIES_AT = {2 * (n - FIRST) + 1: n for n in range(FIRST, B * NPAIR)}

        def q_banks(n):
            return (bank[(7, 6)[n % 2]], bank[(LATQ, 4)[n % 2]]) if n < FIRST else (bank[7], bank[LATQ])

        block = ctx.enter_context(nc.Block())

        @block.sync
        def _(sp):
            def load(name, dst, src=None):
                sp.dma_start(dst, d[name] if src is None else src).then_inc(sem(GROUP[name]), 16)

            load("wq", wq)
            load("tab_q", tab_q)
            for half in range(2):
                hh = slice(half * HALF, (half + 1) * HALF)
                sp.dma_start(xT[:, :, hh], d["xT"][:, :, hh]).then_inc(sem(f"ld_xT{half}"), 16)
            load("wk_raw", wk_raw)
            load("wk_swp", wk_swp)
            load("tab_c", tab_c)
            load("tab_s", tab_s)
            load("wv", wv)
            load("ident", ident[:, :])
            load("causal", causal[:, :])
            load("decay", decay[:, :, :])
            load("x_tok", x_tok[:, :, :])
            load("tid", tid_i, d["tid"].partition_broadcast(P))
            load("wo_pad", wo_pad)
            load("ctxT", ctxT[:, :, :, :])
            load("w1", w1)
            load("vT", vT)
            load("uw", uw)
            load("w2s", w2s[:, :, :])
            load("vecs", vecs[:, :, :])
            load("rows", rows[:, :])
            load("wBT", wBT[:, :, :])
            load("onesel", onesel[:, :, :])
            load("seg", seg_i[:, :])
            load("wgateT", wgateT[:, :, :])
            load("sel_e", sel_e[:, :].bitcast(u16))
            sp.wait_ge(sem("fin0"), NT)
            load("w_uqT", w_uqT)
            load("w_ukT", w_ukT)
            load("w_uvT", w_uvT)
            load("w_o", w_o)
            sp.wait_ge(sem("fin1"), NT)
            load("pinT", pinT)
            load("poutT", poutT)
            load("CwP", CwP)
            sp.wait_ge(sem("fin2"), NT)
            load("wqr_raw", wqr_raw)
            load("wqr_swp", wqr_swp)
            load("w_dq", w_dq)
            load("w_kvc", w_kvc)
            load("w_kr", w_kr)
            load("tab_kc", tab_kc)
            load("tab_ks", tab_ks)
            load("iota4", iota4)
            sp.wait_ge(sem("fin3"), NT)
            sp.wait_ge(sem("k_tok"), 1)
            load("tab_qc", tab_qc)
            load("tab_qs", tab_qs)
            load("reset", reset)
            sp.wait_ge(sem("fin4"), 1)
            for c in range(FCH):
                if c >= RAW:
                    sp.wait_ge(sem("m_w"), c - RAW + 1)
                sp.dma_start(raw[c % RAW], d["experts"][c]).then_inc(sem(f"ld_raw{c % RAW}"), 16)
            for i in range(NT):
                sp.wait_ge(sem("ln5_x"), i + 1)
                sp.dma_start(out[i], x_tok[:, i, :]).then_inc(sem("stored"), 16)
            sp.wait_ge(sem("stored"), 16 * NT)

        @block.tensor
        def _(pe):
            mm = pe.matmul

            def product3(o, left, right, first, last):
                for n, (l, r) in enumerate(((0, 0), (1, 0), (0, 1))):
                    ins = mm(o, left[l], right[r], start=first and n == 0, stop=last and n == 2,
                             skip_group_check=True)
                return ins

            def ln_transposes(k, half):
                for q in (2 * half, 2 * half + 1):
                    pe.wait_ge(sem(f"ln{k}_x"), 2 * q + 2)
                    if q >= 2:
                        pe.wait_ge(sem(f"ln{k}_xT"), q - 1)
                    for j in range(2):
                        for c in range(DC):
                            o = (2 * j + c) * P
                            last = pe.transpose(bank[4 + q % 2][:, o:o + P],
                                                x_tok[:, 2 * q + j, c * P:(c + 1) * P], ident[:, :])
                    last.then_inc(sem(f"ln{k}_t"), 1)

            def final(k, tiles, emit):
                for i in tiles:
                    if i >= 2:
                        pe.wait_ge(sem(f"ln{k}_r"), i - 1)
                    emit(i, bank[6 + i % 2][:, 0:D]).then_inc(sem(f"fin{k}"), 1)

            def close(k, emit):
                final(k, range(7), emit)
                ln_transposes(k, 0)
                final(k, range(7, NT), emit)

            def proj(o, w, col, half, m=P):
                for c in range(DC):
                    last = mm(o, w[:, c, col:col + m], xT[:, c, half * HALF:(half + 1) * HALF],
                              start=(c == 0), stop=(c == DC - 1))
                return last

            def attention(n, scores, apply, causal_keys, ring, filler=None):
                U = 2 * B * NPAIR
                for u in range(U + LAG[n] + 2 + 2 * AT_ONCE[n]):
                    if u < U:
                        if u >= len(ring):
                            pe.wait_ge(sem(n + ("exp" if causal_keys else "masked")), u - len(ring) + 1)
                        scores(u, bank[ring[u % len(ring)]]).then_inc(sem(n + "sc"), 1)
                    if filler:
                        filler(u)
                    v = u - LAG[n]
                    if 0 <= v < U:
                        pe.wait_ge(sem(n + "norm"), v + 1)
                        if v >= 2:
                            pe.wait_ge(sem(n + "pT" + "ad"[v % 2]), v // 2)
                        for kc in range(1 + v % 2 if causal_keys else 2):
                            for j in range(2):
                                o = (2 * kc + j) * P
                                last = pe.transpose(bank[2 + v % 2][:, o:o + P],
                                                    probs_slot(n, v)[:, j, kc * P:(kc + 1) * P], ident[:, :])
                        last.then_inc(sem(n + "tr"), 1)
                    G = group_at(n, u - LAG[n] - 1 - 2 * AT_ONCE[n])
                    if G is not None:
                        pe.wait_ge(sem(n + "pTa"), AT_ONCE[n] * (G + 1))
                        pe.wait_ge(sem(n + "pTd"), AT_ONCE[n] * (G + 1))
                        if G >= 2:
                            pe.wait_ge(sem(n + "oT"), G - 1)
                        apply(G, bank[(4, 6)[G % 2]]).then_inc(sem(n + "av"), 1)

            for n, (w, c, half) in enumerate(QKV):
                if n in (0, 4, 8, 16):
                    pe.wait_ge(sem("operand_lo"), {0: 2, 4: 3, 8: 4, 16: 5}[n])
                if n >= 4:
                    pe.wait_ge(sem("qkv_out"), n - 3)
                hh = slice(half * HALF, (half + 1) * HALF)
                for dc in range(DC):
                    last = product3(bank[n % 4][:, :],
                                    [qkv_parts[w][:, r, dc, c * P:(c + 1) * P] for r in range(2)],
                                    [x0_parts[:, r, dc, hh] for r in range(2)], dc == 0, dc == DC - 1)
                last.then_inc(sem("qkv"), 1)
            loaded(pe, "wv")
            for i in range(NT):
                if i >= 2:
                    pe.wait_ge(sem("v_out"), i - 1)
                for c in range(DC):
                    last = mm(bank[4 + i % 2][:, 0:D], xT[:, c, i * P:(i + 1) * P], wv[:, c, :],
                              start=(c == 0), stop=(c == DC - 1))
                last.then_inc(sem("v"), 1)

            pe.wait_ge(sem("kT"), 8)
            pe.wait_ge(sem("qkv_out"), 24)
            pe.wait_ge(sem("v_out"), NT)
            pe.wait_ge(sem("const_b"), 2)
            loaded(pe, "ident")

            def scores0(u, o):
                b, p, qt = u // 16, u // 2 % 8, u % 2
                o3 = o[:, :].rearrange("p (j k) -> p j k", j=2)
                for j in range(2):
                    r, c = PAD * (p % 4), 2 * (p // 4) + j
                    mm(o3[:, j, 0:(qt + 1) * P], qT[r:r + PAD, c, b * S + qt * P:b * S + (qt + 1) * P],
                       kT[r:r + PAD, c, b * S:b * S + (qt + 1) * P],
                       start=(j == 0), stop=False, skip_group_check=True)
                return mm(o3[:, :, qt * P:(qt + 1) * P], ident_b[:, :], bc(causal_b[:, :], 2),
                          start=False, stop=True, skip_group_check=True)

            def apply0(G, o):
                b, p = G // 4, 2 * (G % 4)
                for j in range(2):
                    for kc in range(2):
                        for i in range(2):
                            r = PAD * ((p + i) % 4)
                            h = 4 * (2 * (p // 4) + j) + (p + i) % 4
                            last = mm(o[r:r + PAD, j * S + kc * P:(j + 1) * S],
                                      v_pad[:, 2 * b + kc, PAD * h:PAD * h + PAD],
                                      pT_slot("a0_", 2 * G + i)[:, kc, j, kc * P:S], start=(kc == 0),
                                      stop=(kc == 1), skip_group_check=True)
                return last

            def keep_clock(u):
                for _ in range(1 if u >= LAG["a0_"] + 2 else 3):
                    mm(bank[7][:, 0:256], ident_b[:, :], bc(ident_b[:, :], 2), start=True, stop=True)

            attention("a0_", scores0, apply0, True, (0, 1, 5), keep_clock)
            pe.wait_ge(sem("a0_oT"), B * NPAIR // 2)
            loaded(pe, "wo_pad")

            def out0(i, o):
                for c in range(4):
                    last = mm(o, oT[:, c, i * P:(i + 1) * P], wo_pad[:, c, :], start=(c == 0), stop=(c == 3))
                return last

            close(0, out0)

            loaded(pe, "ctxT")
            for k in range(16):
                half, e, fc = k // 8, k // 2 % 4, k % 2
                if k == 8:
                    ln_transposes(0, 1)
                pe.wait_ge(sem("ln0_xT"), 2 * (half + 1))
                if k >= 4:
                    pe.wait_ge(sem("r_mul"), k - 3)
                proj(bank[k % 4][:, :], ctxT[:, e], fc * P, half).then_inc(sem("r_up"), 1)

            def out1(i, o):
                pe.wait_ge(sem("r_hid"), 8 * (i // 4 + 1))
                for k in range(8):
                    last = mm(o, hid0[:, k, i * P:(i + 1) * P], ctxT[:, k // 2, k % 2, :],
                              start=(k == 0), stop=(k == 7))
                return last

            close(1, out1)

            loaded(pe, "w1", "w2s", "vT", "uw", "rows")

            def hidden(half):
                for c in range(DC):
                    k = 2 * half + c
                    pe.wait_ge(sem("ln1_xT"), 2 * (half + 1))
                    if half:
                        pe.wait_ge(sem("f_hT"), c + 1)
                    proj(bank[c][:, :], w1, c * P, half).then_inc(sem("f_h"), 1)

            def low_rank(k):
                if k in (2, 3):
                    pe.wait_ge(sem("f_hT"), k + 1)
                if k >= 4:
                    pe.wait_ge(sem("f_vx"), k - 3)
                proj(bank[(2 + k) % 4][:, :], vT, (k % 4) * P, k // 4).then_inc(sem("f_v"), 1)

            def mixing(k):
                c, half = k % 4, k // 4
                pe.wait_ge(sem("f_alpha"), 1)
                if k >= 2:
                    pe.wait_ge(sem("f_bc_s"), k - 1)
                for i in range(4):
                    for j in range(2):
                        at = 8 * (4 * half + i) + 2 * c + j
                        last = mm(bank[6 + k % 2][64 * j:64 * j + 64, i * P:(i + 1) * P],
                                  small[:, 5, at:at + 1].broadcast_to([P, 64]), ident[:, :],
                                  start=True, stop=True, skip_group_check=True)
                last.then_inc(sem("f_bc"), 1)

            def fold(f):
                o = bank[6 + f % 2]
                if f >= 2:
                    pe.wait_ge(sem("fold_out"), f - 1)
                for p in range(4 * f, 4 * f + 4) if f < 2 else range(2 * f - 4, 2 * f - 2):
                    for j in range(2):
                        h = 2 * p + j
                        if f < 2:
                            at = (p % 4) * P + (1 - j) * KVC
                            last = mm(o[0:QC, at:at + KVC], w_uqT[:, h, :], w_ukT[:, h, :],
                                      start=True, stop=True)
                        else:
                            last = mm(o[KVC * j:KVC * j + KVC, (p % 2) * D:(p % 2 + 1) * D],
                                      w_uvT[:, h, :], w_o[:, h, :], start=True, stop=True)
                last.then_inc(sem("fold"), 1)

            hidden(0)
            low_rank(0)
            low_rank(1)
            ln_transposes(1, 1)
            hidden(1)
            pe.wait_ge(sem("f_hT"), 4)
            for i in range(NT):
                o = bank[4][:, 8 * i:8 * i + 8]
                for c in range(DC):
                    mm(o, h1T[:, c, i * P:(i + 1) * P], w2s[:, c, :], start=(c == 0), stop=False)
                last = mm(o, rows[0:1, 264:264 + P], rows[0:1, 0:8], start=False, stop=True)
            last.then_inc(sem("f_lg"), 1)
            low_rank(2)
            low_rank(3)
            loaded(pe, "w_uqT", "w_ukT", "w_uvT", "w_o")
            for f in range(6):
                fold(f)
            pe.wait_ge(sem("fold_out"), 6)
            for k in range(8):
                mixing(k)
                if 1 <= k < 5:
                    low_rank(k + 3)

            def out2(i, o):
                pe.wait_ge(sem("f_vx"), 4 * (i // 4 + 1))
                pe.wait_ge(sem("f_bc_s"), 8)
                for c in range(4):
                    last = mm(o, vxa[:, c, i * P:(i + 1) * P], uw[:, c, :], start=(c == 0), stop=(c == 3))
                return last

            close(2, out2)

            loaded(pe, "pinT", "wBT", "CwP", "onesel", "poutT")
            for k in range(4):
                c, half = k % 2, k // 2
                if k == 2:
                    ln_transposes(2, 1)
                pe.wait_ge(sem("ln2_xT"), 2 * (half + 1))
                proj(bank[k][:, :], pinT, c * P, half).then_inc(sem("s_xp"), 1)
            pe.wait_ge(sem("s_xpT"), 4)
            for i in range(NT):
                for c in range(DC):
                    last = mm(bank[4][:, ST * i:ST * i + ST], xpT[:, c, i * P:(i + 1) * P], wBT[:, c, :],
                              start=(c == 0), stop=(c == DC - 1))
            last.then_inc(sem("s_pre"), 1)

            for k in range(4):
                for i in range(2):
                    for c in range(DC):
                        last = pe.transpose(bank[k][:, (2 * i + c) * P:(2 * i + c + 1) * P],
                                            xpT[:, c, (2 * k + i) * P:(2 * k + i + 1) * P], ident[:, :])
                last.then_inc(sem("s_xp_t"), 1)

            def transposes3(n):
                for name in ("s_scaled_a", "s_scaled_p"):
                    pe.wait_ge(sem(name), n + 1)
                for c in range(DC):
                    m = 2 * n + c
                    if m >= 6:
                        pe.wait_ge(sem("s_scan"), m - 5)
                    for i in range(4):
                        last = pe.transpose(bank[m % 6][:, i * P:(i + 1) * P],
                                            scaled[:, n % 4, i, c * P:(c + 1) * P], ident[:, :])
                    last.then_inc(sem("s_uT"), 1)

            def state_sums(G):
                q, half = G // 2, G % 2
                pe.wait_ge(sem("s_scan"), 8 * (G + 1))
                for c in range(DC):
                    for j in range(4):
                        last = mm(bank[6 + half][32 * j:32 * j + 32, :], onesel[:, q, :], hs[:, half, c, j, :],
                                  start=(q == 0 and c == 0), stop=(q == 3 and c == 1), skip_group_check=True)
                last.then_inc(sem("s_z"), 1)

            pe.wait_ge(sem("x_p"), 4)
            pe.wait_ge(sem("s_soft"), 1)
            for n in range(SCAN_UNITS + 2):
                if n < SCAN_UNITS:
                    transposes3(n)
                if n % 4 == 1 and n > 4:
                    state_sums(n // 4 - 1)
            pe.wait_ge(sem("s_zT"), 2)
            for k in range(4):
                c, half = k % 2, k // 2
                mm(bank[k][:, :], CwP[:, c, :], zT[:, half * HALF:(half + 1) * HALF],
                   start=True, stop=True).then_inc(sem("s_y"), 1)

            def out3(i, o):
                pe.wait_ge(sem("s_yT"), 2 * (i // 4 + 1))
                for c in range(DC):
                    mm(o, xpT[:, c, i * P:(i + 1) * P], poutT[:, c, :], start=(c == 0), stop=False)
                return mm(o, rows[0:1, 264:264 + P], rows[0:1, 8:264], start=False, stop=True)

            close(3, out3)

            loaded(pe, "w_kvc", "w_kr", "w_dq")
            for half in range(2):
                for c in range(DC):
                    last = mm(bank[half][:, :], w_kvc[:, c, :],
                              ctxT[:, 2 * half:2 * half + 2, c, :], start=(c == 0), stop=(c == DC - 1))
                last.then_inc(sem("k_lat"), 1)
            for i in range(NT):
                for c in range(DC):
                    last = mm(bank[2][:, KVC * i:KVC * i + KVC],
                              ctxT[:, i // 2, c, (i % 2) * P:(i % 2 + 1) * P], w_kvc[:, c, 0:KVC],
                              start=(c == 0), stop=(c == DC - 1))
            last.then_inc(sem("k_tok"), 1)
            for half in range(2):
                pe.wait_ge(sem("k_latT"), 2 * (half + 1))
                if half:
                    pe.wait_ge(sem("k_tokT"), 1)
                for r in range(2):
                    mm(bank[KROPE[2 * half + r]][:, :], w_kr[:, r, :],
                       keys_b[0:KVC, half * HALF:(half + 1) * HALF], start=True, stop=True
                       ).then_inc(sem("k_rope"), 1)
            ln_transposes(3, 1)
            pe.wait_ge(sem("k_mul"), 4)
            for half in range(2):
                pe.wait_ge(sem("ln3_xT"), 2 * (half + 1))
                for c in range(DC):
                    last = mm(bank[half][0:QC, :], w_dq[:, c, :], xT[:, c, half * HALF:(half + 1) * HALF],
                              start=(c == 0), stop=(c == DC - 1))
                last.then_inc(sem("qc"), 1)
            pe.wait_ge(sem("q_split"), 3)
            pe.wait_ge(sem("operand_lo"), QC_AT + 2)
            pe.wait_ge(sem("k_add"), 4)
            pe.wait_ge(sem("k_tokT"), 1)

            def query_pair(n):
                rhs = [qc_parts[:, r, n // NPAIR * S:(n // NPAIR + 1) * S] for r in range(2)]
                p = n % NPAIR
                rope, lat = q_banks(n)
                if n >= 2:
                    ahead = 1 if n >= FIRST else 2
                    pe.wait_ge(sem("q_mul"), n + 1 - ahead)
                    pe.wait_ge(sem("q_lat"), n + 1 - ahead)
                left = lambda w: [w[:, r, p, :] for r in range(2)]
                product3(rope[:, 0:S], left(wqr_raw_parts), rhs, True, True)
                product3(rope[:, S:2 * S], left(wqr_swp_parts), rhs, True, True).then_inc(sem("q_rope"), 1)
                product3(lat[:, 0:S], left(qk_parts), rhs, True, True).then_inc(sem("q_l"), 1)

            def next_queries(u):
                if u in QUERIES_AT:
                    query_pair(QUERIES_AT[u])

            def scores4(u, o):
                b, p, qt = u // 16, u // 2 % 8, u % 2
                if qt == 0:
                    pe.wait_ge(sem("q_add"), NPAIR * b + p + 1)
                    pe.wait_ge(sem("q_lat"), NPAIR * b + p + 1)
                o3 = o[:, :].rearrange("p (j k) -> p j k", j=2)
                for j in range(2):
                    last = mm(o3[:, j, :], qm[:, NH * (b % 2) + 2 * p + j, qt * P:(qt + 1) * P],
                              (keys_a, keys_b)[j][:, b * S:(b + 1) * S], start=True, stop=True,
                              skip_group_check=True)
                return last

            def apply4(g, o):
                b = g // 8
                for kc in range(2):
                    for j in range(2):
                        last = mm(o[KVC * j:KVC * j + KVC, 0:S], kv_tok[:, 2 * b + kc, :],
                                  probsT[:, g % 2, kc, j, :], start=(kc == 0), stop=(kc == 1),
                                  skip_group_check=True)
                return last

            for n in range(FIRST):
                query_pair(n)
            attention("a4_", scores4, apply4, False, (0, 1), next_queries)
            pe.wait_ge(sem("a4_oT"), B * NPAIR)

            def out4(i, o):
                for p in range(NPAIR):
                    last = mm(o, om[:, p, i * P:(i + 1) * P], vo_fold[:, p, :], start=(p == 0),
                              stop=(p == NPAIR - 1))
                return last

            close(4, out4)

            loaded(pe, "wgateT", "sel_e")

            def gate_up(k):
                c, half = k // 2, k % 2
                hh = slice(half * HALF, (half + 1) * HALF)
                pe.wait_ge(sem("m_w"), c + 1)
                if k >= 2:
                    pe.wait_ge(sem("m_silu"), k - 1)
                    pe.wait_ge(sem("m_mul"), k - 1)
                for w, name in enumerate(("m_g", "m_u")):
                    if k == 1 and w == 1:
                        pe.wait_ge(sem("m_sub"), 1)
                    for dc in range(DC):
                        at = (DC * w + dc) * P
                        last = product3(bank[2 * w + k % 2][:, :],
                                        [gu_parts[:, c % 2, r, at:at + P] for r in range(2)],
                                        [x_parts[:, r, dc, hh] for r in range(2)], dc == 0, dc == DC - 1)
                    last.then_inc(sem(name), 1)

            def down(k):
                c, half = k // 2, k % 2
                pe.wait_ge(sem("m_lo"), k + 1)
                for i in range(4):
                    last = product3(bank[4 + 2 * half + i // 2][:, (i % 2) * D:(i % 2 + 1) * D],
                                    [hid_parts[:, k % HID, r, i * P:(i + 1) * P] for r in range(2)],
                                    [down_parts[:, c % 3, r, :] for r in range(2)],
                                    c == 0 and i % 2 == 0, c == FCH - 1)
                    if c == FCH - 1:
                        last.then_inc(sem("fin5"), 1)
                if c < FCH - 1:
                    last.then_inc(sem("m_down"), 1)

            for half in range(2):
                if half:
                    ln_transposes(4, 1)
                pe.wait_ge(sem("ln4_xT"), 2 * half + 2)
                for i in range(4 * half, 4 * half + 4):
                    for c in range(DC):
                        last = mm(bank[3][:, NE * i:NE * i + NE], xT[:, c, i * P:(i + 1) * P], wgateT[:, c, :],
                                  start=(c == 0), stop=(c == DC - 1))
                if half:
                    last.then_inc(sem("m_lg"), 1)
                pe.wait_ge(sem("operand_lo"), X_AT + half + 1)
                gate_up(half)
            pe.wait_ge(sem("m_pieces"), 1)
            for i in range(NT):
                last = pe.transpose(bank[4 + i // 4][0:48, (i % 4) * P:(i % 4 + 1) * P],
                                    pieces[:, i, :], ident[:, :])
            last.then_inc(sem("m_piecesT"), 1)
            pe.wait_ge(sem("ln4_r"), NT)
            for half in range(2):
                pe.wait_ge(sem("m_piecesB"), half + 1)
                mm(bank[6 + half][:, :], sel_e[:, :], piecesT[:, half * HALF:(half + 1) * HALF],
                   start=True, stop=True).then_inc(sem("m_cw"), 1)
            for k in range(2, 2 * FCH + 2):
                if k < 2 * FCH:
                    gate_up(k)
                if k == 2:
                    pe.wait_ge(sem("cw_rows"), 2)
                down(k - 2)

        @block.vector
        def _(dve):
            tt, ts, stt, cp = dve.tensor_tensor, dve.tensor_scalar, dve.scalar_tensor_tensor, dve.tensor_copy
            chain = [0]

            def link(ins):
                chain[0] += 1
                ins.then_inc(sem("dve_chain"), 1)
                dve.wait_ge(sem("dve_chain"), chain[0])

            def norm(k, scale, place):

                def residual(i):
                    dve.wait_ge(sem(f"fin{k}"), i + 1)
                    if i == 0:
                        if k == 0:
                            loaded(dve, "x_tok")
                        else:
                            dve.wait_ge(sem(f"ln{k-1}_t"), 4)
                    stt(x_tok[:, i, :], x_tok[:, i, :], scale, place(i), ALU.mult, ALU.add
                        ).then_inc(sem(f"ln{k}_r"), 1)
                    dve.wait_ge(sem(f"ln{k}_r"), i + 1)
                    link(dve.bn_stats(stats[:, i, :], x_tok[:, i, :]))
                    dve.bn_aggr(meanvar[:, i, :], stats[:, i, :]).then_inc(sem(f"ln{k}_v"), 1)

                def normalise(i):
                    dve.wait_ge(sem(f"ln{k}_v"), i + 1)
                    dve.wait_ge(sem(f"ln{k}_rstd"), i // 4 + 1)
                    ts(x_tok[:, i, :], x_tok[:, i, :], meanvar[:, i, 0:1], rstd[:, i:i + 1],
                       ALU.subtract, ALU.mult).then_inc(sem(f"ln{k}_x"), 1)

                for i in range(6):
                    residual(i)
                for i in range(4):
                    normalise(i)
                for i in range(6, NT):
                    residual(i)
                for i in range(4, NT):
                    normalise(i)

            fin_bank = lambda i: bank[6 + i % 2][:, 0:D]

            def softmax_small(n, lg, w, e_row):
                sh = lambda r: small[:, r, 0:NT * w].rearrange("p (i w) -> p i w", w=w)
                col = small[:, 11, 0:NT]
                link(dve.tensor_reduce(col, lg, axis=AX, op=ALU.max, negate=True))
                tt(sh(0), lg, bc(col, w, 2), ALU.add).then_inc(sem(n + "sub"), 1)
                dve.wait_ge(sem(n + "e"), 1)
                link(dve.tensor_reduce(small[:, 11, 8:16], sh(1), axis=AX, op=ALU.add))
                link(dve.reciprocal(small[:, 11, 16:24], small[:, 11, 8:16]))
                return tt(sh(e_row), sh(1), bc(small[:, 11, 16:24], w, 2), ALU.mult)

            def split(n, row):
                src = small[:, row, :].rearrange("p (i w) -> p i w", w=16)
                cur = src
                b3 = small_b[:, :].rearrange("p (i w) -> p i w", w=16)
                rest = small[:, 10, :].rearrange("p (i w) -> p i w", w=16)
                for j in range(2):
                    link(cp(b3, cur))
                    link(cp(pieces[:, :, 16 * j:16 * j + 16], b3))
                    link(tt(rest, cur, pieces[:, :, 16 * j:16 * j + 16], ALU.subtract))
                    cur = rest
                cp(pieces[:, :, 32:48], rest).then_inc(sem(n + "pieces"), 1)

            def attention(n, causal_keys, ring, extra=None):
                U = 2 * B * NPAIR
                for u in range(U + LAG[n] + 2):
                    v = u - LAG[n] - 1
                    if 0 <= v < U and v % 2 == 1:
                        copy_probs(dve, n, v, causal_keys, lambda o, i: cp(o, i), "d")
                    if u < U:
                        keys = (u % 2 + 1) * P if causal_keys else 256
                        s3 = bank[ring[u % len(ring)]][:, :].rearrange("p (j k) -> p j k", j=2)
                        dve.wait_ge(sem(n + "sc"), u + 1)
                        if not causal_keys:
                            if u >= RING[n]:
                                dve.wait_ge(sem(n + "tr"), u - RING[n] + 1)
                            tt(probs_slot(n, u), s3, bc(mask_m[:, 2 * (u // 16) + u % 2, :], 2), ALU.add
                               ).then_inc(sem(n + "masked"), 1)
                            s3 = probs_slot(n, u)
                            dve.wait_ge(sem(n + "masked"), u + 1)
                        dve.tensor_reduce(neg_max[:, u % RING[n], :], s3[:, :, 0:keys], axis=AX, op=ALU.max,
                                          negate=True).then_inc(sem(n + "max"), 1)
                    v = u - SUMS[n]
                    if 0 <= v < U:
                        dve.wait_ge(sem(n + "exp"), v + 1)
                        if v >= RING[n]:
                            dve.wait_ge(sem(n + "norm"), v - RING[n] + 1)
                        dve.reciprocal(row_rec[:, v % RING[n], :], row_sum[:, v % RING[n], :]).then_inc(sem(n + "rec"), 1)
                    if extra:
                        extra(u)


            def low_part0(i):
                dve.wait_ge(sem("operand_hi"), i + 1)
                name, whole, both = SPLIT0[i]
                tt(both[:, 1], whole, both[:, 0].bitcast(f32), ALU.subtract).then_inc(sem("operand_lo"), 1)

            for i in range(3):
                low_part0(i)
            loaded(dve, "tab_q")
            for n, (w, c, half) in enumerate(QKV):
                if n in (2, 6):
                    low_part0(3 + n // 6)
                src = bank[n % 4][:, :].rearrange("p (b s) -> p b s", b=2)
                hh = slice(half * HALF, (half + 1) * HALF)
                if n == 8:
                    loaded(dve, "tab_c", "tab_s")
                dve.wait_ge(sem("qkv"), n + 1)
                if w == 0:
                    dst, tab = qT[:, c, hh], tab_q
                elif w == 1:
                    dst, tab = kT[:, c, hh], tab_c
                else:
                    if c * 2 + half >= 2:
                        dve.wait_ge(sem("kT"), c * 2 + half - 1)
                    dst, tab = probs[:, half].rearrange("p a b -> p (a b)"), tab_s
                tt(dst.rearrange("p (b s) -> p b s", b=2), src, bc(tab, 2), ALU.mult
                   ).then_inc(sem("qkv_out"), 1)
            loaded(dve, "ident", "causal", "tid")
            cp(ident_b[:, :], ident[:, :]).then_inc(sem("const_b"), 1)
            cp(causal_b[:, :], causal[:, :]).then_inc(sem("const_b"), 1)
            link(cp(tid_f, tid_i))
            ts(emask[0], tid_f, float(PER_EXPERT), None, ALU.is_lt).then_inc(sem("emask"), 1)
            for e in (1, 2):
                link(ts(lt_tmp, tid_f, float(PER_EXPERT * (e + 1)), None, ALU.is_lt))
                stt(emask[e], tid_f, float(PER_EXPERT * e), lt_tmp, ALU.is_ge, ALU.mult).then_inc(sem("emask"), 1)
                dve.wait_ge(sem("emask"), e + 1)
            ts(emask[3], tid_f, float(PER_EXPERT * 3), None, ALU.is_ge).then_inc(sem("emask"), 1)

            attention("a0_", True, (0, 1, 5))
            norm(0, 1.0, fin_bank)

            for k in range(16):
                half = k // 8
                dve.wait_ge(sem("r_silu"), k + 1)
                tt(hid0[:, k % 8, half * HALF:(half + 1) * HALF], silu0[:, k % 4, :], bank[k % 4][:, :],
                   ALU.mult).then_inc(sem("r_mul"), 1)
            norm(1, 1.0, fin_bank)

            dve.wait_ge(sem("f_lg"), 1)
            softmax_small("f_", bank[4][:, 0:64].rearrange("p (i w) -> p i w", w=8), 8, 5
                          ).then_inc(sem("f_alpha"), 1)
            for k in range(8):
                c, half = k % 4, k // 4
                dve.wait_ge(sem("f_v"), k + 1)
                dve.wait_ge(sem("f_bc_s"), k + 1)
                tt(vxa[:, c, half * HALF:(half + 1) * HALF], bc_s[:, k % 2, :], bank[(2 + k) % 4][:, :],
                   ALU.mult).then_inc(sem("f_vx"), 1)
            norm(2, 1.0, fin_bank)

            for k in range(4):
                dve.wait_ge(sem("s_xp_t"), k + 1)
                cp(x_p[:, 2 * k:2 * k + 2, :], bank[k][:, :].rearrange("p (i d) -> p i d", i=2)
                   ).then_inc(sem("x_p"), 1)
            dve.wait_ge(sem("s_soft"), 1)
            tt(small[:, 3, :], small[:, 2, :], small[:, 1, :], ALU.add).then_inc(sem("s_delta"), 1)
            dve.wait_ge(sem("decayed"), 1)
            for m in range(2 * SCAN_UNITS):
                n, c = m // 2, m % 2
                q, half, j = scan_unit(n)
                G = n // 4
                if G >= 2 and n % 4 == 0 and c == 0:
                    dve.wait_ge(sem("s_z"), G - 1)
                dve.wait_ge(sem("s_uT"), m + 1)
                for b in range(2):
                    at = slice(b * S, (b + 1) * S)
                    last = dve.tensor_tensor_scan(
                        hs[:, half, c, j, at], decay[:, c, 4 * q + j:4 * q + j + 1].broadcast_to([P, S]),
                        bank[m % 6][:, at], 0.0, ALU.mult, ALU.add)
                last.then_inc(sem("s_scan"), 1)
            for k in range(4):
                c, half = k % 2, k // 2
                hh = slice(half * HALF, (half + 1) * HALF)
                dve.wait_ge(sem("s_y"), k + 1)
                stt(xpT[:, c, hh], xpT[:, c, hh], vecs[:, 2, c:c + 1], bank[k][:, :], ALU.mult, ALU.add
                    ).then_inc(sem("s_yT"), 1)
            norm(3, 2.0, fin_bank)

            loaded(dve, "tab_kc", "tab_ks", "iota4", "seg")
            for half in range(2):
                for r in range(2):
                    n = 2 * half + r
                    dve.wait_ge(sem("k_rope"), n + 1)
                    if half == 1 and r == 0:
                        dve.wait_ge(sem("k_add"), 2)
                    src = bank[KROPE[n]][:, :].rearrange("p (b s) -> p b s", b=2)
                    tt(ropes[:, r, :].rearrange("p (b s) -> p b s", b=2), src, bc((tab_kc, tab_ks)[r], 2),
                       ALU.mult).then_inc(sem("k_mul"), 1)
                dve.wait_ge(sem("k_mul"), 2 * half + 2)
                hh = slice(half * HALF, (half + 1) * HALF)
                tt(keys_a[0:64, hh], ropes[0:64, 0, :], ropes[0:64, 1, :], ALU.add).then_inc(sem("k_add"), 1)
                tt(keys_b[64:128, hh], ropes[64:128, 0, :], ropes[64:128, 1, :], ALU.add).then_inc(sem("k_add"), 1)
            link(cp(seg_f[:, :], seg_i[:, :]))
            dve.wait_ge(sem("k_tok"), 1)

            def window_mask(i):
                link(ts(distance, iota4, seg_f[:, i:i + 1], None, ALU.subtract))
                link(tt(distance, distance, distance, ALU.mult))
                ts(mask_m[:, i, :], distance, 16.0, NEG, ALU.is_gt, ALU.mult).then_inc(sem("mask"), 1)
                dve.wait_ge(sem("mask"), i + 1)

            def rotate_pair(n):
                rope = q_banks(n)[0]
                dve.wait_ge(sem("q_rope"), n + 1)
                if n >= 2:
                    dve.wait_ge(sem("q_add"), n - 1)
                tt(ropes[:, n % 2, 0:S], rope[:, 0:S], tab_qc, ALU.mult)
                tt(ropes[:, n % 2, S:2 * S], rope[:, S:2 * S], tab_qs, ALU.mult).then_inc(sem("q_mul"), 1)

            def rotate_next(u):
                if u in QUERIES_AT:
                    rotate_pair(QUERIES_AT[u])
                if u % 16 in (10, 12) and u < 16 * (B - 1):
                    window_mask(2 * (u // 16) + 2 + u % 16 // 12)

            for half in range(2):
                hh = slice(half * HALF, (half + 1) * HALF)
                dve.wait_ge(sem("operand_hi"), QC_AT + half + 1)
                tt(qc_parts[:, 1, hh], bank[half][0:QC, :], qc_parts[:, 0, hh].bitcast(f32), ALU.subtract
                   ).then_inc(sem("operand_lo"), 1)
            loaded(dve, "tab_qc", "tab_qs")
            for n in range(FIRST):
                rotate_pair(n)
            window_mask(0)
            window_mask(1)
            attention("a4_", False, (0, 1), rotate_next)
            norm(4, 1.0, fin_bank)

            dve.wait_ge(sem("m_lg"), 1)
            link(softmax_small("m_", bank[3][:, 0:128].rearrange("p (i w) -> p i w", w=16), 16, 3))
            sc3 = small[:, 3, :].rearrange("p (i w) -> p i w", w=16)
            r3 = lambda r: small[:, r, :].rearrange("p (i w) -> p i w", w=16)
            for i in range(NT):
                last = dve.max(top8[:, i, :], sc3[:, i, :])
            link(last)
            thr = top8[:, :, TOPK - 1].unsqueeze(2).broadcast_to([P, NT, NE])
            link(tt(r3(4), sc3, thr, ALU.is_gt))
            link(tt(r3(5), sc3, thr, ALU.is_equal))
            link(dve.tensor_reduce(small[:, 11, 24:32], r3(4), axis=AX, op=ALU.add))
            loaded(dve, "reset")
            link(dve.tensor_tensor_scan(small[:, 6, :], reset[:, :], small[:, 5, :], 0.0, ALU.mult, ALU.add))
            link(tt(r3(7), r3(6), bc(small[:, 11, 24:32], NE, 2), ALU.add))
            link(stt(small[:, 8, :], small[:, 7, :], float(TOPK), small[:, 5, :], ALU.is_le, ALU.mult))
            link(tt(small[:, 9, :], small[:, 8, :], small[:, 4, :], ALU.add))
            link(tt(small[:, 9, :], small[:, 9, :], small[:, 3, :], ALU.mult))
            split("m_", 9)
            def low_part(k):
                dve.wait_ge(sem("m_hi"), k + 1)
                tt(hid_parts[:, k % HID, 1, :], hid1[:, k % 2, :], hid_parts[:, k % HID, 0, :].bitcast(f32),
                   ALU.subtract).then_inc(sem("m_lo"), 1)

            for k in range(2 * FCH):
                half = k % 2
                dve.wait_ge(sem("m_silu"), k + 1)
                dve.wait_ge(sem("m_u"), k + 1)
                if k >= 2:
                    dve.wait_ge(sem("m_lo"), k - 1)
                tt(hid1[:, k % 2, :], silu1[:, k % 2, :], bank[2 + k % 2][:, :], ALU.mult
                   ).then_inc(sem("m_mul"), 1)
                if k < 2:
                    dve.wait_ge(sem("cw_rows"), k + 1)
                dve.wait_ge(sem("m_mul"), k + 1)
                tt(hid1[:, k % 2, :], hid1[:, k % 2, :], cw_rows[:, half * HALF:(half + 1) * HALF], ALU.mult
                   ).then_inc(sem("m_hid"), 1)
                if k:
                    low_part(k - 1)
            low_part(2 * FCH - 1)
            dve.wait_ge(sem("ln4_t"), 4)
            for i in range(NT):
                dve.wait_ge(sem("fin5"), i // 2 * 2 + 2)
                stt(x_tok[:, i, :], x_tok[:, i, :], 1.0,
                    bank[4 + i // 2][:, (i % 2) * D:(i % 2 + 1) * D], ALU.mult, ALU.add
                    ).then_inc(sem("ln5_r"), 1)
            for i in range(NT):
                dve.wait_ge(sem("ln5_r"), i + 1)
                link(dve.bn_stats(stats[:, i, :], x_tok[:, i, :]))
                dve.bn_aggr(meanvar[:, i, :], stats[:, i, :]).then_inc(sem("ln5_v"), 1)
            for i in range(NT):
                dve.wait_ge(sem("ln5_v"), i + 1)
                dve.wait_ge(sem("ln5_rstd"), i // 4 + 1)
                ts(x_tok[:, i, :], x_tok[:, i, :], meanvar[:, i, 0:1], rstd[:, i:i + 1],
                   ALU.subtract, ALU.mult).then_inc(sem("ln5_x"), 1)

        @block.scalar
        def _(act):
            af = act.activation

            def ln_out(k, half):
                for q in (2 * half, 2 * half + 1):
                    act.wait_ge(sem(f"ln{k}_t"), q + 1)
                    src = bank[4 + q % 2][:, :].rearrange("p (i c t) -> p i c t", i=2, c=2)
                    dst = xT[:, :, q * 2 * P:(q + 1) * 2 * P].rearrange("p c (i t) -> p i c t", i=2)
                    af(dst, src, ACT.Copy).then_inc(sem(f"ln{k}_xT"), 1)

            def attention(n, causal_keys, ring, out_of, extra=None):
                U = 2 * B * NPAIR
                for u in range(U + LAG[n] + 3 + 2 * AT_ONCE[n]):
                    v = u - LAG[n] - 1
                    if 0 <= v < U and v % 2 == 0:
                        copy_probs(act, n, v, causal_keys, lambda o, i: af(o, i, ACT.Copy), "a")
                    if u < U:
                        keys = (u % 2 + 1) * P if causal_keys else 256
                        act.wait_ge(sem(n + "max"), u + 1)
                        if u >= RING[n]:
                            act.wait_ge(sem(n + "tr"), u - RING[n] + 1)
                            act.wait_ge(sem(n + "rec"), u - RING[n] + 1)
                        for j in range(2):
                            slot = probs_slot(n, u)[:, j, 0:keys]
                            scores = bank[ring[u % len(ring)]][:, j * 256:j * 256 + keys] if causal_keys else slot
                            last = af(slot, scores, ACT.Exp,
                                      bias=neg_max[:, u % RING[n], j:j + 1],
                                      accum_out=row_sum[:, u % RING[n], j:j + 1])
                        last.then_inc(sem(n + "exp"), 1)
                    G = group_at(n, u - LAG[n] - 2 - 2 * AT_ONCE[n])
                    if G is not None:
                        act.wait_ge(sem(n + "av"), G + 1)
                        dst, src = out_of(G)
                        af(dst, src, ACT.Copy).then_inc(sem(n + "oT"), 1)
                    if extra:
                        extra(u)

            for name, whole, both in SPLIT0:
                if name in GROUP:
                    loaded(act, name)
                else:
                    act.wait_ge(sem("ld_" + name), 16)
                af(both[:, 0], whole, ACT.Copy).then_inc(sem("operand_hi"), 1)
            loaded(act, "decay")
            af(decay[:, :, :], decay[:, :, :], ACT.Sigmoid).then_inc(sem("decayed"), 1)
            act.wait_ge(sem("zeroed"), 1)
            for i in range(NT):
                act.wait_ge(sem("v"), i + 1)
                af(v_pad[:, i, :].rearrange("p (h w) -> p h w", w=PAD)[:, :, 0:HD0],
                   bank[4 + i % 2][:, 0:D].rearrange("p (h w) -> p h w", w=HD0), ACT.Copy
                   ).then_inc(sem("v_out"), 1)

            def out_of0(G):
                b, p = G // 4, 2 * (G % 4)
                r, c = PAD * (p % 4), 2 * (p // 4)
                return (oT[r:r + 2 * PAD, c:c + 2, b * S:(b + 1) * S],
                        bank[(4, 6)[G % 2]][r:r + 2 * PAD, :].rearrange("p (j q) -> p j q", j=2))

            attention("a0_", True, (0, 1, 5), out_of0)
            ln_out(0, 0)

            for k in range(16):
                if k == 8:
                    ln_out(0, 1)
                act.wait_ge(sem("r_up"), k + 1)
                if k >= 4:
                    act.wait_ge(sem("r_mul"), k - 3)
                af(silu0[:, k % 4, :], bank[k % 4][:, :], ACT.Silu).then_inc(sem("r_silu"), 1)
            ln_out(1, 0)

            loaded(act, "vecs")
            for k in range(4):
                c, half = k % 2, k // 2
                if k == 2:
                    ln_out(1, 1)
                act.wait_ge(sem("f_h"), k + 1)
                af(h1T[:, c, half * HALF:(half + 1) * HALF], bank[c][:, :], ACT.Relu,
                   bias=vecs[:, 0, c:c + 1]).then_inc(sem("f_hT"), 1)
            act.wait_ge(sem("f_sub"), 1)
            af(small[:, 1, 0:64], small[:, 0, 0:64], ACT.Exp).then_inc(sem("f_e"), 1)
            for f in range(6):
                act.wait_ge(sem("fold"), f + 1)
                o = bank[6 + f % 2]
                if f < 2:
                    af(qk_fold[:, 4 * f:4 * f + 4, :], o[0:QC, :].rearrange("p (a b) -> p a b", a=4),
                       ACT.Copy, scale=MLA_SCALE).then_inc(sem("fold_out"), 1)
                else:
                    af(vo_fold[:, 2 * f - 4:2 * f - 2, :], o[:, :].rearrange("p (a b) -> p a b", a=2),
                       ACT.Copy).then_inc(sem("fold_out"), 1)
            for k in range(8):
                act.wait_ge(sem("f_bc"), k + 1)
                if k >= 2:
                    act.wait_ge(sem("f_vx"), k - 1)
                af(bc_s[:, k % 2, :], bank[6 + k % 2][:, :], ACT.Copy).then_inc(sem("f_bc_s"), 1)
            ln_out(2, 0)

            for k in range(4):
                c, half = k % 2, k // 2
                if k == 2:
                    ln_out(2, 1)
                act.wait_ge(sem("s_xp"), k + 1)
                af(xpT[:, c, half * HALF:(half + 1) * HALF], bank[k][:, :], ACT.Identity,
                   bias=vecs[:, 1, c:c + 1]).then_inc(sem("s_xpT"), 1)
            act.wait_ge(sem("s_pre"), 1)
            pre = bank[4][:, 0:P]
            af(small[:, 0, :], pre, ACT.Abs).then_inc(sem("s_sp"), 1)
            af(small[:, 2, :], pre, ACT.Relu)
            act.wait_ge(sem("s_sp"), 1)
            af(small[:, 0, :], small[:, 0, :], ACT.Exp, scale=-1.0).then_inc(sem("s_sp"), 1)
            act.wait_ge(sem("s_sp"), 2)
            af(small[:, 1, :], small[:, 0, :], ACT.Ln, bias=1.0).then_inc(sem("s_soft"), 1)
            act.wait_ge(sem("s_delta"), 1)
            act.wait_ge(sem("x_p"), 4)
            for n in range(SCAN_UNITS):
                scale_tokens(act, n, (0, 1), lambda o, i, a: af(o, i, ACT.Copy, scale=a), "s_scaled_a")
            for half in range(2):
                act.wait_ge(sem("s_z"), 7 + half)
                af(zT[:, half * HALF:(half + 1) * HALF], bank[6 + half][:, :], ACT.Copy
                   ).then_inc(sem("s_zT"), 1)

            ln_out(3, 0)
            for half in range(2):
                hh = slice(half * HALF, (half + 1) * HALF)
                act.wait_ge(sem("k_lat"), half + 1)
                af(keys_b[0:64, hh], bank[half][0:64, :], ACT.Copy).then_inc(sem("k_latT"), 1)
                af(keys_a[64:128, hh], bank[half][64:128, :], ACT.Copy).then_inc(sem("k_latT"), 1)
            act.wait_ge(sem("k_tok"), 1)
            af(kv_tok, bank[2][:, :].rearrange("p (i c) -> p i c", i=NT), ACT.Copy).then_inc(sem("k_tokT"), 1)
            ln_out(3, 1)
            for half in range(2):
                act.wait_ge(sem("qc"), half + 1)
                af(qc_parts[:, 0, half * HALF:(half + 1) * HALF], bank[half][0:QC, :], ACT.Copy
                   ).then_inc(sem("operand_hi"), 1)

            def latent_pair(n):
                lat = q_banks(n)[1]
                at = NH * (n // NPAIR % 2) + 2 * (n % NPAIR)
                act.wait_ge(sem("q_l"), n + 1)
                af(qm[0:64, at + 1, :], lat[0:64, 0:S], ACT.Copy)
                af(qm[64:128, at, :], lat[64:128, 0:S], ACT.Copy).then_inc(sem("q_lat"), 1)

            def latent_next(u):
                if u in QUERIES_AT:
                    latent_pair(QUERIES_AT[u])

            def out_of4(g):
                b, p = g // 8, g % 8
                return om[:, p, b * S:(b + 1) * S], bank[(4, 6)[g % 2]][:, 0:S]

            for n in range(FIRST):
                latent_pair(n)
            attention("a4_", False, (0, 1), out_of4, latent_next)
            for half in range(2):
                ln_out(4, half)
                act.wait_ge(sem("ln4_xT"), 2 * half + 2)
                hh = slice(half * HALF, (half + 1) * HALF)
                af(x_parts[:, 0, :, hh], xT[:, :, hh], ACT.Copy).then_inc(sem("operand_hi"), 1)

            act.wait_ge(sem("m_sub"), 1)
            af(small[:, 1, :], small[:, 0, :], ACT.Exp).then_inc(sem("m_e"), 1)

            def silu(k):
                act.wait_ge(sem("m_g"), k + 1)
                if k >= 2:
                    act.wait_ge(sem("m_mul"), k - 1)
                af(silu1[:, k % 2, :], bank[k % 2][:, :], ACT.Silu).then_inc(sem("m_silu"), 1)

            def high_part(k):
                act.wait_ge(sem("m_hid"), k + 1)
                if k >= HID:
                    act.wait_ge(sem("m_down"), k - HID + 1)
                af(hid_parts[:, k % HID, 0, :], hid1[:, k % 2, :], ACT.Copy).then_inc(sem("m_hi"), 1)

            silu(0)
            silu(1)
            act.wait_ge(sem("m_piecesT"), 1)
            for half in range(2):
                af(piecesT[:, half * HALF:(half + 1) * HALF], bank[4 + half][0:48, :], ACT.Copy
                   ).then_inc(sem("m_piecesB"), 1)
            for half in range(2):
                act.wait_ge(sem("m_cw"), half + 1)
                af(cw_rows[:, half * HALF:(half + 1) * HALF], bank[6 + half][:, :], ACT.Copy
                   ).then_inc(sem("cw_rows"), 1)
            for k in range(2 * FCH):
                high_part(k)
                if k + 2 < 2 * FCH:
                    silu(k + 2)

        @block.gpsimd
        def _(pool):
            step = [0]

            def link(ins):
                step[0] += 1
                ins.then_inc(sem("pool_chain"), 1)
                pool.wait_ge(sem("pool_chain"), step[0])

            def rstd_of(k, halves=(0, 1)):
                for half in halves:
                    s = slice(4 * half, 4 * half + 4)
                    pool.wait_ge(sem(f"ln{k}_v"), 4 * half + 4)
                    link(pool.tensor_scalar(veps[:, s], meanvar[:, s, 1], EPS, 1.0, ALU.add, ALU.mult))
                    pool.tensor_tensor(rstd[:, s], veps[:, s], minus_half[:, s], ALU.pow
                                       ).then_inc(sem(f"ln{k}_rstd"), 1)

            def attention(n, causal_keys, extra=None):
                for u in range(2 * B * NPAIR):
                    if extra:
                        extra(u)
                    keys = (u % 2 + 1) * P if causal_keys else 256
                    pool.wait_ge(sem(n + "rec"), u + 1)
                    for j in range(2):
                        pr = probs_slot(n, u)[:, j, 0:keys]
                        last = pool.tensor_scalar(pr, pr, row_rec[:, u % RING[n], j:j + 1], 1.0, ALU.mult, ALU.mult)
                    last.then_inc(sem(n + "norm"), 1)

            pool.memset(v_pad, 0.0).then_inc(sem("zeroed"), 1)
            link(pool.memset(minus_half[:, :], -0.5))
            for k in range(8):
                c, half = k // 2, k % 2
                hh = slice(half * HALF, (half + 1) * HALF)
                pool.wait_ge(sem("qkv_out"), 17 + k)
                pool.tensor_tensor(kT[:, c, hh], kT[:, c, hh], probs[:, k % 2].rearrange("p a b -> p (a b)"),
                                   ALU.add).then_inc(sem("kT"), 1)
            attention("a0_", True)
            rstd_of(0)
            pool.wait_ge(sem("emask"), 4)
            for k in range(16):
                half, e = k // 8, k // 2 % 4
                hh = slice(half * HALF, (half + 1) * HALF)
                pool.wait_ge(sem("r_mul"), k + 1)
                pool.tensor_tensor(hid0[:, k % 8, hh], hid0[:, k % 8, hh], emask[e][:, hh], ALU.mult
                                   ).then_inc(sem("r_hid"), 1)
            rstd_of(1)

            def both_parts(parts_of, w):
                link(pool.tensor_copy(parts_of[:, 0], w))
                return pool.tensor_tensor(parts_of[:, 1], w, parts_of[:, 0].bitcast(f32), ALU.subtract)

            pool.wait_ge(sem("fold_out"), 2)
            both_parts(qk_parts, qk_fold[:, :, :]).then_inc(sem("q_split"), 1)
            rstd_of(2)
            loaded(pool, "wqr_raw", "wqr_swp")
            both_parts(wqr_raw_parts, wqr_raw).then_inc(sem("q_split"), 1)
            both_parts(wqr_swp_parts, wqr_swp).then_inc(sem("q_split"), 1)
            pool.wait_ge(sem("s_delta"), 1)
            pool.wait_ge(sem("x_p"), 4)
            for n in range(SCAN_UNITS):
                scale_tokens(pool, n, (2, 3), lambda o, i, a: pool.tensor_scalar(o, i, a, 1.0, ALU.mult, ALU.mult),
                             "s_scaled_p")
            rstd_of(3)

            def add_pair(n):
                at = NH * (n // NPAIR % 2) + 2 * (n % NPAIR)
                pool.wait_ge(sem("q_mul"), n + 1)
                link(pool.tensor_tensor(qm[0:64, at, :], ropes[0:64, n % 2, 0:S],
                                        ropes[0:64, n % 2, S:2 * S], ALU.add))
                pool.tensor_tensor(qm[64:128, at + 1, :], ropes[64:128, n % 2, 0:S],
                                   ropes[64:128, n % 2, S:2 * S], ALU.add).then_inc(sem("q_add"), 1)
                pool.wait_ge(sem("q_add"), n + 1)

            def add_next(u):
                if u in QUERIES_AT:
                    if u:
                        pool.wait_ge(sem("a4_norm"), u)
                    add_pair(QUERIES_AT[u])

            for n in range(FIRST):
                add_pair(n)
            attention("a4_", False, add_next)
            def split_weights(c):
                w = raw[c % RAW]
                pool.wait_ge(sem(f"ld_raw{c % RAW}"), 16 * (c // RAW + 1))
                for words, both, r in ((slice(0, GU), gu_parts, c % 2),
                                       (slice(GU, GU + DN), down_parts, c % 3)):
                    if both is gu_parts and c >= 2:
                        pool.wait_ge(sem("m_u"), 2 * c - 2)
                    if both is down_parts and c >= 3:
                        pool.wait_ge(sem("m_down"), 2 * c - 4)
                    link(pool.tensor_copy(both[:, r, 0, :], w[:, words]))
                    last = pool.tensor_tensor(both[:, r, 1, :], w[:, words], both[:, r, 0, :].bitcast(f32),
                                              ALU.subtract)
                last.then_inc(sem("m_w"), 1)

            split_weights(0)
            for half in range(2):
                rstd_of(4, (half,))
                hh = slice(half * HALF, (half + 1) * HALF)
                pool.wait_ge(sem("operand_hi"), X_AT + half + 1)
                pool.tensor_tensor(x_parts[:, 1, :, hh], xT[:, :, hh], x_parts[:, 0, :, hh].bitcast(f32),
                                   ALU.subtract).then_inc(sem("operand_lo"), 1)
            for c in range(1, FCH):
                split_weights(c)
            rstd_of(5)


def laid_out(x):
    import numpy as np

    f = np.float32
    a = {k: np.asarray(v) for k, v in x.items()}
    o = {}

    def chunks(w):
        return w.reshape(-1, 128, w.shape[-1]).transpose(1, 0, 2)

    X = a["x"].reshape(1024, 256)
    o["x_tok"] = chunks(X)
    o["xT"] = chunks(X.T)
    head = np.arange(16)[:, None] * 16
    j = np.arange(16)[None, :]
    plain, swapped = head + j, head + (j + 8) % 16
    both = lambda l, r: np.concatenate([l, r], axis=1).ravel()
    o["wq"] = chunks(a["L0_attn_Wq"].T[:, both(plain, swapped)])
    o["wk_raw"] = chunks(a["L0_attn_Wk"].T[:, both(plain, plain)])
    o["wk_swp"] = chunks(a["L0_attn_Wk"].T[:, both(swapped, swapped)])
    o["wv"] = chunks(a["L0_attn_Wv"].T)
    wo = np.zeros((16, 32, 256), f)
    wo[:, :16] = a["L0_attn_Wo"].T.reshape(16, 16, 256)
    o["wo_pad"] = chunks(wo.reshape(512, 256))
    fr = np.arange(256, dtype=f)[:, None] * (1.0 / 10000.0 ** (np.arange(0, 16, 2, dtype=f) / 16)).astype(f)
    emb = np.concatenate([fr, fr], axis=-1)
    cos, sin = np.cos(emb).T.astype(f), np.sin(emb).T.astype(f)
    sgn = np.where(np.arange(16) < 8, -1, 1).astype(f)[:, None] * sin
    o["tab_q"] = np.tile(np.concatenate([cos, sgn]), (4, 1)) * f(0.25)
    o["tab_c"] = np.tile(cos, (8, 1))
    o["tab_s"] = np.tile(sgn, (8, 1))
    o["ident"] = np.eye(128, dtype=f)
    neg = -(np.array([1e30], f).view(np.uint32) & np.uint32(0xFFFF0000)).view(f)[0]
    k = np.arange(128)
    o["causal"] = np.where(k[None, :] > k[:, None], neg, 0).astype(f)
    o["tid"] = a["itok_BxS_13_99985"].reshape(1024).astype(np.int32)
    o["w_uqT"] = a["L1_xattn_W_uq"].reshape(96, 16, 128).transpose(2, 1, 0)
    o["w_ukT"] = a["L1_xattn_W_uk"].reshape(64, 16, 128).transpose(2, 1, 0)
    o["w_uvT"] = a["L1_xattn_W_uv"].reshape(64, 16, 128).transpose(2, 1, 0)
    o["w_o"] = a["L1_xattn_W_o"].reshape(16, 128, 256).transpose(1, 0, 2)
    o["ctxT"] = a["ctx_2048"].transpose(2, 0, 1).reshape(2, 128, 4, 256).transpose(1, 2, 0, 3)
    o["w1"] = chunks(a["L0_ffn_W1"])
    o["vT"] = chunks(a["L0_ffn_V"].reshape(512, 256).T)
    o["uw"] = chunks(a["L0_ffn_U"].transpose(0, 2, 1).reshape(512, 256))
    o["w2s"] = chunks(a["L0_ffn_W2"])
    vecs = np.zeros((128, 8, 2), f)
    vecs[:, 0] = a["L0_ffn_b1"].reshape(2, 128).T
    vecs[:, 1] = a["L1_attn_proj_in_b"].reshape(2, 128).T
    vecs[:, 2] = a["L1_attn_D_param"].reshape(2, 128).T
    o["vecs"] = vecs
    o["rows"] = np.concatenate([a["L0_ffn_b2"], a["L1_attn_proj_out_b"], np.ones(128, f)])[None]
    o["decay"] = chunks(a["L1_attn_A"])
    o["pinT"] = chunks(a["L1_attn_proj_in_w"].T)
    o["poutT"] = chunks(a["L1_attn_proj_out_w"].T)
    o["wBT"] = chunks(a["L1_attn_B_w"].T)
    cw = np.zeros((4, 32, 256), f)
    cw[:, :4] = a["L1_attn_C_w"].T.reshape(4, 4, 256).transpose(1, 0, 2)
    o["CwP"] = cw.reshape(128, 2, 128)
    onesel = np.zeros((128, 4, 32), f)
    for q in range(4):
        onesel[:, q, q] = 1
    o["onesel"] = onesel
    o["sel_e"] = np.tile(np.repeat(np.eye(16, dtype=f), 8, axis=1), (3, 1)).astype(np.uint16) * np.uint16(0x3F80)
    o["seg"] = a["itok_BxS_0_1023"].reshape(8, 128).T.astype(np.int32)
    o["wgateT"] = chunks(a["L1_ffn_gate_w"].T)
    r = np.arange(64)
    swp = (r + 32) % 64
    wqr = a["L1_xattn_W_qr"].reshape(96, 16, 64)
    o["wqr_raw"] = wqr.reshape(96, 8, 128)
    o["wqr_swp"] = wqr[:, :, swp].reshape(96, 8, 128)
    o["w_dq"] = chunks(a["L1_xattn_W_dq"])
    o["w_kvc"] = chunks(np.tile(a["L1_xattn_W_kvc"], (1, 2)))
    kr = a["L1_xattn_W_kr"]
    o["w_kr"] = np.stack([np.tile(kr, (1, 2)), np.tile(kr[:, swp], (1, 2))], axis=1)
    inv = (1.0 / 10000.0 ** (np.arange(32, dtype=f) / 32)).astype(f)
    ang = np.arange(256, dtype=f)[:, None] * inv
    c, s = np.cos(ang).T.astype(f), np.sin(ang).T.astype(f)
    o["tab_kc"] = np.concatenate([c, c, c, c])
    o["tab_ks"] = np.concatenate([-s, s, -s, s])
    scale = f(192 ** -0.5)
    o["tab_qc"] = o["tab_kc"] * scale
    o["tab_qs"] = o["tab_ks"] * scale
    o["iota4"] = np.tile(np.arange(256, dtype=f) + 4, (128, 1))
    o["reset"] = np.tile((np.arange(128) % 16 != 0).astype(f), (128, 1))


    def by_chunk(w):
        return w.reshape(16, 22, 8, 256).transpose(1, 0, 2, 3).reshape(22, 128, 256)

    def transposed(w):
        return by_chunk(w).reshape(22, 128, 2, 128).transpose(0, 3, 2, 1).reshape(22, 128, 256)

    o["experts"] = np.concatenate([transposed(a["L1_ffn_w_gate"]), transposed(a["L1_ffn_w_up"]),
                                   by_chunk(a["L1_ffn_w_down"].transpose(0, 2, 1))], axis=2)
    return {k: np.ascontiguousarray(v) for k, v in o.items()}


def kernel(**inputs):
    import concourse.bacc as bacc
    from concourse import mybir
    from concourse.bass_utils import run_bass_kernel_spmd

    arrays = laid_out(inputs)
    nc = bacc.Bacc("TRN2", target_bir_lowering=False, num_devices=1)
    d = {k: nc.dram_tensor("in_" + k, v.shape, mybir.dt.from_np(v.dtype), kind="ExternalInput").ap()
         for k, v in arrays.items()}
    out = nc.dram_tensor("out", (8, 128, 256), mybir.dt.float32, kind="ExternalOutput").ap()
    build(nc, d, out)
    r = run_bass_kernel_spmd(nc, [{"in_" + k: v for k, v in arrays.items()}], core_ids=[0])
    return r.results[0]["out"].reshape(4, 256, 256)
```
